# Optimizing a Trainium2 kernel written in Bass

```python
import numpy as np
import jax
import jax.numpy as jnp

def _softmax(x, axis=-1):
    return jax.nn.softmax(x, axis=axis)

def _gelu(x):
    return jax.nn.gelu(x, approximate=True)

def _silu(x):
    return jax.nn.silu(x)

def _sigmoid(x):
    return jax.nn.sigmoid(x)

def _layernorm(x, axis=-1, eps=1e-05):
    m = jnp.mean(x, axis=axis, keepdims=True)
    v = jnp.var(x, axis=axis, keepdims=True)
    return (x - m) / jnp.sqrt(v + eps)

def _scatter_add(tgt, idx, src, axis=0):
    return tgt.at[idx].add(src)

def _segment_sum(src, seg, n):
    return jax.ops.segment_sum(src, seg, n)
kernel_name = 'mk_vit_tower_postln_d1_tok_img768_r4_3446f7'

def setup_inputs(seed: int=0):
    np.random.seed(seed)
    _w = jnp.asarray

    def _rec_inputs():
        import jax
        import jax.numpy as jnp
        _rk = jax.random.key(seed)
        x = -0.00040386 + 0.999972 * jax.random.normal(jax.random.fold_in(_rk, 1), (64, 3, 128, 128), jnp.float32)
        return x
    x = _rec_inputs()

    def _L0_tok_setup():
        import jax, jax.numpy as jnp
        import numpy as np
        P = 16
        WIN = 64
        NH = 12

        def _layernorm(x, g, b, eps=1e-05):
            m = x.mean(-1, keepdims=True)
            v = ((x - m) ** 2).mean(-1, keepdims=True)
            return (x - m) * jax.lax.rsqrt(v + eps) * g + b

        def _sinusoidal_pe(n, d):
            pos = jnp.arange(n, dtype=jnp.float32)[:, None]
            i = jnp.arange(d // 2, dtype=jnp.float32)[None, :]
            ang = pos / jnp.power(10000.0, 2.0 * i / d)
            pe = jnp.zeros((n, d), jnp.float32)
            pe = pe.at[:, 0::2].set(jnp.sin(ang)).at[:, 1::2].set(jnp.cos(ang))
            return pe
        key = jax.random.key(seed)
        ks = jax.random.split(key, 8)
        B, C, H, W, D, F = (16, 3, 128, 128, 192, 768)
        s = lambda k, shape: jax.random.normal(k, shape, jnp.float32) * 0.02
        return {'input': jax.random.normal(ks[0], (B, C, H, W), jnp.float32), 'patch_w': s(ks[1], (D, C, P, P)), 'patch_b': jnp.zeros((D,), jnp.float32), 'ln_g': jnp.ones((D,), jnp.float32), 'ln_b': jnp.zeros((D,), jnp.float32), 'qkv_w': s(ks[2], (D, 3 * D)), 'qkv_b': jnp.zeros((3 * D,), jnp.float32), 'proj_w': s(ks[3], (D, D)), 'proj_b': jnp.zeros((D,), jnp.float32), 'ff1_w': s(ks[4], (D, F)), 'ff1_b': jnp.zeros((F,), jnp.float32), 'ff2_w': s(ks[5], (F, D)), 'ff2_b': jnp.zeros((D,), jnp.float32)}
    _L0_tok_all = _L0_tok_setup()
    _L0_tok_in = {k: v for k, v in _L0_tok_all.items() if k in ('patch_w', 'patch_b', 'ln_g', 'ln_b', 'qkv_w', 'qkv_b', 'proj_w', 'proj_b', 'ff1_w', 'ff1_b', 'ff2_w', 'ff2_b')}
    del _L0_tok_all

    def _L0_attn_setup():
        import jax, jax.numpy as jnp
        import numpy as np
        N_HEADS = 12
        key = jax.random.key(seed)
        ks = jax.random.split(key, 5)
        B, N, D = (16, 256, 192)
        x = jax.random.normal(ks[0], (B, N, D), dtype=jnp.float32)
        w_qkv = jax.random.normal(ks[1], (D, 3 * D), dtype=jnp.float32) * D ** (-0.5)
        b_qkv = jax.random.normal(ks[2], (3 * D,), dtype=jnp.float32) * 0.02
        w_proj = jax.random.normal(ks[3], (D, D), dtype=jnp.float32) * D ** (-0.5)
        b_proj = jax.random.normal(ks[4], (D,), dtype=jnp.float32) * 0.02
        return {'x': x, 'w_qkv': w_qkv, 'b_qkv': b_qkv, 'w_proj': w_proj, 'b_proj': b_proj}
    _L0_attn_all = _L0_attn_setup()
    _L0_attn_in = {k: v for k, v in _L0_attn_all.items() if k in ('w_qkv', 'b_qkv', 'w_proj', 'b_proj')}
    del _L0_attn_all

    def _L0_ffn_setup():
        import jax, jax.numpy as jnp
        import numpy as np
        B, T, H, F, E = (128, 32, 192, 768, 3)
        key = jax.random.key(seed)
        ks = jax.random.split(key, 4)
        s = 0.02
        return {'x': jax.random.normal(ks[0], (B, T, H), jnp.float32), 'Wg': jax.random.normal(ks[1], (E, H), jnp.float32) * s, 'W1': jax.random.normal(ks[2], (E, H, F), jnp.float32) * s, 'b1': jnp.zeros((E, F), jnp.float32), 'W2': jax.random.normal(ks[3], (E, F, H), jnp.float32) * s, 'b2': jnp.zeros((E, H), jnp.float32)}
    _L0_ffn_all = _L0_ffn_setup()
    _L0_ffn_in = {k: v for k, v in _L0_ffn_all.items() if k in ('Wg', 'W1', 'b1', 'W2', 'b2')}
    del _L0_ffn_all
    return {'x': x, 'L0_tok_patch_w': _L0_tok_in['patch_w'], 'L0_tok_patch_b': _L0_tok_in['patch_b'], 'L0_tok_ln_g': _L0_tok_in['ln_g'], 'L0_tok_ln_b': _L0_tok_in['ln_b'], 'L0_tok_qkv_w': _L0_tok_in['qkv_w'], 'L0_tok_qkv_b': _L0_tok_in['qkv_b'], 'L0_tok_proj_w': _L0_tok_in['proj_w'], 'L0_tok_proj_b': _L0_tok_in['proj_b'], 'L0_tok_ff1_w': _L0_tok_in['ff1_w'], 'L0_tok_ff1_b': _L0_tok_in['ff1_b'], 'L0_tok_ff2_w': _L0_tok_in['ff2_w'], 'L0_tok_ff2_b': _L0_tok_in['ff2_b'], 'L0_attn_w_qkv': _L0_attn_in['w_qkv'], 'L0_attn_b_qkv': _L0_attn_in['b_qkv'], 'L0_attn_w_proj': _L0_attn_in['w_proj'], 'L0_attn_b_proj': _L0_attn_in['b_proj'], 'L0_ffn_Wg': _L0_ffn_in['Wg'], 'L0_ffn_W1': _L0_ffn_in['W1'], 'L0_ffn_b1': _L0_ffn_in['b1'], 'L0_ffn_W2': _L0_ffn_in['W2'], 'L0_ffn_b2': _L0_ffn_in['b2']}

def reference(x, L0_tok_patch_w, L0_tok_patch_b, L0_tok_ln_g, L0_tok_ln_b, L0_tok_qkv_w, L0_tok_qkv_b, L0_tok_proj_w, L0_tok_proj_b, L0_tok_ff1_w, L0_tok_ff1_b, L0_tok_ff2_w, L0_tok_ff2_b, L0_attn_w_qkv, L0_attn_b_qkv, L0_attn_w_proj, L0_attn_b_proj, L0_ffn_Wg, L0_ffn_W1, L0_ffn_b1, L0_ffn_W2, L0_ffn_b2):
    import jax
    import jax.numpy as jnp

    def _L0_tok_ref(input, patch_w, patch_b, ln_g, ln_b, qkv_w, qkv_b, proj_w, proj_b, ff1_w, ff1_b, ff2_w, ff2_b):
        import jax, jax.numpy as jnp
        import numpy as np
        P = 16
        WIN = 64
        NH = 12

        def _layernorm(x, g, b, eps=1e-05):
            m = x.mean(-1, keepdims=True)
            v = ((x - m) ** 2).mean(-1, keepdims=True)
            return (x - m) * jax.lax.rsqrt(v + eps) * g + b

        def _sinusoidal_pe(n, d):
            pos = jnp.arange(n, dtype=jnp.float32)[:, None]
            i = jnp.arange(d // 2, dtype=jnp.float32)[None, :]
            ang = pos / jnp.power(10000.0, 2.0 * i / d)
            pe = jnp.zeros((n, d), jnp.float32)
            pe = pe.at[:, 0::2].set(jnp.sin(ang)).at[:, 1::2].set(jnp.cos(ang))
            return pe
        B, C, H, W = input.shape
        D = patch_w.shape[0]
        dh = D // NH
        xp = input.reshape(B, C, H // P, P, W // P, P)
        x = jnp.einsum('bchpwq,dcpq->bhwd', xp, patch_w) + patch_b
        x = x.reshape(B, -1, D)
        x = _layernorm(x, ln_g, ln_b)
        N = x.shape[1]
        x = x + _sinusoidal_pe(N, D)

        def ff(y):
            return jax.nn.gelu(y @ ff1_w + ff1_b) @ ff2_w + ff2_b

        def sparse_attn(y):
            nW = N // WIN
            qkv = (y @ qkv_w + qkv_b).reshape(B, nW, WIN, 3, NH, dh)
            q, k, v = (qkv[:, :, :, 0], qkv[:, :, :, 1], qkv[:, :, :, 2])
            scores = jnp.einsum('bwqhd,bwkhd->bwhqk', q, k) * dh ** (-0.5)
            a = jax.nn.softmax(scores, axis=-1)
            o = jnp.einsum('bwhqk,bwkhd->bwqhd', a, v).reshape(B, N, D)
            return o @ proj_w + proj_b
        identity = x
        x = ff(x)
        x = sparse_attn(x)
        x = x + identity
        identity = x
        x = ff(x)
        x = x + identity
        return x

    def _L0_attn_ref(x, w_qkv, b_qkv, w_proj, b_proj):
        import jax, jax.numpy as jnp
        import numpy as np
        N_HEADS = 12
        B, N, D = x.shape
        H = N_HEADS
        hd = D // H
        scale = hd ** (-0.5)
        qkv = x @ w_qkv + b_qkv
        qkv = qkv.reshape(B, N, 3, H, hd)
        qkv = jnp.transpose(qkv, (2, 0, 3, 1, 4))
        q, k, v = (qkv[0], qkv[1], qkv[2])
        scores = jnp.einsum('bhqd,bhkd->bhqk', q, k) * scale
        attn = jax.nn.softmax(scores, axis=-1)
        out = jnp.einsum('bhqk,bhkd->bhqd', attn, v)
        out = jnp.transpose(out, (0, 2, 1, 3)).reshape(B, N, D)
        return out @ w_proj + b_proj

    def _L0_ffn_ref(x, Wg, W1, b1, W2, b2):
        import jax, jax.numpy as jnp
        import numpy as np
        B, T, H, F, E = (128, 32, 192, 768, 3)
        scores = jax.nn.softmax(jnp.mean(x, axis=1) @ Wg.T, axis=-1)
        _, idx = jax.lax.top_k(scores, 1)
        sel = idx[:, 0]
        h = jax.nn.gelu(jnp.einsum('bth,ehf->betf', x, W1) + b1[None, :, None, :], approximate=False)
        y = jnp.einsum('betf,efh->beth', h, W2) + b2[None, :, None, :]
        w = scores * jax.nn.one_hot(sel, E, dtype=scores.dtype)
        out = jnp.einsum('beth,be->bth', y, w)
        return out
    h = _L0_tok_ref(x, L0_tok_patch_w, L0_tok_patch_b, L0_tok_ln_g, L0_tok_ln_b, L0_tok_qkv_w, L0_tok_qkv_b, L0_tok_proj_w, L0_tok_proj_b, L0_tok_ff1_w, L0_tok_ff1_b, L0_tok_ff2_w, L0_tok_ff2_b)
    h = _layernorm(h + _L0_attn_ref(h, L0_attn_w_qkv, L0_attn_b_qkv, L0_attn_w_proj, L0_attn_b_proj), axis=-1)
    h = _layernorm(h + _L0_ffn_ref(h, L0_ffn_Wg, L0_ffn_W1, L0_ffn_b1, L0_ffn_W2, L0_ffn_b2), axis=-1)
    return h

_drawn_inputs = setup_inputs


def setup_inputs(seed=0):
    import zlib

    import numpy as np

    out = dict(_drawn_inputs(seed))
    spreads = {'L0_tok_patch_b': (0.0, 0.1),
     'L0_tok_ln_g': (1.0, 0.2),
     'L0_tok_ln_b': (0.0, 0.1),
     'L0_tok_qkv_b': (0.0, 0.3),
     'L0_tok_proj_b': (0.0, 0.1),
     'L0_tok_ff1_b': (0.0, 0.1),
     'L0_tok_ff2_b': (0.0, 0.1),
     'L0_ffn_b1': (0.0, 0.66),
     'L0_ffn_b2': (0.0, 0.1)}
    factors = {'L0_tok_qkv_w': 5.885, 'L0_attn_b_qkv': 3.542, 'L0_attn_b_proj': 4.035}
    for name, (base, spread) in spreads.items():
        noise = np.random.default_rng([zlib.crc32(name.encode()), seed]).standard_normal(out[name].shape)
        drawn = base * np.exp(spread * noise) if base else spread * noise
        out[name] = jnp.asarray(drawn.astype(out[name].dtype))
    for name, factor in factors.items():
        out[name] = (out[name] * factor).astype(out[name].dtype)
    return out
```

```python
from contextlib import ExitStack

import numpy as np

import concourse.bass as bass
from concourse import mybir

F32 = mybir.dt.float32
F32R = mybir.dt.float32r
BF16 = mybir.dt.bfloat16
F16 = mybir.dt.float16
I32 = mybir.dt.int32
ACT = mybir.ActivationFunctionType
ALU = mybir.AluOpType
AX = mybir.AxisListType

P = 128
IMGS, TOK = 64, 64
D, FF, NH, DH = 192, 768, 12, 16
FA, FB = 128, 64
TILE = 512
NT = IMGS * TOK // TILE
BLK = TILE // P
NC = FF // P
PC = 3 * 16 * 16 // P
EPS = 1e-5
NE = 3
GRP = TILE // TOK
NB = IMGS // GRP + NE - 1
SLOTS = NB * GRP
W_FF = 2 * FF + NC * 2 * P
W_MOE = 2 * FF + NC * D
VW = 2 * DH + 2


def need(eng, sem, value):
    if isinstance(value, int) and value <= 0:
        return
    eng.wait_ge(sem, value)


def tiles(eng, body, last):
    body(0, 0)
    with eng.Fori(0, 3) as i:
        body(2 * i + 1, 1)
        body(2 * i + 2, 0)
    for t in range(7, last + 1):
        body(t, t % 2)


def product_fm(nc, out, w, cols, x, last=True):
    wah, wal, wbh, wbl = w
    xah, xal, xb = x
    nc.tensor.matmul(out, wah[:, cols], xah, start=True, stop=False)
    nc.tensor.matmul(out, wah[:, cols], xal, start=False, stop=False)
    nc.tensor.matmul(out, wal[:, cols], xah, start=False, stop=False)
    nc.tensor.matmul(out, wbh[:, cols], xb, start=False, stop=False)
    return nc.tensor.matmul(out, wbl[:, cols], xb, start=False, stop=last)


def product_tm(nc, out, x, w, cols, last=True):
    wah, wal, wbh, wbl = w
    xah, xal, xb = x
    nc.tensor.matmul(out, xah, wah[:, cols], start=True, stop=False)
    nc.tensor.matmul(out, xah, wal[:, cols], start=False, stop=False)
    nc.tensor.matmul(out, xal, wah[:, cols], start=False, stop=False)
    nc.tensor.matmul(out, xb, wbh[:, cols], start=False, stop=False)
    return nc.tensor.matmul(out, xb, wbl[:, cols], start=False, stop=last)


class Memory:
    def __init__(self, nc, ctx, stage):
        self.nc, self.ctx, self.stage = nc, ctx, stage
        self.semaphores = []
        ctx.callback(self.clear)

    def clear(self):
        self.nc.all_engine_barrier()
        self.nc.clear_and_free_semaphores(self.semaphores)
        self.nc.all_engine_barrier()

    def sb(self, name, shape, dt):
        return self.ctx.enter_context(self.nc.sbuf_tensor(f"{self.stage}_{name}", shape, dt))

    def ps(self, name, shape, dt=F32):
        return self.ctx.enter_context(self.nc.psum_tensor(f"{self.stage}_{name}", shape, dt))

    def sem(self, name):
        self.semaphores.append(self.nc.alloc_semaphore(f"{self.stage}_{name}"))
        return self.semaphores[-1]

    def sems(self, name, n):
        return [self.sem(f"{name}{i}") for i in range(n)]


def patch_stage(nc, stored, patches, w_patch, rows, ident_d, state_out):
    with ExitStack() as ctx:
        m = Memory(nc, ctx, "pe")
        raw = m.sb("raw", [P, 2, PC, TILE], F32)
        xh = m.sb("xh", [P, 2, PC, TILE], F32R)
        xl = m.sb("xl", [P, 2, PC, TILE], F32R)
        wraw = m.sb("wraw", [P, PC * D], F32)
        wh = m.sb("wh", [P, PC * D], F32R)
        wl = m.sb("wl", [P, PC * D], F32R)
        cst = m.sb("cst", [P, 3, D], F32)
        lnb = m.sb("lnb", [P, D], F32)
        ident = m.sb("ident", [P, P], F32)
        half = m.sb("half", [P, BLK], F32)
        y = m.sb("y", [P, BLK, D], F32)
        st = m.sb("st", [P, BLK, 6], F32)
        mv = m.sb("mv", [P, BLK, 2], F32)
        ve = m.sb("ve", [P, BLK], F32)
        mark = m.sb("mark", [P, 1], F32)
        rstd = m.sb("rstd", [P, BLK], F32)
        z = m.sb("z", [P, BLK, D], F32)
        x0 = m.sb("x0", [P, BLK, 2 * P], F32)
        out = m.sb("out", [P, 2, 3, TILE], F32R)
        emb = [m.ps(f"emb{i}", [P, BLK, 2 * P]) for i in range(2)]
        tr = m.ps("tr", [P, 2, TILE])
        s_w, s_const = m.sem("w_loaded"), m.sem("const_loaded")
        s_wh, s_wl, s_pos, s_half = m.sem("w_hi"), m.sem("w_lo"), m.sem("pos_ready"), m.sem("half_ready")
        s_ld = m.sems("patches_loaded", 2)
        s_hi, s_lo, s_emb, s_y = m.sem("patch_hi"), m.sem("patch_lo"), m.sem("embedded"), m.sem("emb_read")
        s_st, s_ag, s_ve, s_rs, s_z, s_x0, s_dup = (m.sem(n) for n in
            ("stats", "aggr", "var_eps", "rstd", "centered", "x0_ready", "x0_dup"))
        s_tr, s_oh, s_ol = m.sem("transposed"), m.sem("out_hi"), m.sem("out_lo")
        s_st_out = stored
        with nc.Block() as block:

            @block.sync
            def _(sp):
                sp.dma_start(wraw[:], w_patch).then_inc(s_w, 16)
                sp.dma_start(raw[:, 0], patches[0]).then_inc(s_ld[0], 16)
                sp.dma_start(cst[:], rows[:, 0:3]).then_inc(s_const, 16)
                sp.dma_start(lnb[:], rows[:, 3]).then_inc(s_const, 16)
                sp.dma_start(ident[:], ident_d).then_inc(s_const, 16)

                def load(t, u):
                    need(sp, s_hi, 3 * (t - 1))
                    need(sp, s_lo, 3 * (t - 1))
                    src = patches[t] if isinstance(t, int) else patches[bass.ds(t, 1)].squeeze(0)
                    sp.dma_start(raw[:, u], src).then_inc(s_ld[u], 16)

                sp.dma_start(raw[:, 1], patches[1]).then_inc(s_ld[1], 16)
                with sp.Fori(0, 3) as i:
                    load(2 * i + 2, 0)
                    load(2 * i + 3, 1)

            @block.gpsimd
            def _(pool):
                nc.gpsimd.memset(half[:], -0.5).then_inc(s_half, 1)
                pool.wait_ge(s_half, 1)

                def store(t, u):
                    need(pool, s_ve, t + 1)
                    need(pool, s_x0, BLK * t)
                    nc.gpsimd.tensor_tensor(rstd[:], ve[:], half[:], ALU.pow).then_inc(s_rs, 1)
                    pool.wait_ge(s_oh, 2 * t + 2)
                    pool.wait_ge(s_ol, 2 * t + 2)
                    dst = state_out[:, :, bass.ds(t * TILE, TILE)]
                    pool.dma_start(dst, out[:, u].bitcast(F32)).then_inc(s_st_out[u], 16)

                tiles(pool, store, NT - 1)
                for s in s_st_out:
                    pool.wait_ge(s, 16 * NT // 2)

            @block.scalar
            def _(act):
                act.wait_ge(s_w, 16)
                nc.scalar.copy(wh[:], wraw[:]).then_inc(s_wh, 1)

                def split(t, u):
                    need(act, s_ld[u], 16 * ((t - u) // 2 + 1) if isinstance(t, int) else (t - u) * 8 + 16)
                    need(act, s_emb, BLK * (t - 1))
                    for c in range(0, PC, 2):
                        nc.scalar.copy(xh[:, u, c:c + 2], raw[:, u, c:c + 2]).then_inc(s_hi, 1)

                def finish(t, u):
                    act.wait_ge(s_x0, BLK * t + BLK)
                    need(act, s_tr, 2 * t)
                    nc.scalar.copy(x0[:, :, P + FB:], x0[:, :, P:P + FB]).then_inc(s_dup, 1)
                    act.wait_ge(s_tr, 2 * t + 2)
                    need(act, s_st_out[u], 8 * (t - u))
                    nc.scalar.copy(out[:, u, 0], tr[:, 0]).then_inc(s_oh, 1)
                    nc.scalar.copy(out[:, u, 2], tr[:, 1]).then_inc(s_oh, 1)

                def body(t, u):
                    if not (isinstance(t, int) and t == NT - 1):
                        split(t + 1, 1 - u)
                    finish(t, u)

                split(0, 0)
                tiles(act, body, NT - 1)

            @block.vector
            def _(dve):
                dve.wait_ge(s_wh, 1)
                nc.vector.tensor_tensor(wl[:], wraw[:], wh[:].bitcast(F32), ALU.subtract).then_inc(s_wl, 1)
                dve.wait_ge(s_const, 48)
                nc.vector.tensor_tensor(cst[:, 2], cst[:, 2], lnb[:], ALU.add).then_inc(s_pos, 1)
                dve.wait_ge(s_pos, 1)

                def split(t, u):
                    need(dve, s_emb, BLK * (t - 1))
                    for k, c in enumerate(range(0, PC, 2)):
                        dve.wait_ge(s_hi, 3 * t + k + 1)
                        nc.vector.tensor_tensor(xl[:, u, c:c + 2], raw[:, u, c:c + 2],
                                                xh[:, u, c:c + 2].bitcast(F32), ALU.subtract).then_inc(s_lo, 1)

                def finish(t, u):
                    dve.wait_ge(s_emb, BLK * t + BLK)
                    nc.vector.tensor_tensor(y[:], emb[u][:, :, 0:D],
                                            cst[:, 0].unsqueeze(1).broadcast_to([P, BLK, D]), ALU.add).then_inc(s_y, 1)
                    dve.wait_ge(s_y, t + 1)
                    for b in range(BLK):
                        nc.vector.bn_stats(st[:, b], y[:, b]).then_inc(s_st, 1)
                    dve.wait_ge(s_st, BLK * t + BLK)
                    nc.vector.memset(mark[:], 0.0)
                    for b in range(BLK):
                        nc.vector.bn_aggr(mv[:, b], st[:, b]).then_inc(s_ag, 1)
                    dve.wait_ge(s_ag, BLK * t + BLK)
                    need(dve, s_rs, t)
                    nc.vector.tensor_scalar(ve[:], mv[:, :, 1], EPS, None, ALU.add).then_inc(s_ve, 1)
                    for b in range(BLK):
                        nc.vector.scalar_tensor_tensor(out=z[:, b], in0=y[:, b], scalar=mv[:, b, 0:1], in1=cst[:, 1],
                                                       op0=ALU.subtract, op1=ALU.mult).then_inc(s_z, 1)
                    dve.wait_ge(s_rs, t + 1)
                    need(dve, s_tr, 2 * t)
                    for b in range(BLK):
                        dve.wait_ge(s_z, BLK * t + b + 1)
                        nc.vector.scalar_tensor_tensor(out=x0[:, b, 0:D], in0=z[:, b], scalar=rstd[:, b:b + 1],
                                                       in1=cst[:, 2], op0=ALU.mult, op1=ALU.add).then_inc(s_x0, 1)
                    dve.wait_ge(s_oh, 2 * t + 1)
                    nc.vector.tensor_tensor(out[:, u, 1], tr[:, 0], out[:, u, 0].bitcast(F32),
                                            ALU.subtract).then_inc(s_ol, 1)
                    dve.wait_ge(s_oh, 2 * t + 2)
                    low = out[FB:P, u, 2]
                    nc.vector.tensor_tensor(low, tr[FB:P, 1], low.bitcast(F32), ALU.subtract).then_inc(s_ol, 1)

                def body(t, u):
                    if not (isinstance(t, int) and t == NT - 1):
                        split(t + 1, 1 - u)
                    finish(t, u)

                split(0, 0)
                tiles(dve, body, NT - 1)

            @block.tensor
            def _(pe):
                pe.wait_ge(s_wl, 1)
                pe.wait_ge(s_const, 48)

                def embed(t, u):
                    need(pe, s_y, t - 1)
                    pe.wait_ge(s_lo, 3 * t + 3)
                    for b in range(BLK):
                        o = emb[u][:, b, 0:D]
                        for c in range(PC):
                            h, l = xh[:, u, c, P * b:P * b + P], xl[:, u, c, P * b:P * b + P]
                            w0, w1 = wh[:, D * c:D * c + D], wl[:, D * c:D * c + D]
                            nc.tensor.matmul(o, h, w0, start=c == 0, stop=False)
                            nc.tensor.matmul(o, h, w1, start=False, stop=False)
                            last = nc.tensor.matmul(o, l, w0, start=False, stop=c == PC - 1)
                        last.then_inc(s_emb, 1)

                def transpose(t, u):
                    pe.wait_ge(s_dup, t + 1)
                    need(pe, s_oh, 2 * t)
                    need(pe, s_ol, 2 * t)
                    for k in range(2):
                        for b in range(BLK):
                            last = nc.tensor.transpose(tr[:, k, P * b:P * b + P], x0[:, b, P * k:P * k + P], ident[:])
                        last.then_inc(s_tr, 1)

                def body(t, u):
                    if not (isinstance(t, int) and t == NT - 1):
                        embed(t + 1, 1 - u)
                    transpose(t, u)

                embed(0, 0)
                tiles(pe, body, NT - 1)


def ff_stage(nc, stored, name, state_in, state_out, w_ff, b_ff, ident_d, residual):
    LAG, HB = 3, 4
    RING = 6
    with ExitStack() as ctx:
        m = Memory(nc, ctx, name)
        x = m.sb("x", [P, 2, 3, TILE], F32R)
        wraw = m.sb("wraw", [P, W_FF], F32)
        wh = m.sb("wh", [P, W_FF], F32R)
        wl = m.sb("wl", [P, W_FF], F32R)
        bias = m.sb("bias", [P, NC + 2], F32)
        idraw = m.sb("idraw", [P, 2 * P], F32)
        ident = m.sb("ident", [P, 2, P], F32R)
        g = m.sb("g", [P, HB, TILE], F32)
        gh = m.sb("gh", [P, RING, TILE], F32R)
        gl = m.sb("gl", [P, RING, TILE], F32R)
        out = m.sb("out", [P, 2, 3, TILE], F32R)
        hid = [m.ps(f"hid{i}", [P, TILE]) for i in range(HB)]
        acc = [[m.ps(f"acc{u}{k}", [P, TILE]) for k in range(2)] for u in range(2)]
        s_w, s_wh, s_wl, s_id = m.sem("w_loaded"), m.sem("w_hi"), m.sem("w_lo"), m.sem("ident_ready")
        s_ld = m.sems("x_loaded", 2)
        s_hid, s_g, s_gh, s_gl, s_ff2 = (m.sem(n) for n in ("hidden", "gelu", "gelu_hi", "gelu_lo", "second_used"))
        s_oh, s_ol = m.sem("out_hi"), m.sem("out_lo")
        s_st = stored
        W1 = (wh[:, 0:FF], wl[:, 0:FF], wh[:, FF:2 * FF], wl[:, FF:2 * FF])

        def w2(w, f, k):
            at = 2 * FF + 2 * P * f + P * k
            return w[:, at:at + P]

        with nc.Block() as block:

            @block.sync
            def _(sp):
                sp.dma_start(wraw[:], w_ff).then_inc(s_w, 16)
                sp.dma_start(bias[:], b_ff).then_inc(s_w, 16)
                sp.dma_start(idraw[:], ident_d).then_inc(s_w, 16)
                sp.dma_start(x[:, 0].bitcast(F32), state_in[:, :, 0:TILE]).then_inc(s_ld[0], 16)
                sp.dma_start(x[:, 1].bitcast(F32), state_in[:, :, TILE:2 * TILE]).then_inc(s_ld[1], 16)

                def load(t, u):
                    sp.wait_ge(s_ff2, NC * (t - 1))
                    sp.dma_start(x[:, u].bitcast(F32), state_in[:, :, bass.ds(t * TILE, TILE)]).then_inc(s_ld[u], 16)

                with sp.Fori(0, 3) as i:
                    load(2 * i + 2, 0)
                    load(2 * i + 3, 1)

            @block.gpsimd
            def _(pool):
                def store(t, u):
                    pool.wait_ge(s_oh, 2 * t + 2)
                    pool.wait_ge(s_ol, 2 * t + 2)
                    pool.dma_start(state_out[:, :, bass.ds(t * TILE, TILE)], out[:, u].bitcast(F32)).then_inc(s_st[u], 16)

                tiles(pool, store, NT - 1)
                for s in s_st:
                    pool.wait_ge(s, 16 * NT // 2)

            @block.scalar
            def _(act):
                act.wait_ge(s_w, 48)
                nc.scalar.copy(wh[:], wraw[:]).then_inc(s_wh, 1)

                def finish(t, u):
                    act.wait_ge(s_ff2, NC * t + NC)
                    need(act, s_st[u], 8 * (t - u))
                    nc.scalar.activation(out[:, u, 0], acc[u][0][:], ACT.Identity, bias=bias[:, NC:NC + 1]).then_inc(s_oh, 1)
                    nc.scalar.activation(out[:, u, 2], acc[u][1][:], ACT.Identity, bias=bias[:, NC + 1:]).then_inc(s_oh, 1)

                def body(t, u):
                    if isinstance(t, int) and t == NT:
                        return finish(t - 1, 1 - u)
                    for f in range(NC):
                        n = (NC * u + f)
                        act.wait_ge(s_hid, NC * t + f + 1)
                        need(act, s_gl, NC * t + f + 1 - HB)
                        nc.scalar.activation(g[:, n % HB], hid[n % HB][:], ACT.Gelu_apprx_tanh,
                                             bias=bias[:, f:f + 1]).then_inc(s_g, 1)
                        if f == LAG + 1 and not (isinstance(t, int) and t == 0):
                            finish(t - 1, 1 - u)

                tiles(act, body, NT)

            @block.vector
            def _(dve):
                dve.wait_ge(s_wh, 1)
                nc.vector.tensor_tensor(wl[:], wraw[:], wh[:].bitcast(F32), ALU.subtract).then_inc(s_wl, 1)
                nc.vector.tensor_copy(ident[:].rearrange("p k c -> p (k c)"), idraw[:]).then_inc(s_id, 1)

                def finish(t, u):
                    dve.wait_ge(s_oh, 2 * t + 1)
                    nc.vector.scalar_tensor_tensor(out=out[:, u, 1], in0=acc[u][0][:], scalar=bias[:, NC:NC + 1],
                                                   in1=out[:, u, 0].bitcast(F32), op0=ALU.add,
                                                   op1=ALU.subtract).then_inc(s_ol, 1)
                    dve.wait_ge(s_oh, 2 * t + 2)
                    low = out[FB:P, u, 2]
                    nc.vector.scalar_tensor_tensor(out=low, in0=acc[u][1][FB:P], scalar=bias[FB:P, NC + 1:],
                                                   in1=low.bitcast(F32), op0=ALU.add, op1=ALU.subtract).then_inc(s_ol, 1)

                def body(t, u):
                    if isinstance(t, int) and t == NT:
                        return finish(t - 1, 1 - u)
                    for f in range(NC):
                        n = (NC * u + f)
                        dve.wait_ge(s_g, NC * t + f + 1)
                        need(dve, s_ff2, NC * t + f + 1 - RING)
                        nc.vector.tensor_copy(gh[:, n % RING], g[:, n % HB]).then_inc(s_gh, 1)
                        dve.wait_ge(s_gh, NC * t + f + 1)
                        nc.vector.tensor_tensor(gl[:, n % RING], g[:, n % HB], gh[:, n % RING].bitcast(F32),
                                                ALU.subtract).then_inc(s_gl, 1)
                        if f == LAG + 1 and not (isinstance(t, int) and t == 0):
                            finish(t - 1, 1 - u)

                tiles(dve, body, NT)

            @block.tensor
            def _(pe):
                pe.wait_ge(s_wl, 1)
                pe.wait_ge(s_id, 1)

                def second(t, u, f):
                    n = NC * u + f
                    pe.wait_ge(s_gl, NC * t + f + 1)
                    if f == 0:
                        need(pe, s_ol, 2 * (t - 1))
                        need(pe, s_oh, 2 * (t - 1))
                    h, l = gh[:, n % RING], gl[:, n % RING]
                    if f == NC - 1 and residual:
                        nc.tensor.matmul(acc[u][0][:], ident[:, 0], x[:, u, 0], start=False, stop=False)
                        nc.tensor.matmul(acc[u][0][:], ident[:, 0], x[:, u, 1], start=False, stop=False)
                        nc.tensor.matmul(acc[u][1][:], ident[:, 1], x[:, u, 2], start=False, stop=False)
                    for k in range(2):
                        o = acc[u][k][:]
                        end = f == NC - 1
                        nc.tensor.matmul(o, w2(wh, f, k), h, start=f == 0, stop=False)
                        nc.tensor.matmul(o, w2(wl, f, k), h, start=False, stop=False)
                        last = nc.tensor.matmul(o, w2(wh, f, k), l, start=False, stop=end)
                    last.then_inc(s_ff2, 1)

                def body(t, u):
                    if isinstance(t, int) and t == NT:
                        for f in range(LAG):
                            second(t - 1, 1 - u, f + NC - LAG)
                        return
                    need(pe, s_ld[u], (t - u) * 8 + 16)
                    for f in range(NC):
                        n = NC * u + f
                        need(pe, s_g, NC * t + f + 1 - HB)
                        product_fm(nc, hid[n % HB][:], W1, slice(P * f, P * f + P),
                                   (x[:, u, 0], x[:, u, 1], x[:, u, 2])).then_inc(s_hid, 1)
                        if f >= LAG:
                            second(t, u, f - LAG)
                        elif not (isinstance(t, int) and t == 0):
                            second(t - 1, 1 - u, f + NC - LAG)

                tiles(pe, body, NT)


def att_stage(nc, stored, name, state_in, state_res, w_att, cols_d, ident_d, state_out=None, rows_d=None, sel_d=None,
              hidden=None, means=None):
    normed = state_out is None
    WP = D if normed else 2 * P
    WQ = 4 * P + D
    SC = NH * TOK
    HP = NH // 2
    HA = FA // DH
    HBN = NH - HA
    LASTS = NT * BLK
    with ExitStack() as ctx:
        m = Memory(nc, ctx, name)
        x = m.sb("x", [P, 2, 3, TILE], F32R)
        res = m.sb("res", [P, 2, 3, TILE], F32R)
        wh = m.sb("wh", [P, 2, WQ + WP], F32R)
        wl = m.sb("wl", [P, 2, WQ + WP], F32R)
        cols = m.sb("cols", [P, 8], F32)
        idf = m.sb("idf", [P, P], F32)
        idh = m.sb("idh", [P, P], F16)
        idr = m.sb("idr", [P, 2, D if normed else P], F32R)
        q = m.sb("q", [P, 2, 3, GRP * P], F32R)
        ks = m.sb("ks", [P, 2, 2, 2, TILE], F32R)
        kbA = m.sb("kbA", [P, 2, 2, HA, 2 * P], F32R)
        kbB = m.sb("kbB", [P, 2, 2, HBN, 2 * P], F32R)
        vt = m.sb("vt", [P, 2, 3, D], BF16)
        vr = m.sb("vr", [P, 2, 2, D], F32)
        vb = m.sb("vb", [P, 2, 2, BLK * 3, HP, VW], BF16)
        mx = m.sb("mx", [P, NH], F32)
        es = m.sb("es", [P, SC], F32)
        ee = m.sb("ee", [P, 2, SC], F32)
        eh = m.sb("eh", [P, 2, SC], F16)
        el = m.sb("el", [P, 2, SC], F16)
        et = m.sb("et", [P, 2, 2, SC], F16)
        rs = m.sb("rs", [P, NH], F32)
        o = m.sb("o", [P, 2 * P], F32)
        ot = m.sb("ot", [P, 2, 3, TILE], F32R)
        sc = m.ps("sc", [P, 1024])
        pt = m.ps("pt", [P, 2, 1024], F16)
        pq = m.ps("pq", [P, TILE])
        pv = m.ps("pv", [P, TILE])
        po = m.ps("po", [P, TILE])
        pp = m.ps("pp", [P, TILE])
        s_w, s_wl, s_wh, s_zero, s_id = (m.sem(n) for n in ("w_loaded", "w_lo", "w_hi", "zeroed", "ident"))
        s_x, s_res = m.sems("x_loaded", 2), m.sems("res_loaded", 2)
        s_kb = m.sems("k_placed", 2)
        s_qk, s_qkh, s_qkl = m.sem("qk"), m.sem("qk_hi"), m.sem("qk_lo")
        s_v, s_va, s_vr, s_vb2, s_vr2, s_vc, s_vpd, s_vpa = (m.sem(n) for n in
            ("v", "v_first", "v_rest", "v_second", "v_rest2", "v_third", "v_placed_dve", "v_placed_act"))
        s_sc, s_mx, s_sub, s_ex, s_eh, s_el = (m.sem(n) for n in ("scores", "max", "sub", "exp", "e_hi", "e_lo"))
        s_t, s_th, s_tl, s_pv, s_rc, s_nm, s_dup = (m.sem(n) for n in
            ("e_transposed", "et_hi", "et_lo", "pv", "recip", "normed", "o_dup"))
        s_ot, s_oth, s_otl, s_pj = m.sem("o_transposed"), m.sem("ot_hi"), m.sem("ot_lo"), m.sem("projected")
        s_oh, s_ol = m.sem("out_hi"), m.sem("out_lo")
        s_st = stored
        if normed:
            rows = m.sb("rows", [P, D], F32)
            sel = m.sb("sel", [P, 2], F32)
            y = m.sb("y", [P, D], F32)
            st = m.sb("st", [P, 6], F32)
            mv = m.sb("mv", [P, 2], F32)
            ve = m.sb("ve", [P, 1], F32)
            mark = m.sb("mark", [P, 1], F32)
            half = m.sb("half", [P, 1], F32)
            rstd = m.sb("rstd", [P, 1], F32)
            out = m.sb("out", [P, 2, D], F32)
            s_y, s_bs, s_ag, s_ve, s_rt, s_mm, s_half = (m.sem(n) for n in
                ("y", "stats", "aggr", "var_eps", "rstd", "mean", "half"))
            s_me = m.sem("means_out")
        else:
            out = m.sb("out", [P, 1, 3, TILE], F32R)

        def weights(at):
            return wh[:, 0, at:], wl[:, 0, at:], wh[:, 1, at:], wl[:, 1, at:]

        WK, WV, WO = weights(0), weights(4 * P), weights(WQ)
        wraw = m.sb("wraw", [P, 2 * (WQ + WP)], F32)[:]
        idraw = m.sb("idraw", [P, 2 * (D if normed else P)], F32)[:]

        def at_start(t):
            return isinstance(t, int) and t == 0

        with nc.Block() as block:

            @block.sync
            def _(sp):
                sp.dma_start(x[:, 0].bitcast(F32), state_in[:, :, 0:TILE]).then_inc(s_x[0], 16)
                sp.dma_start(wraw, w_att).then_inc(s_w, 16)
                sp.dma_start(idraw, ident_d[0]).then_inc(s_w, 16)
                sp.dma_start(idf[:], ident_d[1]).then_inc(s_w, 16)
                sp.dma_start(cols[:], cols_d).then_inc(s_w, 16)
                if normed:
                    sp.dma_start(rows[:], rows_d).then_inc(s_w, 16)
                    sp.dma_start(sel[:], sel_d).then_inc(s_w, 16)
                sp.dma_start(x[:, 1].bitcast(F32), state_in[:, :, TILE:2 * TILE]).then_inc(s_x[1], 16)
                sp.dma_start(res[:, 0].bitcast(F32), state_res[:, :, 0:TILE]).then_inc(s_res[0], 16)

                def place(t, u, unit):
                    read, made = BLK * (t - 1) + 2 * unit + 2, 4 * t + 2
                    if not isinstance(t, int):
                        read, made = sp.snap(read), sp.snap(made)
                    need(sp, s_sc, read)
                    sp.wait_ge(s_qkl, made)
                    for hd in range(HA):
                        r = slice(DH * hd, DH * hd + DH)
                        sp.dma_start(kbA[r, unit, :, hd, :].bitcast(F32),
                                     ks[r, u, 0, :, 2 * P * unit:2 * P * unit + 2 * P].bitcast(F32)).then_inc(s_kb[unit], 16)
                    for hd in range(HBN):
                        for k in range(2):
                            r = slice(FB * k + DH * hd, FB * k + DH * hd + DH)
                            sp.dma_start(kbB[r, unit, :, hd, :].bitcast(F32),
                                         ks[r, u, 1, :, 2 * P * unit:2 * P * unit + 2 * P].bitcast(F32)).then_inc(s_kb[unit], 16)

                def body(t, u):
                    last = isinstance(t, int) and t >= NT - 1
                    if not last:
                        place(t + 1, 1 - u, 0)
                        place(t + 1, 1 - u, 1)
                        need(sp, s_pj, t * (4 if normed else 2))
                        sp.dma_start(res[:, 1 - u].bitcast(F32),
                                     state_res[:, :, bass.ds((t + 1) * TILE, TILE)]).then_inc(s_res[1 - u], 16)

                def load_x(t, u):
                    sp.wait_ge(s_v, 2 * (t - 1))
                    sp.dma_start(x[:, u].bitcast(F32), state_in[:, :, bass.ds(t * TILE, TILE)]).then_inc(s_x[u], 16)

                sp.wait_ge(s_zero, 3)
                sp.wait_ge(s_wl, 1)
                sp.wait_ge(s_id, 2)
                place(0, 0, 0)
                place(0, 0, 1)
                load_x(2, 0)
                body(0, 0)
                with sp.Fori(0, 2) as i:
                    for d in (1, 2):
                        load_x(2 * i + d + 2, d % 2)
                        body(2 * i + d, d % 2)
                load_x(7, 1)
                body(5, 1)
                body(6, 0)

            @block.gpsimd
            def _(pool):
                if normed:
                    nc.gpsimd.memset(half[:], -0.5).then_inc(s_half, 1)
                    pool.wait_ge(s_half, 1)

                def slot(t, u, j):
                    n = BLK * t + j
                    if not (isinstance(t, int) and t >= NT):
                        pool.wait_ge(s_eh, n + 1)
                        need(pool, s_t, n - 1)
                        nc.gpsimd.tensor_tensor(el[:, j % 2], ee[:, j % 2], eh[:, j % 2], ALU.subtract).then_inc(s_el, 1)
                    if normed and not (isinstance(n, int) and not 3 <= n < LASTS + 3):
                        need(pool, s_ve, n - 2)
                        nc.gpsimd.tensor_tensor(rstd[:], ve[:], half[:], ALU.pow).then_inc(s_rt, 1)
                        pool.wait_ge(s_oh, n - 2)
                        pool.dma_start(hidden[bass.ds((n - 3) * P, P), :], out[:, (j - 3) % 2]).then_inc(s_st[(j - 3) % 2], 16)
                    if not normed and j == 3 and not at_start(t):
                        pool.wait_ge(s_oh, 2 * t)
                        pool.wait_ge(s_ol, 2 * t)
                        pool.dma_start(state_out[:, :, bass.ds((t - 1) * TILE, TILE)], out[:, 0].bitcast(F32)).then_inc(s_st[0], 16)

                tiles(pool, lambda t, u: [slot(t, u, j) for j in range(BLK)], NT)
                if normed:
                    pool.wait_ge(s_st[0], 16 * LASTS // 2)
                    pool.wait_ge(s_st[1], 16 * LASTS // 2)
                else:
                    pool.wait_ge(s_st[0], 16 * NT)

            @block.scalar
            def _(act):
                act.wait_ge(s_w, 96 if normed else 64)
                nc.scalar.copy(wh[:].rearrange("p a b -> p (a b)"), wraw).then_inc(s_wh, 1)
                nc.scalar.copy(idr[:].rearrange("p a b -> p (a b)"), idraw).then_inc(s_id, 1)
                nc.scalar.copy(idh[:], idf[:]).then_inc(s_id, 1)

                def project(t, u, j):
                    act.wait_ge(s_qk, 4 * t + j + 1)
                    b = cols[:, j:j + 1]
                    if j < 2:
                        for unit in range(2):
                            need(act, s_kb[unit], 16 * 16 * (t - 1))
                        nc.scalar.activation(ks[:, u, j, 0], pq[:], ACT.Identity, bias=b).then_inc(s_qkh, 1)
                    else:
                        need(act, s_sc, BLK * (t - 1))
                        dst = q[:, u, 2 * (j - 2)].rearrange("p (s n) -> p s n", n=P)[:, :, 0:TOK]
                        src = pq[:].rearrange("p (s n) -> p s n", n=TOK)
                        nc.scalar.activation(dst, src, ACT.Identity, bias=b).then_inc(s_qkh, 1)

                def values(t, u, v):
                    k = 2 * t + v
                    src = pv[:, 0:2 * D].rearrange("p (b d) -> p b d", b=2)
                    act.wait_ge(s_v, k + 1)
                    need(act, s_vpd, 2 * k)
                    need(act, s_vpa, 2 * k)
                    nc.scalar.copy(vt[:, :, 0], src).then_inc(s_va, 1)
                    act.wait_ge(s_vr, k + 1)
                    nc.scalar.copy(vt[:, :, 1], vr[:, 0]).then_inc(s_vb2, 1)
                    act.wait_ge(s_vr2, k + 1)
                    nc.scalar.copy(vt[:, :, 2], vr[:, 1]).then_inc(s_vc, 1)
                    act.wait_ge(s_vc, k + 1)
                    need(act, s_pv, BLK * (t - 1))
                    for i in range(2):
                        place_v(nc.scalar.copy, u, v, 1, i).then_inc(s_vpa, 1)

                def place_v(copy, u, v, par, i):
                    src = vt[TOK * i:TOK * i + TOK].rearrange("p b t (h c d) -> p (b t) h c d", c=2, d=DH)[:, :, :, par]
                    dst = vb[TOK * par:TOK * par + TOK, u, i, 6 * v:6 * v + 6, :, DH * par:DH * par + DH]
                    return copy(dst, src)

                def slot(t, u, j):
                    n = BLK * t + j
                    if not (isinstance(t, int) and t >= NT):
                        act.wait_ge(s_sub, n + 1)
                        need(act, s_el, n - 1)
                        nc.scalar.activation(ee[:, j % 2], es[:], ACT.Exp, scale=DH ** -0.5).then_inc(s_ex, 1)
                        act.wait_ge(s_ex, n + 1)
                        need(act, s_t, n - 1)
                        nc.scalar.copy(eh[:, j % 2], ee[:, j % 2]).then_inc(s_eh, 1)
                    if not (isinstance(n, int) and not 3 <= n < LASTS + 3):
                        act.wait_ge(s_ot, n - 2)
                        ou = u if j == 3 else 1 - u
                        at = slice(P * ((j + 1) % 4), P * ((j + 1) % 4) + P)
                        need(act, s_pj, (4 * (t - 1) if normed else 2 * (t - 1)) if not (isinstance(n, int) and n < 8) else 0)
                        nc.scalar.activation(ot[:, ou, 0, at], po[:, 0:P], ACT.Identity, bias=cols[:, 4:5]).then_inc(s_oth, 1)
                        nc.scalar.activation(ot[:, ou, 2, at], po[:, P:2 * P], ACT.Identity, bias=cols[:, 5:6]).then_inc(s_oth, 1)
                    if not (isinstance(t, int) and t >= NT - 1):
                        project(t + 1, 1 - u, j)
                        if j % 2:
                            values(t + 1, 1 - u, j // 2)
                    if not (isinstance(n, int) and not 2 <= n < LASTS + 2):
                        act.wait_ge(s_nm, 2 * (n - 1))
                        nc.scalar.copy(o[:, D:], o[:, FA:D]).then_inc(s_dup, 1)
                    if not (isinstance(n, int) and not 1 <= n < LASTS + 1):
                        act.wait_ge(s_t, n)
                        need(act, s_pv, n - 2)
                        nc.scalar.copy(et[:, (j + 1) % 2, 1], pt[:, 1, 0:SC]).then_inc(s_tl, 1)
                    if not normed and j >= 2 and not at_start(t):
                        k = 2 * (t - 1) + j - 2
                        act.wait_ge(s_pj, k + 1)
                        if j == 2:
                            need(act, s_st[0], 16 * (t - 1))
                        nc.scalar.activation(out[:, 0, 2 * (j - 2)], pp[:], ACT.Identity,
                                             bias=cols[:, 4 + j:5 + j]).then_inc(s_oh, 1)

                for j in range(BLK):
                    project(0, 0, j)
                    if j % 2:
                        if j == 1:
                            act.wait_ge(s_zero, 3)
                        values(0, 0, j // 2)
                tiles(act, lambda t, u: [slot(t, u, j) for j in range(BLK)], NT)

            @block.vector
            def _(dve):
                nc.vector.memset(q[:].rearrange("p a b c -> p (a b c)").bitcast(F32), 0.0).then_inc(s_zero, 1)
                nc.vector.memset(vb[:].rearrange("p a b c d e -> p (a b c d e)").bitcast(F32), 0.0).then_inc(s_zero, 1)
                dve.wait_ge(s_zero, 2)
                for par in range(2):
                    ones = vb[TOK * par:TOK * par + TOK].rearrange("p a i k h w -> p (a i) k h w")
                    last = nc.vector.memset(ones[:, :, 0::3, :, 2 * DH + par:2 * DH + par + 1], 1.0)
                dve.wait_ge(s_wh, 1)
                nc.vector.tensor_tensor(wl[:].rearrange("p a b -> p (a b)"), wraw,
                                        wh[:].rearrange("p a b -> p (a b)").bitcast(F32), ALU.subtract).then_inc(s_wl, 1)
                dve.wait_ge(s_wl, 1)
                nc.vector.memset(kbA[:].rearrange("p a b c d -> p (a b c d)").bitcast(F32), 0.0)
                dve.wait_ge(s_id, 2)
                nc.vector.memset(kbB[:].rearrange("p a b c d -> p (a b c d)").bitcast(F32), 0.0).then_inc(s_zero, 1)

                def project(t, u, j):
                    dve.wait_ge(s_qkh, 4 * t + j + 1)
                    b = cols[:, j:j + 1]
                    if j < 2:
                        if j == 0:
                            for unit in range(2):
                                need(dve, s_kb[unit], 16 * 16 * (t - 1))
                        nc.vector.scalar_tensor_tensor(out=ks[:, u, j, 1], in0=pq[:], scalar=b,
                                                       in1=ks[:, u, j, 0].bitcast(F32), op0=ALU.add,
                                                       op1=ALU.subtract).then_inc(s_qkl, 1)
                        return
                    r = slice(0, P) if j == 2 else slice(FB, P)
                    view = lambda k: q[r, u, k].rearrange("p (s n) -> p s n", n=P)[:, :, 0:TOK]
                    src = pq[r].rearrange("p (s n) -> p s n", n=TOK)
                    hi, lo = (view(0), view(1)) if j == 2 else (view(2), view(2))
                    need(dve, s_sc, BLK * (t - 1))
                    nc.vector.scalar_tensor_tensor(out=lo, in0=src, scalar=cols[r, j:j + 1], in1=hi.bitcast(F32),
                                                   op0=ALU.add, op1=ALU.subtract).then_inc(s_qkl, 1)

                def values(t, u, v):
                    k = 2 * t + v
                    src = pv[:, 0:2 * D].rearrange("p (b d) -> p b d", b=2)
                    dve.wait_ge(s_va, k + 1)
                    nc.vector.tensor_tensor(vr[:, 0], src, vt[:, :, 0], ALU.subtract).then_inc(s_vr, 1)
                    dve.wait_ge(s_vb2, k + 1)
                    nc.vector.tensor_tensor(vr[:, 1], vr[:, 0], vt[:, :, 1], ALU.subtract).then_inc(s_vr2, 1)

                def place_values(t, u, v):
                    k = 2 * t + v
                    dve.wait_ge(s_vc, k + 1)
                    need(dve, s_pv, BLK * (t - 1))
                    for i in range(2):
                        src = vt[TOK * i:TOK * i + TOK].rearrange("p b t (h c d) -> p (b t) h c d", c=2, d=DH)[:, :, :, 0]
                        dst = vb[0:TOK, u, i, 6 * v:6 * v + 6, :, 0:DH]
                        nc.vector.tensor_copy(dst, src).then_inc(s_vpd, 1)

                def slot(t, u, j):
                    n = BLK * t + j
                    if not (isinstance(t, int) and t >= NT):
                        dve.wait_ge(s_sc, n + 1)
                        s3 = sc[:, 0:SC].rearrange("p (h k) -> p h k", h=NH)
                        need(dve, s_sub, n)
                        nc.vector.tensor_reduce(mx[:], s3, AX.X, ALU.max).then_inc(s_mx, 1)
                        dve.wait_ge(s_mx, n + 1)
                        need(dve, s_ex, n)
                        nc.vector.tensor_tensor(es[:].rearrange("p (h k) -> p h k", h=NH), s3,
                                                mx[:].unsqueeze(2).broadcast_to([P, NH, TOK]), ALU.subtract).then_inc(s_sub, 1)
                    if not (isinstance(n, int) and not 3 <= n < LASTS + 3):
                        dve.wait_ge(s_oth, 2 * (n - 2))
                        ou = u if j == 3 else 1 - u
                        at = slice(P * ((j + 1) % 4), P * ((j + 1) % 4) + P)
                        nc.vector.scalar_tensor_tensor(out=ot[:, ou, 1, at], in0=po[:, 0:P], scalar=cols[:, 4:5],
                                                       in1=ot[:, ou, 0, at].bitcast(F32), op0=ALU.add,
                                                       op1=ALU.subtract).then_inc(s_otl, 1)
                        low = ot[FB:P, ou, 2, at]
                        nc.vector.scalar_tensor_tensor(out=low, in0=po[FB:P, P:2 * P], scalar=cols[FB:P, 5:6],
                                                       in1=low.bitcast(F32), op0=ALU.add,
                                                       op1=ALU.subtract).then_inc(s_otl, 1)
                    if not (isinstance(t, int) and t >= NT - 1):
                        project(t + 1, 1 - u, j)
                        if j % 2:
                            values(t + 1, 1 - u, j // 2)
                    if not (isinstance(n, int) and not 2 <= n < LASTS + 2):
                        dve.wait_ge(s_pv, n - 1)
                        need(dve, s_ot, n - 2)
                        for i in range(2):
                            r = slice(TOK * i, TOK * i + TOK)
                            pr = po[r, 0:HP * 2 * VW].rearrange("p (h i w) -> p h i w", h=HP, i=2)[:, :, i]
                            nc.vector.reciprocal(rs[r].rearrange("p (h c) -> p h c", c=2), pr[:, :, 2 * DH:]).then_inc(s_rc, 1)
                        for i in range(2):
                            r = slice(TOK * i, TOK * i + TOK)
                            pr = po[r, 0:HP * 2 * VW].rearrange("p (h i w) -> p h i w", h=HP, i=2)[:, :, i]
                            dve.wait_ge(s_rc, 2 * (n - 2) + i + 1)
                            nc.vector.tensor_tensor(o[r, 0:D].rearrange("p (h c d) -> p h c d", h=HP, c=2),
                                                    pr[:, :, 0:2 * DH].rearrange("p h (c d) -> p h c d", c=2),
                                                    rs[r].rearrange("p (h c) -> p h c", c=2).unsqueeze(3).broadcast_to([TOK, HP, 2, DH]),
                                                    ALU.mult).then_inc(s_nm, 1)
                    if not (isinstance(n, int) and not 1 <= n < LASTS + 1):
                        dve.wait_ge(s_t, n)
                        need(dve, s_pv, n - 2)
                        nc.vector.tensor_copy(et[:, (j + 1) % 2, 0], pt[:, 0, 0:SC]).then_inc(s_th, 1)
                    if not (isinstance(t, int) and t >= NT - 1) and j % 2:
                        place_values(t + 1, 1 - u, j // 2)
                    if not normed and j >= 2 and not at_start(t):
                        k = 2 * (t - 1) + j - 2
                        dve.wait_ge(s_oh, k + 1)
                        r, c = (slice(0, P), 1) if j == 2 else (slice(FB, P), 2)
                        nc.vector.scalar_tensor_tensor(out=out[r, 0, c], in0=pp[r], scalar=cols[r, 4 + j:5 + j],
                                                       in1=out[r, 0, 2 * (j - 2)].bitcast(F32), op0=ALU.add,
                                                       op1=ALU.subtract).then_inc(s_ol, 1)
                    if normed and not (isinstance(n, int) and not 3 <= n < LASTS + 3):
                        c = n - 2
                        dve.wait_ge(s_pj, c)
                        nc.vector.tensor_tensor(y[:], pp[:, 0:D], rows[:], ALU.add).then_inc(s_y, 1)
                        dve.wait_ge(s_y, c)
                        nc.vector.bn_stats(st[:], y[:]).then_inc(s_bs, 1)
                        dve.wait_ge(s_bs, c)
                        nc.vector.memset(mark[:], 0.0)
                        nc.vector.bn_aggr(mv[:], st[:]).then_inc(s_ag, 1)
                        dve.wait_ge(s_ag, c)
                        nc.vector.tensor_scalar(ve[:], mv[:, 1:2], EPS, None, ALU.add).then_inc(s_ve, 1)
                        dve.wait_ge(s_rt, c)
                        need(dve, s_mm, c - 2)
                        need(dve, s_st[(j - 3) % 2], 8 * (n - 3 - (j - 3) % 2))
                        nc.vector.tensor_scalar(out[:, (j - 3) % 2], y[:], mv[:, 0:1], rstd[:], ALU.subtract,
                                                ALU.mult).then_inc(s_oh, 1)

                for j in range(BLK):
                    project(0, 0, j)
                    if j % 2:
                        values(0, 0, j // 2)
                        place_values(0, 0, j // 2)
                tiles(dve, lambda t, u: [slot(t, u, j) for j in range(BLK)], NT)
                if normed:
                    dve.wait_ge(s_mm, LASTS)
                    nc.vector.tensor_copy(means[:, 0:IMGS], pp[:, 2 * P:2 * P + IMGS]).then_inc(s_me, 1)
                    nc.vector.tensor_copy(means[0:FB, IMGS:2 * IMGS], pp[0:FB, 3 * P:3 * P + IMGS]).then_inc(s_me, 1)

            @block.tensor
            def _(pe):
                pe.wait_ge(s_wl, 1)
                pe.wait_ge(s_id, 2)
                pe.wait_ge(s_zero, 3)

                def project(t, u, j):
                    xs = (x[:, u, 0], x[:, u, 1], x[:, u, 2])
                    if j == 0:
                        need(pe, s_x[u], 8 * (t - u) + 16)
                    need(pe, s_qkl, 4 * t + j)
                    product_fm(nc, pq[:], WK, slice(P * j, P * j + P), xs).then_inc(s_qk, 1)
                    if j % 2:
                        v = j // 2
                        need(pe, s_vr, 2 * t + v)
                        for b in range(2):
                            at = slice(P * (2 * v + b), P * (2 * v + b) + P)
                            last = product_tm(nc, pv[:, D * b:D * b + D], tuple(k[:, at] for k in xs), WV, slice(0, D))
                        last.then_inc(s_v, 1)

                def scores(t, u, j):
                    n = BLK * t + j
                    unit, g = j // 2, j % 2
                    pe.wait_ge(s_kb[unit], 16 * 16 * (t + 1))
                    pe.wait_ge(s_qkl, 4 * t + 4)
                    need(pe, s_sub, n)
                    for a in range(2):
                        kb = (kbA, kbB)[a]
                        o_ = sc[:, 0:HA * TOK] if a == 0 else sc[:, HA * TOK:SC]
                        for i in range(2):
                            at = slice(P * g + TOK * i, P * g + TOK * i + TOK)
                            kh, kl = kb[:, unit, 0, :, at], kb[:, unit, 1, :, at]
                            own = slice(P * (2 * j + i) - TOK * i, P * (2 * j + i) - TOK * i + P)
                            if a == 0:
                                qh, ql = q[:, u, 0, own], q[:, u, 1, own]
                                nc.tensor.matmul(o_, qh, kh, start=i == 0, stop=False)
                                nc.tensor.matmul(o_, qh, kl, start=False, stop=False)
                                last = nc.tensor.matmul(o_, ql, kh, start=False, stop=i == 1)
                            else:
                                qb = q[:, u, 2, own]
                                nc.tensor.matmul(o_, qb, kh, start=i == 0, stop=False)
                                last = nc.tensor.matmul(o_, qb, kl, start=False, stop=i == 1)
                    last.then_inc(s_sc, 1)

                def slot(t, u, j):
                    n = BLK * t + j
                    if not (isinstance(t, int) and t >= NT):
                        scores(t, u, j)
                    if not (isinstance(n, int) and not 3 <= n < LASTS + 3):
                        pe.wait_ge(s_nm, 2 * (n - 2))
                        pe.wait_ge(s_dup, n - 2)
                        for k in range(2):
                            last = nc.tensor.transpose(po[:, P * k:P * k + P], o[:, P * k:P * k + P], idf[:])
                        last.then_inc(s_ot, 1)
                    if not (isinstance(t, int) and t >= NT - 1):
                        project(t + 1, 1 - u, j)
                    if not (isinstance(n, int) and not 2 <= n < LASTS + 2):
                        jj, uu = (j - 2) % 4, u if j >= 2 else 1 - u
                        pe.wait_ge(s_th, n - 1)
                        pe.wait_ge(s_tl, n - 1)
                        need(pe, s_otl, 2 * (n - 2))
                        if jj == 0 or jj == 2:
                            tt = (t if j >= 2 else t - 1)
                            pe.wait_ge(s_vpa, 4 * tt + 2 * (jj // 2) + 2)
                            pe.wait_ge(s_vpd, 4 * tt + 2 * (jj // 2) + 2)
                        for hp in range(HP):
                            o_ = po[:, 2 * VW * hp:2 * VW * hp + 2 * VW].rearrange("p (i w) -> p i w", i=2)
                            terms = [(0, 0), (0, 1), (0, 2), (1, 0), (1, 1)]
                            for k, (e, v) in enumerate(terms):
                                last = nc.tensor.matmul(o_, et[:, j % 2, e, P * hp:P * hp + P], vb[:, uu, :, 3 * jj + v, hp],
                                                        start=k == 0, stop=k == len(terms) - 1)
                        last.then_inc(s_pv, 1)
                    if not (isinstance(n, int) and not 1 <= n < LASTS + 1):
                        pe.wait_ge(s_el, n)
                        need(pe, s_th, n - 1)
                        need(pe, s_tl, n - 1)
                        for e, src in ((0, eh), (1, el)):
                            for hp in range(HP):
                                last = nc.tensor.transpose(pt[:, e, P * hp:P * hp + P], src[:, (j + 1) % 2, P * hp:P * hp + P], idh[:])
                        last.then_inc(s_t, 1)
                    if not normed and j >= 2 and not at_start(t):
                        a, uu = j - 2, 1 - u
                        pe.wait_ge(s_otl, 2 * BLK * t)
                        need(pe, s_ol, 2 * (t - 1) + a)
                        if a == 0:
                            need(pe, s_res[uu], 8 * (t - 1 - uu) + 16)
                        product_fm(nc, pp[:], WO, slice(P * a, P * a + P), (ot[:, uu, 0], ot[:, uu, 1], ot[:, uu, 2]), last=False)
                        if a == 0:
                            nc.tensor.matmul(pp[:], idr[:, 0], res[:, uu, 0], start=False, stop=False)
                            nc.tensor.matmul(pp[:], idr[:, 0], res[:, uu, 1], start=False, stop=True).then_inc(s_pj, 1)
                        else:
                            nc.tensor.matmul(pp[:], idr[:, 1], res[:, uu, 2], start=False, stop=True).then_inc(s_pj, 1)
                            
                    if normed:
                        if not (isinstance(n, int) and not 4 <= n < LASTS + 4):
                            pe.wait_ge(s_oh, n - 3)
                            src = out[:, (j - 4) % 2]
                            c = 2 * (n - 4)
                            nc.tensor.matmul(pp[:, bass.ds(2 * P + c, 2)], src[:, 0:P], sel[:], start=True, stop=True)
                            nc.tensor.matmul(pp[0:FB, bass.ds(3 * P + c, 2)], src[:, P:D], sel[:], start=True,
                                             stop=True).then_inc(s_mm, 1)
                        if not (isinstance(n, int) and not 3 <= n < LASTS + 3):
                            uu, at = (u if j == 3 else 1 - u), slice(P * ((j + 1) % 4), P * ((j + 1) % 4) + P)
                            pe.wait_ge(s_otl, 2 * (n - 2))
                            need(pe, s_y, n - 3)
                            if j == 3:
                                need(pe, s_res[uu], 8 * (t - uu) + 16)
                            product_tm(nc, pp[:, 0:D], tuple(ot[:, uu, k, at] for k in range(3)), WO, slice(0, D), last=False)
                            nc.tensor.matmul(pp[:, 0:D], res[:, uu, 0, at], idr[:, 0], start=False, stop=False)
                            nc.tensor.matmul(pp[:, 0:D], res[:, uu, 1, at], idr[:, 0], start=False, stop=False)
                            nc.tensor.matmul(pp[:, 0:D], res[:, uu, 2, at], idr[:, 1], start=False, stop=True).then_inc(s_pj, 1)

                for j in range(BLK):
                    project(0, 0, j)
                tiles(pe, lambda t, u: [slot(t, u, j) for j in range(BLK)], NT)


W1C = 2 * (2 * FF) + NC
W2C = 2 * NC * D + D


def expert_stage(nc, w_exp, b1, b2, first, second):
    with ExitStack() as ctx:
        m = Memory(nc, ctx, "ex")
        raw = m.sb("raw", [P, NE, W_MOE], F32)
        wh = m.sb("wh", [P, NE, W_MOE], F32R)
        wl = m.sb("wl", [P, NE, W_MOE], F32R)
        s_ld = m.sems("loaded", NE)
        s_hi, s_lo, s_st = m.sem("hi"), m.sem("lo"), m.sem("stored")
        with nc.Block() as block:

            @block.sync
            def _(sp):
                for e in range(NE):
                    sp.dma_start(raw[:, e], w_exp[e]).then_inc(s_ld[e], 16)
                for e in range(NE):
                    sp.dma_start(first[e][:, 4 * FF:], b1[e]).then_inc(s_st, 16)
                    sp.dma_start(second[e][:, 2 * NC * D:], b2[e]).then_inc(s_st, 16)
                for e in range(NE):
                    for k, (w, s) in enumerate(((wh, s_hi), (wl, s_lo))):
                        sp.wait_ge(s, e + 1)
                        sp.dma_start(first[e][:, 2 * FF * k:2 * FF * k + 2 * FF], w[:, e, 0:2 * FF].bitcast(F32)).then_inc(s_st, 16)
                        sp.dma_start(second[e][:, NC * D * k:NC * D * k + NC * D], w[:, e, 2 * FF:].bitcast(F32)).then_inc(s_st, 16)
                sp.wait_ge(s_st, 16 * 6 * NE)

            @block.scalar
            def _(act):
                for e in range(NE):
                    act.wait_ge(s_ld[e], 16)
                    nc.scalar.copy(wh[:, e], raw[:, e]).then_inc(s_hi, 1)

            @block.vector
            def _(dve):
                for e in range(NE):
                    dve.wait_ge(s_hi, e + 1)
                    nc.vector.tensor_tensor(wl[:, e], raw[:, e], wh[:, e].bitcast(F32), ALU.subtract).then_inc(s_lo, 1)


def route_stage(nc, means, wg_d, consts_d, hidden, lists, weights):
    with ExitStack() as ctx:
        m = Memory(nc, ctx, "ro")
        wg = m.sb("wg", [P, 2, NE], F32)
        C = m.sb("consts", [P, 3 * P + SLOTS], F32)
        ones = m.sb("ones", [TOK, P], F32)
        zero = m.sb("zero", [TOK, D], F32)
        s1 = m.sb("s1", [TOK, 32], F32)
        e3 = m.sb("e3", [TOK, 8, NE], F32)
        cnt = m.sb("cnt", [P, 4, NE], F32)
        gt = m.sb("gt", [P, NE, 8], F32)
        pm = m.sb("pm", [TOK, 2, SLOTS], F32)
        row = m.sb("row", [1, 4, SLOTS], F32)
        ps = m.ps("ps", [P, TILE])
        pr = m.ps("pr", [P, TILE])
        s_ld, s_d, s_p, s_e, s_z = m.sem("loaded"), m.sem("dve_step"), m.sem("product"), m.sem("exp"), m.sem("zeros_stored")
        before, image = C[0:IMGS, 0:IMGS], C[0:IMGS, IMGS:IMGS + 1]
        thresholds = C[:, P:P + 8]
        slots = C[:, 3 * P:3 * P + SLOTS]
        prob, onehot = e3[:, 2], e3[:, 5]
        with nc.Block() as block:

            @block.sync
            def _(sp):
                sp.dma_start(wg[:], wg_d).then_inc(s_ld, 16)
                sp.dma_start(C[:], consts_d).then_inc(s_ld, 16)
                sp.wait_ge(s_d, 2)
                sp.dma_start(hidden[IMGS * TOK:], zero[:]).then_inc(s_z, 16)
                sp.wait_ge(s_z, 16)

            @block.scalar
            def _(act):
                act.wait_ge(s_d, 4)
                nc.scalar.activation(e3[:, 1], e3[:, 0], ACT.Exp).then_inc(s_e, 1)

            @block.vector
            def _(dve):
                steps = [0]

                def step(ins):
                    ins.then_inc(s_d, 1)
                    steps[0] += 1
                    dve.wait_ge(s_d, steps[0])

                v = nc.vector
                step(v.memset(ones[:], 1.0))
                step(v.memset(zero[:], 0.0))
                dve.wait_ge(s_ld, 32)
                dve.wait_ge(s_p, 1)
                step(v.tensor_reduce(s1[:, 0:1], ps[0:IMGS, 0:NE], AX.X, ALU.max))
                step(v.tensor_scalar(e3[:, 0], ps[0:IMGS, 0:NE], s1[:, 0:1], None, ALU.subtract))
                dve.wait_ge(s_e, 1)
                step(v.tensor_reduce(s1[:, 1:2], e3[:, 1], AX.X, ALU.add))
                step(v.reciprocal(s1[:, 2:3], s1[:, 1:2]))
                step(v.tensor_scalar(prob, e3[:, 1], s1[:, 2:3], None, ALU.mult))
                step(v.tensor_reduce(s1[:, 3:4], prob, AX.X, ALU.max))
                step(v.tensor_scalar(e3[:, 3], prob, s1[:, 3:4], None, ALU.is_equal))
                step(v.tensor_scalar(e3[:, 4], e3[:, 3], -1.0, 1.0, ALU.mult, ALU.add))
                step(v.tensor_copy(onehot[:, 0:1], e3[:, 3, 0:1]))
                step(v.tensor_tensor(onehot[:, 1:2], e3[:, 3, 1:2], e3[:, 4, 0:1], ALU.mult))
                step(v.tensor_tensor(s1[:, 4:5], e3[:, 4, 0:1], e3[:, 4, 1:2], ALU.mult))
                step(v.tensor_tensor(onehot[:, 2:3], e3[:, 3, 2:3], s1[:, 4:5], ALU.mult))
                dve.wait_ge(s_p, 2)
                step(v.tensor_copy(cnt[:, 0], ps[:, P:P + NE]))
                step(v.tensor_tensor(gt[:], cnt[:, 0].unsqueeze(2).broadcast_to([P, NE, 8]),
                                     thresholds.unsqueeze(1).broadcast_to([P, NE, 8]), ALU.is_gt))
                step(v.tensor_reduce(cnt[:, 1], gt[:], AX.X, ALU.add))
                step(v.memset(cnt[:, 2], 0.0))
                step(v.tensor_copy(cnt[:, 2, 1:2], cnt[:, 1, 0:1]))
                step(v.tensor_tensor(cnt[:, 2, 2:3], cnt[:, 1, 0:1], cnt[:, 1, 1:2], ALU.add))
                step(v.scalar_tensor_tensor(out=e3[:, 6], in0=cnt[0:IMGS, 2], scalar=float(GRP), in1=ps[0:IMGS, 2 * P:2 * P + NE],
                                            op0=ALU.mult, op1=ALU.add))
                step(v.tensor_tensor(e3[:, 7], e3[:, 6], onehot, ALU.mult))
                step(v.tensor_reduce(s1[:, 5:6], e3[:, 7], AX.X, ALU.add))
                step(v.tensor_scalar(pm[:, 0], slots[0:IMGS], s1[:, 5:6], None, ALU.is_equal))
                step(v.tensor_scalar(pm[:, 1], pm[:, 0], s1[:, 3:4], None, ALU.mult))
                dve.wait_ge(s_p, 3)
                step(v.tensor_scalar(row[:, 0], pr[0:1, P:P + SLOTS], -1.0, 1.0, ALU.mult, ALU.add))
                step(v.scalar_tensor_tensor(out=row[:, 1], in0=row[:, 0], scalar=float(IMGS), in1=pr[0:1, 0:SLOTS],
                                            op0=ALU.mult, op1=ALU.add))
                step(v.tensor_tensor(row[:, 2], row[:, 0], slots[0:1], ALU.mult))
                step(v.tensor_tensor(row[:, 3], row[:, 1], row[:, 2], ALU.add))
                step(v.tensor_scalar(lists[:, 0:SLOTS], row[:, 1], float(TOK), None, ALU.mult))
                step(v.tensor_scalar(lists[:, SLOTS:2 * SLOTS], row[:, 3], float(TOK), None, ALU.mult))
                step(v.tensor_scalar(row[:, 0, 0:NB], slots[0:1, 0:NB], cnt[0:1, 2, 1:2], None, ALU.is_ge))
                step(v.scalar_tensor_tensor(out=lists[:, 2 * SLOTS:], in0=slots[0:1, 0:NB], scalar=cnt[0:1, 2, 2:3],
                                            in1=row[:, 0, 0:NB], op0=ALU.is_ge, op1=ALU.add))
                for i in range(2):
                    r = slice(TOK * i, TOK * i + TOK)
                    step(v.tensor_copy(weights[r], pr[r, 2 * P:2 * P + SLOTS].rearrange("p (k c) -> p k c", c=2)[:, :, i]))

            @block.tensor
            def _(pe):
                pe.wait_ge(s_ld, 32)
                nc.tensor.matmul(ps[0:IMGS, 0:NE], means[:, 0:IMGS], wg[:, 0], start=True, stop=False)
                nc.tensor.matmul(ps[0:IMGS, 0:NE], means[0:FB, IMGS:2 * IMGS], wg[0:FB, 1], start=False, stop=True).then_inc(s_p, 1)
                pe.wait_ge(s_d, 14)
                nc.tensor.matmul(ps[:, P:P + NE], ones[:], onehot, start=True, stop=True)
                nc.tensor.matmul(ps[0:IMGS, 2 * P:2 * P + NE], before, onehot, start=True, stop=True).then_inc(s_p, 1)
                pe.wait_ge(s_d, 25)
                nc.tensor.matmul(pr[0:1, 0:SLOTS], image, pm[:, 0], start=True, stop=True)
                nc.tensor.matmul(pr[0:1, P:P + SLOTS], ones[:, 0:1], pm[:, 0], start=True, stop=True)
                nc.tensor.matmul(pr[:, 2 * P:2 * P + SLOTS], ones[:], pm[:, 1], start=True, stop=True).then_inc(s_p, 1)


def moe_stage(nc, stored, hidden, lists, weights, first, second, ident_d, out_d):
    UN = 4
    HB, AB, RING = 3, 3, 2 * NC
    with ExitStack() as ctx:
        m = Memory(nc, ctx, "mo")
        xt = m.sb("xt", [P, UN, BLK, 2 * P], F32)
        xs = m.sb("xs", [P, 2, 3, TILE], F32R)
        w1 = m.sb("w1", [P, 2, W1C], F32R)
        w2 = m.sb("w2", [P, 2, W2C], F32R)
        idf = m.sb("idf", [P, P], F32)
        g = m.sb("g", [P, 4, TILE], F32)
        gh = m.sb("gh", [P, RING, TILE], F32R)
        gl = m.sb("gl", [P, RING, TILE], F32R)
        wc = m.sb("wc", [P, BLK], F32)
        ya = m.sb("ya", [P, D], F32)
        yb = m.sb("yb", [P, 2, D], F32)
        st = m.sb("st", [P, 6], F32)
        mv = m.sb("mv", [P, 2, 2], F32)
        ve = m.sb("ve", [P, 1], F32)
        half = m.sb("half", [P, 1], F32)
        mark = m.sb("mark", [P, 1], F32)
        rstd = m.sb("rstd", [P, 1], F32)
        out = m.sb("out", [P, 2, BLK, D], F32)
        hid = [m.ps(f"hid{i}", [P, TILE]) for i in range(HB)]
        acc = [m.ps(f"acc{i}", [P, TILE]) for i in range(2)]
        tr = m.ps("tr", [P, 2, TILE])
        s_id, s_half = m.sem("ident"), m.sem("half")
        s_x = m.sems("x_loaded", UN)
        s_w1, s_w2 = m.sems("w1_loaded", 2), m.sems("w2_loaded", 2)
        s_dup, s_tr, s_xh, s_xl = m.sem("x_dup"), m.sem("transposed"), m.sem("x_hi"), m.sem("x_lo")
        s_hid, s_g, s_gh, s_gl, s_acc = (m.sem(n) for n in ("hidden", "gelu", "gelu_hi", "gelu_lo", "summed"))
        s_wc, s_ya, s_yb, s_bs, s_ag, s_ve, s_rt, s_o = (m.sem(n) for n in
            ("weight", "biased", "added", "stats", "aggr", "var_eps", "rstd", "out_ready"))
        s_st = stored

        def blocks(eng, body):
            body(0, 0)
            with eng.Fori(0, (NB - 2) // UN) as i:
                for d in range(UN):
                    body(UN * i + 1 + d, (1 + d) % UN)
            for b in range(UN * ((NB - 2) // UN) + 1, NB + 1):
                body(b, b % UN)

        def final(b):
            return isinstance(b, int) and b >= NB - 1

        def ended(b):
            return isinstance(b, int) and b == NB

        def started(b):
            return not (isinstance(b, int) and b == 0)

        W1 = lambda u: (w1[:, u, 0:FF], w1[:, u, 2 * FF:3 * FF], w1[:, u, FF:2 * FF], w1[:, u, 3 * FF:4 * FF])
        with nc.Block() as block:

            @block.sync
            def _(sp):
                sp.dma_start(idf[:], ident_d).then_inc(s_id, 16)

                def entry(eng, at, most):
                    return eng.value_load(lists[0:1, bass.ds(at, 1)], min_val=0, max_val=most)

                def load(b, r):
                    u = r % 2
                    e = entry(sp, 2 * SLOTS + b, NE - 1)
                    need(sp, s_g, NC * (b - 1))
                    sp.dma_start(w1[:, u].bitcast(F32), first[bass.ds(e, 1)].squeeze(0)).then_inc(s_w1[u], 16)
                    for s in range(GRP):
                        rows = entry(sp, GRP * b + s, IMGS * TOK)
                        if s == 0:
                            need(sp, s_o, BLK * (b - 2))
                        sp.dma_start(xt[TOK * (s % 2):TOK * (s % 2) + TOK, r, s // 2, 0:D],
                                     hidden[bass.ds(rows, TOK), :]).then_inc(s_x[r], 16)

                def load2(b, r):
                    u = r % 2
                    e = entry(sp, 2 * SLOTS + b, NE - 1)
                    need(sp, s_ya, BLK * (b - 1))
                    sp.dma_start(w2[:, u].bitcast(F32), second[bass.ds(e, 1)].squeeze(0)).then_inc(s_w2[u], 16)

                def body(b, r):
                    if not final(b):
                        load(b + 1, (r + 1) % UN)
                        load2(b + 1, (r + 1) % UN)

                load(0, 0)
                load2(0, 0)
                blocks(sp, body)

            @block.gpsimd
            def _(pool):
                nc.gpsimd.memset(half[:], -0.5).then_inc(s_half, 1)
                pool.wait_ge(s_half, 1)

                def body(b, r):
                    if not started(b):
                        return
                    p, u = b - 1, (r - 1) % 2
                    for j in range(BLK):
                        pool.wait_ge(s_ve, BLK * p + j + 1)
                        nc.gpsimd.tensor_tensor(rstd[:], ve[:], half[:], ALU.pow).then_inc(s_rt, 1)
                    for j in range(BLK):
                        for i in range(2):
                            rows = pool.value_load(lists[0:1, bass.ds(SLOTS + GRP * p + 2 * j + i, 1)], min_val=0,
                                                   max_val=(IMGS + SLOTS - 1) * TOK)
                            if i == 0:
                                pool.wait_ge(s_o, BLK * p + j + 1)
                            pool.dma_start(out_d[bass.ds(rows, TOK), :], out[TOK * i:TOK * i + TOK, u, j]).then_inc(s_st[u], 16)

                blocks(pool, body)
                for s in s_st:
                    pool.wait_ge(s, 16 * GRP * NB // 2)

            @block.scalar
            def _(act):
                def ready(b, r):
                    u = r % 2
                    need(act, s_x[r], 16 * GRP // UN * (b - r) + 16 * GRP)
                    need(act, s_tr, 2 * (b - 2))
                    nc.scalar.copy(xt[:, r, :, D:], xt[:, r, :, FA:D]).then_inc(s_dup, 1)
                    act.wait_ge(s_tr, 2 * b + 2)
                    need(act, s_hid, NC * (b - 1))
                    nc.scalar.copy(xs[:, u, 0], tr[:, 0]).then_inc(s_xh, 1)
                    nc.scalar.copy(xs[:, u, 2], tr[:, 1]).then_inc(s_xh, 1)

                def body(b, r):
                    u = r % 2
                    if ended(b):
                        return
                    need(act, s_w1[u], 8 * (b - u) + 16)
                    for f in range(NC):
                        n = NC * u + f
                        k = NC * b + f
                        act.wait_ge(s_hid, k + 1)
                        need(act, s_gl, k - 3)
                        nc.scalar.activation(g[:, n % 4], hid[n % HB][:], ACT.Gelu,
                                             bias=w1[:, u, 4 * FF + f:4 * FF + f + 1].bitcast(F32)).then_inc(s_g, 1)
                    if not final(b):
                        ready(b + 1, (r + 1) % UN)

                ready(0, 0)
                blocks(act, body)

            @block.vector
            def _(dve):
                def ready(b, r):
                    u = r % 2
                    dve.wait_ge(s_xh, 2 * b + 1)
                    nc.vector.tensor_tensor(xs[:, u, 1], tr[:, 0], xs[:, u, 0].bitcast(F32), ALU.subtract).then_inc(s_xl, 1)
                    dve.wait_ge(s_xh, 2 * b + 2)
                    low = xs[FB:P, u, 2]
                    nc.vector.tensor_tensor(low, tr[FB:P, 1], low.bitcast(F32), ALU.subtract).then_inc(s_xl, 1)

                def finish(b, r):
                    u = r % 2
                    nc.vector.tensor_copy(wc[:], weights[:, bass.ds(BLK * b, BLK)]).then_inc(s_wc, 1)
                    dve.wait_ge(s_wc, b + 1)
                    for j in range(BLK):
                        k = BLK * b + j
                        c = k + 1
                        dve.wait_ge(s_acc, c)
                        nc.vector.tensor_tensor(ya[:], acc[j % 2][:, 0:D], w2[:, u, 2 * NC * D:].bitcast(F32), ALU.add).then_inc(s_ya, 1)
                        dve.wait_ge(s_ya, c)
                        nc.vector.scalar_tensor_tensor(out=yb[:, j % 2], in0=ya[:], scalar=wc[:, j:j + 1], in1=xt[:, r, j, 0:D],
                                                       op0=ALU.mult, op1=ALU.add).then_inc(s_yb, 1)
                        dve.wait_ge(s_yb, c)
                        nc.vector.bn_stats(st[:], yb[:, j % 2]).then_inc(s_bs, 1)
                        dve.wait_ge(s_bs, c)
                        nc.vector.memset(mark[:], 0.0)
                        nc.vector.bn_aggr(mv[:, j % 2], st[:]).then_inc(s_ag, 1)
                        dve.wait_ge(s_ag, c)
                        nc.vector.tensor_scalar(ve[:], mv[:, j % 2, 1:2], EPS, None, ALU.add).then_inc(s_ve, 1)
                        dve.wait_ge(s_rt, c)
                        if j == 0:
                            need(dve, s_st[u], 8 * GRP * (b - u))
                        nc.vector.tensor_scalar(out[:, u, j], yb[:, j % 2], mv[:, j % 2, 0:1], rstd[:], ALU.subtract,
                                                ALU.mult).then_inc(s_o, 1)

                def body(b, r):
                    u = r % 2
                    if not ended(b):
                        for f in range(NC):
                            n = NC * u + f
                            k = NC * b + f
                            dve.wait_ge(s_g, k + 1)
                            if f == 0:
                                need(dve, s_acc, BLK * (b - 1))
                            nc.vector.tensor_copy(gh[:, n], g[:, n % 4]).then_inc(s_gh, 1)
                            dve.wait_ge(s_gh, k + 1)
                            nc.vector.tensor_tensor(gl[:, n], g[:, n % 4], gh[:, n].bitcast(F32), ALU.subtract).then_inc(s_gl, 1)
                    if not final(b):
                        ready(b + 1, (r + 1) % UN)
                    if started(b):
                        finish(b - 1, (r - 1) % UN)

                ready(0, 0)
                blocks(dve, body)

            @block.tensor
            def _(pe):
                pe.wait_ge(s_id, 16)

                def transpose(b, r):
                    pe.wait_ge(s_dup, b + 1)
                    need(pe, s_xl, 2 * b)
                    for k in range(2):
                        for j in range(BLK):
                            last = nc.tensor.transpose(tr[:, k, P * j:P * j + P], xt[:, r, j, P * k:P * k + P], idf[:])
                        last.then_inc(s_tr, 1)

                def second_product(b, r):
                    u = r % 2
                    need(pe, s_w2[u], 8 * (b - u) + 16)
                    pe.wait_ge(s_gl, NC * b + NC)
                    for j in range(BLK):
                        need(pe, s_ya, BLK * b + max(j - 1, 0))
                        o = acc[j % 2][:, 0:D]
                        at = slice(P * j, P * j + P)
                        for f in range(NC):
                            n = NC * u + f
                            h, l = gh[:, n, at], gl[:, n, at]
                            a, c = w2[:, u, D * f:D * f + D], w2[:, u, D * (NC + f):D * (NC + f) + D]
                            nc.tensor.matmul(o, h, a, start=f == 0, stop=False)
                            nc.tensor.matmul(o, h, c, start=False, stop=False)
                            last = nc.tensor.matmul(o, l, a, start=False, stop=f == NC - 1)
                        last.then_inc(s_acc, 1)

                def body(b, r):
                    u = r % 2
                    if not ended(b):
                        need(pe, s_w1[u], 8 * (b - u) + 16)
                        pe.wait_ge(s_xl, 2 * b + 2)
                        for f in range(NC):
                            n = NC * u + f
                            need(pe, s_g, NC * b + f + 1 - HB)
                            product_fm(nc, hid[n % HB][:], W1(u), slice(P * f, P * f + P),
                                       (xs[:, u, 0], xs[:, u, 1], xs[:, u, 2])).then_inc(s_hid, 1)
                    if not final(b):
                        transpose(b + 1, (r + 1) % UN)
                    if started(b):
                        second_product(b - 1, (r - 1) % UN)

                transpose(0, 0)
                blocks(pe, body)


def positions():
    pos = np.arange(TOK, dtype=np.float32)[:, None]
    i = np.arange(D // 2, dtype=np.float32)[None, :]
    ang = (pos / np.power(np.float32(10000.0), np.float32(2.0) * i / np.float32(D))).astype(np.float32)
    pe = np.zeros((TOK, D), np.float32)
    pe[:, 0::2] = np.sin(ang)
    pe[:, 1::2] = np.cos(ang)
    return pe


def stacked(w):
    return np.stack([w[:FA], np.concatenate([w[FA:], w[FA:]])], 1)


def doubled(w):
    return np.concatenate([w, w[..., FA:]], -1)


def lay_out(**a):
    a = {k: np.asarray(v) for k, v in a.items()}
    out = {}
    x = a["x"].reshape(IMGS, 3, 8, 16, 8, 16).transpose(1, 3, 5, 0, 2, 4).reshape(PC, P, NT, TILE)
    out["patches"] = x.transpose(2, 1, 0, 3)
    out["w_patch"] = a["L0_tok_patch_w"].reshape(D, PC, P).transpose(2, 1, 0).reshape(P, PC * D)
    pe = np.concatenate([positions()] * 2)
    row = lambda v: np.broadcast_to(v, (P, D))
    out["rows"] = np.stack([row(a["L0_tok_patch_b"]), row(a["L0_tok_ln_g"]), pe, row(a["L0_tok_ln_b"])], 1)
    eye = np.eye(P, dtype=np.float32)
    out["ident"] = np.concatenate([eye, np.tile(np.eye(FB, dtype=np.float32), (2, 2))], 1)
    w1 = stacked(a["L0_tok_ff1_w"]).reshape(P, 2 * FF)
    w2 = doubled(a["L0_tok_ff2_w"]).reshape(NC, P, 2 * P).transpose(1, 0, 2).reshape(P, NC * 2 * P)
    out["w_ff"] = np.concatenate([w1, w2], 1)
    fm = lambda b: doubled(b).reshape(2, P).T
    out["b_ff"] = np.concatenate([a["L0_tok_ff1_b"].reshape(NC, P).T, fm(a["L0_tok_ff2_b"])], 1)
    def att(wq, bq, wp, bp, normed):
        wq = stacked(np.concatenate([doubled(wq[:, D:2 * D]), doubled(wq[:, 0:D]), wq[:, 2 * D:]], 1))
        wp = stacked(wp if normed else doubled(wp))
        bs = [fm(bq[D:2 * D]), fm(bq[0:D]), fm(bq[2 * D:]), fm(bp)]
        return np.concatenate([wq, wp], 2).reshape(P, -1), np.concatenate(bs, 1)

    out["w_att1"], out["c_att1"] = att(*(a[f"L0_tok_{k}"] for k in ("qkv_w", "qkv_b", "proj_w", "proj_b")), False)
    out["w_att2"], out["c_att2"] = att(*(a[f"L0_attn_{k}"] for k in ("w_qkv", "b_qkv", "w_proj", "b_proj")), True)
    out["b_out2"] = row(a["L0_attn_b_proj"])
    tm = np.zeros((P, 2, D), np.float32)
    tm[:, 0, 0:P] = eye
    tm[:, 1, P:] = np.tile(np.eye(FB, dtype=np.float32), (2, 1))
    out["ident_tm"] = tm.reshape(P, 2 * D)
    sel = np.zeros((P, 2), np.float32)
    sel[:TOK, 0] = sel[TOK:, 1] = 1.0 / TOK
    out["sel"] = sel
    out["wg"] = stacked(a["L0_ffn_Wg"].T)
    c = np.zeros((P, 3 * P + SLOTS), np.float32)
    c[:IMGS, :IMGS] = np.triu(np.ones((IMGS, IMGS)), 1)
    c[:IMGS, IMGS] = np.arange(IMGS)
    c[:, P:P + 8] = GRP * np.arange(8)
    c[:, 3 * P:] = np.arange(SLOTS)
    out["route_consts"] = c
    w1 = np.stack([stacked(w).reshape(P, 2 * FF) for w in a["L0_ffn_W1"]])
    w2 = a["L0_ffn_W2"].reshape(NE, NC, P, D).transpose(0, 2, 1, 3).reshape(NE, P, NC * D)
    out["w_exp"] = np.concatenate([w1, w2], 2)
    out["b1_exp"] = a["L0_ffn_b1"].reshape(NE, NC, P).transpose(0, 2, 1)
    out["b2_exp"] = np.broadcast_to(a["L0_ffn_b2"][:, None], (NE, P, D))
    return {k: np.ascontiguousarray(v) for k, v in out.items()}


def build(nc, arrays, debug=False, upto=9):
    ins = {k: nc.dram_tensor(k, v.shape, mybir.dt.from_np(v.dtype), kind="ExternalInput").ap() for k, v in arrays.items()}
    kind = "ExternalOutput" if debug else "Internal"
    T = IMGS * TOK
    x0, y, x2, x3 = (nc.dram_tensor(n, (P, 3, T), F32, kind=kind).ap() for n in ("x0", "y", "x2", "x3"))
    h = nc.dram_tensor("h", (T + TOK, D), F32, kind=kind).ap()
    idf = ins["ident"][:, 0:P]
    first = nc.dram_tensor("expert_first", (NE, P, W1C), F32, kind="Internal").ap()
    second = nc.dram_tensor("expert_second", (NE, P, W2C), F32, kind="Internal").ap()
    out = nc.dram_tensor("out", ((IMGS + SLOTS) * TOK, D), F32, kind="ExternalOutput").ap()
    stored = [[nc.alloc_semaphore(f"stored{k}{i}") for i in range(2)] for k in range(6)]
    with (
        nc.sbuf_tensor("means", [P, 2 * IMGS], F32) as means,
        nc.sbuf_tensor("lists", [1, 2 * SLOTS + NB], I32) as lists,
        nc.sbuf_tensor("weights", [P, SLOTS // 2], F32) as weights,
    ):
        patch_stage(nc, stored[0], ins["patches"], ins["w_patch"], ins["rows"], idf, x0)
        ff_stage(nc, stored[1], "ff1", x0, y, ins["w_ff"], ins["b_ff"], ins["ident"], False)
        att_stage(nc, stored[2], "at1", y, x0, ins["w_att1"], ins["c_att1"], (ins["ident"], idf), state_out=x2)
        ff_stage(nc, stored[3], "ff2", x2, x3, ins["w_ff"], ins["b_ff"], ins["ident"], True)
        att_stage(nc, stored[4], "at2", x3, x3, ins["w_att2"], ins["c_att2"], (ins["ident_tm"], idf), rows_d=ins["b_out2"],
                  sel_d=ins["sel"], hidden=h, means=means)
        expert_stage(nc, ins["w_exp"], ins["b1_exp"], ins["b2_exp"], first, second)
        route_stage(nc, means, ins["wg"], ins["route_consts"], h, lists, weights)
        moe_stage(nc, stored[5], h, lists, weights, first, second, idf, out)
    return ["x0", "y", "x2", "x3", "h", "out"] if debug else ["out"]


def kernel(**inputs):
    from concourse import bacc
    from concourse.bass_utils import run_bass_kernel_spmd

    arrays = lay_out(**inputs)
    nc = bacc.Bacc("TRN2", target_bir_lowering=False, num_devices=1)
    build(nc, arrays)
    got = run_bass_kernel_spmd(nc, [arrays], core_ids=[0]).results[0]["out"]
    return got[:IMGS * TOK].reshape(IMGS, TOK, D)
```

```python
from contextlib import ExitStack

import numpy as np

import concourse.bass as bass
from concourse import mybir

F32 = mybir.dt.float32
F32R = mybir.dt.float32r
BF16 = mybir.dt.bfloat16
F16 = mybir.dt.float16
I32 = mybir.dt.int32
ACT = mybir.ActivationFunctionType
ALU = mybir.AluOpType
AX = mybir.AxisListType

P = 128
IMGS, TOK = 64, 64
D, FF, NH, DH = 192, 768, 12, 16
FA, FB = 128, 64
TILE = 512
NT = IMGS * TOK // TILE
BLK = TILE // P
NC = FF // P
PC = 3 * 16 * 16 // P
EPS = 1e-5
NE = 3
GRP = TILE // TOK
NB = IMGS // GRP + NE - 1
SLOTS = NB * GRP
W_FF = NC * 4 * P
W_MOE = 2 * FF + NC * D
W1C = 2 * (2 * FF) + NC
W2C = 2 * NC * D + D
SC = NH * TOK
HP = NH // 2
HA = FA // DH
HBN = NH - HA
VW = 2 * DH + 2


def need(eng, sem, value):
    if isinstance(value, int) and value <= 0:
        return
    eng.wait_ge(sem, value)


def tiles(eng, body, last):
    body(0, 0)
    with eng.Fori(0, 3) as i:
        body(2 * i + 1, 1)
        body(2 * i + 2, 0)
    for t in range(7, last + 1):
        body(t, t % 2)


def product_fm(nc, out, w, cols, x, last=True):
    wah, wal, wbh, wbl = w
    xah, xal, xb = x
    nc.tensor.matmul(out, wah[:, cols], xah, start=True, stop=False)
    nc.tensor.matmul(out, wah[:, cols], xal, start=False, stop=False)
    nc.tensor.matmul(out, wal[:, cols], xah, start=False, stop=False)
    nc.tensor.matmul(out, wbh[:, cols], xb, start=False, stop=False)
    return nc.tensor.matmul(out, wbl[:, cols], xb, start=False, stop=last)


def product_tm(nc, out, x, w, cols, last=True):
    wah, wal, wbh, wbl = w
    xah, xal, xb = x
    nc.tensor.matmul(out, xah, wah[:, cols], start=True, stop=False)
    nc.tensor.matmul(out, xah, wal[:, cols], start=False, stop=False)
    nc.tensor.matmul(out, xal, wah[:, cols], start=False, stop=False)
    nc.tensor.matmul(out, xb, wbh[:, cols], start=False, stop=False)
    return nc.tensor.matmul(out, xb, wbl[:, cols], start=False, stop=last)


class Memory:
    def __init__(self, nc, ctx, stage):
        self.nc, self.ctx, self.stage = nc, ctx, stage
        self.semaphores = []
        ctx.callback(self.clear)

    def clear(self):
        self.nc.all_engine_barrier()
        self.nc.clear_and_free_semaphores(self.semaphores)
        self.nc.all_engine_barrier()

    def sb(self, name, shape, dt):
        return self.ctx.enter_context(self.nc.sbuf_tensor(f"{self.stage}_{name}", shape, dt))

    def ps(self, name, shape, dt=F32):
        return self.ctx.enter_context(self.nc.psum_tensor(f"{self.stage}_{name}", shape, dt))

    def sem(self, name):
        self.semaphores.append(self.nc.alloc_semaphore(f"{self.stage}_{name}"))
        return self.semaphores[-1]

    def sems(self, name, n):
        return [self.sem(f"{name}{i}") for i in range(n)]


def patch_stage(nc, stored, patches, w_patch, rows, ident_d, state_out):
    with ExitStack() as ctx:
        m = Memory(nc, ctx, "pe")
        raw = m.sb("raw", [P, 2, PC, TILE], F32)
        xh = m.sb("xh", [P, 2, PC, TILE], F32R)
        xl = m.sb("xl", [P, 2, PC, TILE], F32R)
        wraw = m.sb("wraw", [P, PC * D], F32)
        wh = m.sb("wh", [P, PC * D], F32R)
        wl = m.sb("wl", [P, PC * D], F32R)
        cst = m.sb("cst", [P, 3, D], F32)
        lnb = m.sb("lnb", [P, D], F32)
        ident = m.sb("ident", [P, P], F32)
        half = m.sb("half", [P, BLK], F32)
        y = m.sb("y", [P, BLK, D], F32)
        st = m.sb("st", [P, BLK, 6], F32)
        mv = m.sb("mv", [P, BLK, 2], F32)
        ve = m.sb("ve", [P, BLK], F32)
        mark = m.sb("mark", [P, 1], F32)
        rstd = m.sb("rstd", [P, BLK], F32)
        z = m.sb("z", [P, BLK, D], F32)
        x0 = m.sb("x0", [P, BLK, 2 * P], F32)
        out = m.sb("out", [P, 2, 3, TILE], F32R)
        emb = [m.ps(f"emb{i}", [P, BLK, 2 * P]) for i in range(2)]
        tr = m.ps("tr", [P, 2, TILE])
        s_w, s_const = m.sem("w_loaded"), m.sem("const_loaded")
        s_wh, s_wl, s_pos, s_half = m.sem("w_hi"), m.sem("w_lo"), m.sem("pos_ready"), m.sem("half_ready")
        s_ld = m.sems("patches_loaded", 2)
        s_hi, s_lo, s_emb, s_y = m.sem("patch_hi"), m.sem("patch_lo"), m.sem("embedded"), m.sem("emb_read")
        s_st, s_ag, s_ve, s_rs, s_z, s_x0, s_dup = (m.sem(n) for n in
            ("stats", "aggr", "var_eps", "rstd", "centered", "x0_ready", "x0_dup"))
        s_tr, s_oh, s_ol = m.sem("transposed"), m.sem("out_hi"), m.sem("out_lo")
        s_st_out = stored
        with nc.Block() as block:

            @block.sync
            def _(sp):
                sp.dma_start(wraw[:], w_patch).then_inc(s_w, 16)
                sp.dma_start(raw[:, 0], patches[0]).then_inc(s_ld[0], 16)
                sp.dma_start(cst[:], rows[:, 0:3]).then_inc(s_const, 16)
                sp.dma_start(lnb[:], rows[:, 3]).then_inc(s_const, 16)
                sp.dma_start(ident[:], ident_d).then_inc(s_const, 16)

                def load(t, u):
                    need(sp, s_hi, 3 * (t - 1))
                    need(sp, s_lo, 3 * (t - 1))
                    src = patches[t] if isinstance(t, int) else patches[bass.ds(t, 1)].squeeze(0)
                    sp.dma_start(raw[:, u], src).then_inc(s_ld[u], 16)

                sp.dma_start(raw[:, 1], patches[1]).then_inc(s_ld[1], 16)
                with sp.Fori(0, 3) as i:
                    load(2 * i + 2, 0)
                    load(2 * i + 3, 1)

            @block.gpsimd
            def _(pool):
                nc.gpsimd.memset(half[:], -0.5).then_inc(s_half, 1)
                pool.wait_ge(s_half, 1)

                def store(t, u):
                    need(pool, s_ve, t + 1)
                    need(pool, s_x0, BLK * t)
                    nc.gpsimd.tensor_tensor(rstd[:], ve[:], half[:], ALU.pow).then_inc(s_rs, 1)
                    pool.wait_ge(s_oh, 2 * t + 2)
                    pool.wait_ge(s_ol, 2 * t + 2)
                    dst = state_out[:, :, bass.ds(t * TILE, TILE)]
                    pool.dma_start(dst, out[:, u].bitcast(F32)).then_inc(s_st_out[u], 16)

                tiles(pool, store, NT - 1)
                for s in s_st_out:
                    pool.wait_ge(s, 16 * NT // 2)

            @block.scalar
            def _(act):
                act.wait_ge(s_w, 16)
                nc.scalar.copy(wh[:], wraw[:]).then_inc(s_wh, 1)

                def split(t, u):
                    need(act, s_ld[u], 16 * ((t - u) // 2 + 1) if isinstance(t, int) else (t - u) * 8 + 16)
                    need(act, s_emb, BLK * (t - 1))
                    for c in range(0, PC, 2):
                        nc.scalar.copy(xh[:, u, c:c + 2], raw[:, u, c:c + 2]).then_inc(s_hi, 1)

                def finish(t, u):
                    act.wait_ge(s_x0, BLK * t + BLK)
                    need(act, s_tr, 2 * t)
                    nc.scalar.copy(x0[:, :, P + FB:], x0[:, :, P:P + FB]).then_inc(s_dup, 1)
                    act.wait_ge(s_tr, 2 * t + 2)
                    need(act, s_st_out[u], 8 * (t - u))
                    nc.scalar.copy(out[:, u, 0], tr[:, 0]).then_inc(s_oh, 1)
                    nc.scalar.copy(out[:, u, 2], tr[:, 1]).then_inc(s_oh, 1)

                def body(t, u):
                    if not (isinstance(t, int) and t == NT - 1):
                        split(t + 1, 1 - u)
                    finish(t, u)

                split(0, 0)
                tiles(act, body, NT - 1)

            @block.vector
            def _(dve):
                dve.wait_ge(s_wh, 1)
                nc.vector.tensor_tensor(wl[:], wraw[:], wh[:].bitcast(F32), ALU.subtract).then_inc(s_wl, 1)
                dve.wait_ge(s_const, 48)
                nc.vector.tensor_tensor(cst[:, 2], cst[:, 2], lnb[:], ALU.add).then_inc(s_pos, 1)
                dve.wait_ge(s_pos, 1)

                def split(t, u):
                    need(dve, s_emb, BLK * (t - 1))
                    for k, c in enumerate(range(0, PC, 2)):
                        dve.wait_ge(s_hi, 3 * t + k + 1)
                        nc.vector.tensor_tensor(xl[:, u, c:c + 2], raw[:, u, c:c + 2],
                                                xh[:, u, c:c + 2].bitcast(F32), ALU.subtract).then_inc(s_lo, 1)

                def finish(t, u):
                    dve.wait_ge(s_emb, BLK * t + BLK)
                    nc.vector.tensor_tensor(y[:], emb[u][:, :, 0:D],
                                            cst[:, 0].unsqueeze(1).broadcast_to([P, BLK, D]), ALU.add).then_inc(s_y, 1)
                    dve.wait_ge(s_y, t + 1)
                    for b in range(BLK):
                        nc.vector.bn_stats(st[:, b], y[:, b]).then_inc(s_st, 1)
                    dve.wait_ge(s_st, BLK * t + BLK)
                    nc.vector.memset(mark[:], 0.0)
                    for b in range(BLK):
                        nc.vector.bn_aggr(mv[:, b], st[:, b]).then_inc(s_ag, 1)
                    dve.wait_ge(s_ag, BLK * t + BLK)
                    need(dve, s_rs, t)
                    nc.vector.tensor_scalar(ve[:], mv[:, :, 1], EPS, None, ALU.add).then_inc(s_ve, 1)
                    for b in range(BLK):
                        nc.vector.scalar_tensor_tensor(out=z[:, b], in0=y[:, b], scalar=mv[:, b, 0:1], in1=cst[:, 1],
                                                       op0=ALU.subtract, op1=ALU.mult).then_inc(s_z, 1)
                    dve.wait_ge(s_rs, t + 1)
                    need(dve, s_tr, 2 * t)
                    for b in range(BLK):
                        dve.wait_ge(s_z, BLK * t + b + 1)
                        nc.vector.scalar_tensor_tensor(out=x0[:, b, 0:D], in0=z[:, b], scalar=rstd[:, b:b + 1],
                                                       in1=cst[:, 2], op0=ALU.mult, op1=ALU.add).then_inc(s_x0, 1)
                    dve.wait_ge(s_oh, 2 * t + 1)
                    nc.vector.tensor_tensor(out[:, u, 1], tr[:, 0], out[:, u, 0].bitcast(F32),
                                            ALU.subtract).then_inc(s_ol, 1)
                    dve.wait_ge(s_oh, 2 * t + 2)
                    low = out[FB:P, u, 2]
                    nc.vector.tensor_tensor(low, tr[FB:P, 1], low.bitcast(F32), ALU.subtract).then_inc(s_ol, 1)

                def body(t, u):
                    if not (isinstance(t, int) and t == NT - 1):
                        split(t + 1, 1 - u)
                    finish(t, u)

                split(0, 0)
                tiles(dve, body, NT - 1)

            @block.tensor
            def _(pe):
                pe.wait_ge(s_wl, 1)
                pe.wait_ge(s_const, 48)

                def embed(t, u):
                    need(pe, s_y, t - 1)
                    pe.wait_ge(s_lo, 3 * t + 3)
                    for b in range(BLK):
                        o = emb[u][:, b, 0:D]
                        for c in range(PC):
                            h, l = xh[:, u, c, P * b:P * b + P], xl[:, u, c, P * b:P * b + P]
                            w0, w1 = wh[:, D * c:D * c + D], wl[:, D * c:D * c + D]
                            nc.tensor.matmul(o, h, w0, start=c == 0, stop=False)
                            nc.tensor.matmul(o, h, w1, start=False, stop=False)
                            last = nc.tensor.matmul(o, l, w0, start=False, stop=c == PC - 1)
                        last.then_inc(s_emb, 1)

                def transpose(t, u):
                    pe.wait_ge(s_dup, t + 1)
                    need(pe, s_oh, 2 * t)
                    need(pe, s_ol, 2 * t)
                    for k in range(2):
                        for b in range(BLK):
                            last = nc.tensor.transpose(tr[:, k, P * b:P * b + P], x0[:, b, P * k:P * k + P], ident[:])
                        last.then_inc(s_tr, 1)

                def body(t, u):
                    if not (isinstance(t, int) and t == NT - 1):
                        embed(t + 1, 1 - u)
                    transpose(t, u)

                embed(0, 0)
                tiles(pe, body, NT - 1)


def ff_stage(nc, stored, name, state_in, state_out, w_ff, b_ff, ident_d, residual, operands=None, experts=None):
    LAG, HB = 3, 4
    RING = 6
    with ExitStack() as ctx:
        m = Memory(nc, ctx, name)
        x = m.sb("x", [P, 2, 3, TILE], F32R)
        wraw = m.sb("wraw", [P, W_FF], F32)
        wh = m.sb("wh", [P, W_FF], F32R)
        wl = m.sb("wl", [P, W_FF], F32R)
        bias = m.sb("bias", [P, NC + 2], F32)
        idraw = m.sb("idraw", [P, 2 * P], F32)
        ident = m.sb("ident", [P, 2, P], F32R)
        g = m.sb("g", [P, HB, TILE], F32)
        gh = m.sb("gh", [P, RING, TILE], F32R)
        gl = m.sb("gl", [P, RING, TILE], F32R)
        out = m.sb("out", [P, 2, 3, TILE], F32R)
        hid = [m.ps(f"hid{i}", [P, TILE]) for i in range(HB)]
        acc = [[m.ps(f"acc{u}{k}", [P, TILE]) for k in range(2)] for u in range(2)]
        s_w = m.sems("w_loaded", NC)
        s_wh, s_wl, s_idl, s_id, s_bias = (m.sem(n) for n in ("w_hi", "w_lo", "ident_loaded", "ident_ready", "bias_loaded"))
        s_ld = m.sems("x_loaded", 2)
        s_hid, s_g, s_gh, s_gl, s_ff2 = (m.sem(n) for n in ("hidden", "gelu", "gelu_hi", "gelu_lo", "second_used"))
        s_oh, s_ol = m.sem("out_hi"), m.sem("out_lo")
        s_st = stored
        if operands:
            q, kbA, kbB, vb = operands
            s_zero = m.sem("zeroed")
        if experts:
            w_exp, b1, b2, blob1, blob2 = experts
            eraw = m.sb("eraw", [P, 2 * FF], F32)
            eh = m.sb("eh", [P, 2 * FF], F32R)
            el = m.sb("el", [P, 2 * FF], F32R)
            s_er, s_eh, s_el, s_es, s_eb = (m.sem(n) for n in
                ("expert_loaded", "expert_hi", "expert_lo", "expert_stored", "expert_biases"))
        CH = W_FF // NC

        def chunk(w, f):
            return w[:, CH * f:CH * f + CH]

        def w1(f):
            a, b = slice(CH * f, CH * f + P), slice(CH * f + P, CH * f + 2 * P)
            return wh[:, a], wl[:, a], wh[:, b], wl[:, b]

        def w2(w, f, k):
            at = CH * f + 2 * P + P * k
            return w[:, at:at + P]

        def piece(t, u):
            return (2 * FF, (t - 1) * (W_MOE // 2), (t - 1) * (W1C // 2)) if u else (
                NC * D, (t - 2) * (W_MOE // 2) + 2 * FF, (t - 2) * (W2C // 2))

        def with_piece(t):
            return experts and not (isinstance(t, int) and not 1 <= t <= 2 * NE)

        with nc.Block() as block:

            @block.sync
            def _(sp):
                sp.dma_start(chunk(wraw, 0), chunk(w_ff, 0)).then_inc(s_w[0], 16)
                sp.dma_start(x[:, 0].bitcast(F32), state_in[:, :, 0:TILE]).then_inc(s_ld[0], 16)
                sp.dma_start(bias[:], b_ff).then_inc(s_bias, 16)
                for f in range(1, NC):
                    sp.dma_start(chunk(wraw, f), chunk(w_ff, f)).then_inc(s_w[f], 16)
                sp.dma_start(idraw[:], ident_d).then_inc(s_idl, 16)
                sp.dma_start(x[:, 1].bitcast(F32), state_in[:, :, TILE:2 * TILE]).then_inc(s_ld[1], 16)
                if experts:
                    for e in range(NE):
                        sp.dma_start(blob1[:, W1C * e + 4 * FF:W1C * e + W1C], b1[e]).then_inc(s_eb, 16)
                        sp.dma_start(blob2[:, W2C * e + 2 * NC * D:W2C * e + W2C], b2[e]).then_inc(s_eb, 16)

                def load(t, u):
                    sp.wait_ge(s_ff2, NC * (t - 1))
                    sp.dma_start(x[:, u].bitcast(F32), state_in[:, :, bass.ds(t * TILE, TILE)]).then_inc(s_ld[u], 16)

                def load_piece(t, u):
                    n, at, to = piece(t, u)
                    sp.wait_ge(s_el, t)
                    sp.dma_start(eraw[:, 0:n], w_exp[:, bass.ds(at, n)]).then_inc(s_er, 16)

                def store_piece(t, u):
                    n, at, to = piece(t, u)
                    blob = blob1 if u else blob2
                    sp.wait_ge(s_eh, t)
                    sp.dma_start(blob[:, bass.ds(to, n)], eh[:, 0:n].bitcast(F32)).then_inc(s_es, 16)
                    sp.wait_ge(s_el, t + 1)
                    sp.dma_start(blob[:, bass.ds(to + n, n)], el[:, 0:n].bitcast(F32)).then_inc(s_es, 16)

                with sp.Fori(0, 3) as i:
                    if experts:
                        load_piece(2 * i + 1, 1)
                    load(2 * i + 2, 0)
                    if experts:
                        store_piece(2 * i + 1, 1)
                        load_piece(2 * i + 2, 0)
                    load(2 * i + 3, 1)
                    if experts:
                        store_piece(2 * i + 2, 0)
                if experts:
                    sp.wait_ge(s_es, 16 * 2 * 2 * NE)
                    sp.wait_ge(s_eb, 16 * 2 * NE)

            @block.gpsimd
            def _(pool):
                if operands:
                    nc.gpsimd.memset(q[:].rearrange("p a b c -> p (a b c)").bitcast(F32), 0.0)
                    nc.gpsimd.memset(kbA[:].rearrange("p a b c d -> p (a b c d)").bitcast(F32), 0.0)
                    nc.gpsimd.memset(kbB[:].rearrange("p a b c d -> p (a b c d)").bitcast(F32), 0.0)
                    nc.gpsimd.memset(vb[:].rearrange("p a b c d e -> p (a b c d e)").bitcast(F32), 0.0).then_inc(s_zero, 1)
                    pool.wait_ge(s_zero, 1)
                    for par in range(2):
                        ones = vb[TOK * par:TOK * par + TOK].rearrange("p a i k h w -> p (a i) k h w")
                        nc.gpsimd.memset(ones[:, :, 0::3, :, 2 * DH + par:2 * DH + par + 1], 1.0).then_inc(s_zero, 1)
                if experts:
                    nc.gpsimd.memset(el[0:1, 0:1].bitcast(F32), 0.0).then_inc(s_el, 1)
                    pool.wait_ge(s_el, 1)

                def store(t, u):
                    if with_piece(t):
                        n = piece(t, u)[0]
                        pool.wait_ge(s_eh, t)
                        need(pool, s_es, 32 * (t - 1))
                        nc.gpsimd.tensor_tensor(el[:, 0:n], eraw[:, 0:n], eh[:, 0:n].bitcast(F32), ALU.subtract).then_inc(s_el, 1)
                    pool.wait_ge(s_oh, 2 * t + 2)
                    pool.wait_ge(s_ol, 2 * t + 2)
                    pool.dma_start(state_out[:, :, bass.ds(t * TILE, TILE)], out[:, u].bitcast(F32)).then_inc(s_st[u], 16)

                tiles(pool, store, NT - 1)
                for s in s_st:
                    pool.wait_ge(s, 16 * NT // 2)

            @block.scalar
            def _(act):
                for f in range(NC):
                    act.wait_ge(s_w[f], 16)
                    nc.scalar.copy(chunk(wh, f), chunk(wraw, f)).then_inc(s_wh, 1)
                act.wait_ge(s_bias, 16)

                def finish(t, u):
                    act.wait_ge(s_ff2, NC * t + NC)
                    need(act, s_st[u], 8 * (t - u))
                    nc.scalar.activation(out[:, u, 0], acc[u][0][:], ACT.Identity, bias=bias[:, NC:NC + 1]).then_inc(s_oh, 1)
                    nc.scalar.activation(out[:, u, 2], acc[u][1][:], ACT.Identity, bias=bias[:, NC + 1:]).then_inc(s_oh, 1)

                def body(t, u):
                    if isinstance(t, int) and t == NT:
                        return finish(t - 1, 1 - u)
                    for f in range(NC):
                        n = (NC * u + f)
                        act.wait_ge(s_hid, NC * t + f + 1)
                        need(act, s_gl, NC * t + f + 1 - HB)
                        nc.scalar.activation(g[:, n % HB], hid[n % HB][:], ACT.Gelu_apprx_tanh,
                                             bias=bias[:, f:f + 1]).then_inc(s_g, 1)
                        if f == LAG + 1 and not (isinstance(t, int) and t == 0):
                            finish(t - 1, 1 - u)
                        if f == NC - 1 and with_piece(t):
                            n = piece(t, u)[0]
                            act.wait_ge(s_er, 16 * t)
                            need(act, s_es, 32 * (t - 1))
                            nc.scalar.copy(eh[:, 0:n], eraw[:, 0:n]).then_inc(s_eh, 1)

                tiles(act, body, NT)

            @block.vector
            def _(dve):
                for f in range(NC):
                    dve.wait_ge(s_wh, f + 1)
                    nc.vector.tensor_tensor(chunk(wl, f), chunk(wraw, f), chunk(wh, f).bitcast(F32), ALU.subtract).then_inc(s_wl, 1)
                dve.wait_ge(s_idl, 16)
                dve.wait_ge(s_bias, 16)
                nc.vector.tensor_copy(ident[:].rearrange("p k c -> p (k c)"), idraw[:]).then_inc(s_id, 1)

                def finish(t, u):
                    dve.wait_ge(s_oh, 2 * t + 1)
                    nc.vector.scalar_tensor_tensor(out=out[:, u, 1], in0=acc[u][0][:], scalar=bias[:, NC:NC + 1],
                                                   in1=out[:, u, 0].bitcast(F32), op0=ALU.add,
                                                   op1=ALU.subtract).then_inc(s_ol, 1)
                    dve.wait_ge(s_oh, 2 * t + 2)
                    low = out[FB:P, u, 2]
                    nc.vector.scalar_tensor_tensor(out=low, in0=acc[u][1][FB:P], scalar=bias[FB:P, NC + 1:],
                                                   in1=low.bitcast(F32), op0=ALU.add, op1=ALU.subtract).then_inc(s_ol, 1)

                def body(t, u):
                    if isinstance(t, int) and t == NT:
                        return finish(t - 1, 1 - u)
                    for f in range(NC):
                        n = (NC * u + f)
                        dve.wait_ge(s_g, NC * t + f + 1)
                        need(dve, s_ff2, NC * t + f + 1 - RING)
                        nc.vector.tensor_copy(gh[:, n % RING], g[:, n % HB]).then_inc(s_gh, 1)
                        dve.wait_ge(s_gh, NC * t + f + 1)
                        nc.vector.tensor_tensor(gl[:, n % RING], g[:, n % HB], gh[:, n % RING].bitcast(F32),
                                                ALU.subtract).then_inc(s_gl, 1)
                        if f == LAG + 1 and not (isinstance(t, int) and t == 0):
                            finish(t - 1, 1 - u)

                tiles(dve, body, NT)

            @block.tensor
            def _(pe):
                def second(t, u, f):
                    n = NC * u + f
                    pe.wait_ge(s_gl, NC * t + f + 1)
                    if f == 0:
                        need(pe, s_ol, 2 * (t - 1))
                        need(pe, s_oh, 2 * (t - 1))
                    h, l = gh[:, n % RING], gl[:, n % RING]
                    if f == NC - 1 and isinstance(t, int) and t == 0:
                        pe.wait_ge(s_id, 1)
                    if f == NC - 1 and residual:
                        nc.tensor.matmul(acc[u][0][:], ident[:, 0], x[:, u, 0], start=False, stop=False)
                        nc.tensor.matmul(acc[u][0][:], ident[:, 0], x[:, u, 1], start=False, stop=False)
                        nc.tensor.matmul(acc[u][1][:], ident[:, 1], x[:, u, 2], start=False, stop=False)
                    for k in range(2):
                        o = acc[u][k][:]
                        end = f == NC - 1
                        nc.tensor.matmul(o, w2(wh, f, k), h, start=f == 0, stop=False)
                        nc.tensor.matmul(o, w2(wl, f, k), h, start=False, stop=False)
                        last = nc.tensor.matmul(o, w2(wh, f, k), l, start=False, stop=end)
                    last.then_inc(s_ff2, 1)

                def body(t, u):
                    if isinstance(t, int) and t == NT:
                        for f in range(LAG):
                            second(t - 1, 1 - u, f + NC - LAG)
                        return
                    need(pe, s_ld[u], (t - u) * 8 + 16)
                    for f in range(NC):
                        n = NC * u + f
                        need(pe, s_g, NC * t + f + 1 - HB)
                        if isinstance(t, int) and t == 0:
                            pe.wait_ge(s_wl, f + 1)
                        product_fm(nc, hid[n % HB][:], w1(f), slice(0, P),
                                   (x[:, u, 0], x[:, u, 1], x[:, u, 2])).then_inc(s_hid, 1)
                        if f >= LAG:
                            second(t, u, f - LAG)
                        elif not (isinstance(t, int) and t == 0):
                            second(t - 1, 1 - u, f + NC - LAG)

                tiles(pe, body, NT)


def att_stage(nc, stored, name, state_in, state_res, w_att, cols_d, ident_d, state_out=None, rows_d=None, sel_d=None,
              hidden=None, means=None, operands=None):
    normed = state_out is None
    WP = D if normed else 2 * P
    WQ = 4 * P + D
    LASTS = NT * BLK
    with ExitStack() as ctx:
        m = Memory(nc, ctx, name)
        x = m.sb("x", [P, 2, 3, TILE], F32R)
        res = m.sb("res", [P, 2, 3, TILE], F32R)
        wh = m.sb("wh", [P, 2, WQ + WP], F32R)
        wl = m.sb("wl", [P, 2, WQ + WP], F32R)
        cols = m.sb("cols", [P, 8], F32)
        idf = m.sb("idf", [P, P], F32)
        idh = m.sb("idh", [P, P], F16)
        idr = m.sb("idr", [P, 2, D if normed else P], F32R)
        q, kbA, kbB, vb = operands
        ks = m.sb("ks", [P, 2, 2, 2, TILE], F32R)
        vt = m.sb("vt", [P, 2, 3, D], BF16)
        vr = m.sb("vr", [P, 2, 2, D], F32)
        mx = m.sb("mx", [P, NH], F32)
        es = m.sb("es", [P, SC], F32)
        ee = m.sb("ee", [P, 2, SC], F32)
        eh = m.sb("eh", [P, 2, SC], F16)
        el = m.sb("el", [P, 2, SC], F16)
        et = m.sb("et", [P, 2, 2, SC], F16)
        rs = m.sb("rs", [P, NH], F32)
        o = m.sb("o", [P, 2 * P], F32)
        ot = m.sb("ot", [P, 2, 3, TILE], F32R)
        sc = m.ps("sc", [P, 1024])
        pt = m.ps("pt", [P, 2, 1024], F16)
        pq = m.ps("pq", [P, TILE])
        pv = m.ps("pv", [P, TILE])
        po = m.ps("po", [P, TILE])
        pp = m.ps("pp", [P, TILE])
        s_w, s_wl, s_wh, s_c, s_id = (m.sem(n) for n in ("w_loaded", "w_lo", "w_hi", "consts_loaded", "ident"))
        s_x, s_res = m.sems("x_loaded", 2), m.sems("res_loaded", 2)
        s_kb = m.sems("k_placed", 2)
        s_qk, s_qkh, s_qkl = m.sem("qk"), m.sem("qk_hi"), m.sem("qk_lo")
        s_v, s_va, s_vr, s_vb2, s_vr2, s_vc, s_vpd, s_vpa = (m.sem(n) for n in
            ("v", "v_first", "v_rest", "v_second", "v_rest2", "v_third", "v_placed_dve", "v_placed_act"))
        s_sc, s_mx, s_sub, s_ex, s_eh, s_el = (m.sem(n) for n in ("scores", "max", "sub", "exp", "e_hi", "e_lo"))
        s_t, s_th, s_tl, s_pv, s_rc, s_nm, s_dup = (m.sem(n) for n in
            ("e_transposed", "et_hi", "et_lo", "pv", "recip", "normed", "o_dup"))
        s_ot, s_oth, s_otl, s_pj = m.sem("o_transposed"), m.sem("ot_hi"), m.sem("ot_lo"), m.sem("projected")
        s_oh, s_ol = m.sem("out_hi"), m.sem("out_lo")
        s_st = stored
        if normed:
            rows = m.sb("rows", [P, D], F32)
            sel = m.sb("sel", [P, 2], F32)
            y = m.sb("y", [P, D], F32)
            st = m.sb("st", [P, 6], F32)
            mv = m.sb("mv", [P, 2], F32)
            ve = m.sb("ve", [P, 1], F32)
            mark = m.sb("mark", [P, 1], F32)
            half = m.sb("half", [P, 1], F32)
            rstd = m.sb("rstd", [P, 1], F32)
            out = m.sb("out", [P, 2, D], F32)
            s_y, s_bs, s_ag, s_ve, s_rt, s_mm, s_half = (m.sem(n) for n in
                ("y", "stats", "aggr", "var_eps", "rstd", "mean", "half"))
            s_me = m.sem("means_out")
        else:
            out = m.sb("out", [P, 1, 3, TILE], F32R)

        def weights(at):
            return wh[:, 0, at:], wl[:, 0, at:], wh[:, 1, at:], wl[:, 1, at:]

        WK, WV, WO = weights(0), weights(4 * P), weights(WQ)
        cuts = (0, 2 * P, 4 * P, WQ, WQ + WP)
        WCH = len(cuts) - 1

        def part(w, k):
            return w[:, :, cuts[k]:cuts[k + 1]]

        wraw = m.sb("wraw", [P, 2, WQ + WP], F32)
        idraw = m.sb("idraw", [P, 2 * (D if normed else P)], F32)[:]

        def at_start(t):
            return isinstance(t, int) and t == 0

        with nc.Block() as block:

            @block.sync
            def _(sp):
                sp.dma_start(wraw[:].rearrange("p a b -> p (a b)"), w_att).then_inc(s_w, 16)
                sp.dma_start(x[:, 0].bitcast(F32), state_in[:, :, 0:TILE]).then_inc(s_x[0], 16)
                sp.dma_start(cols[:], cols_d).then_inc(s_c, 16)
                sp.dma_start(idraw, ident_d[0]).then_inc(s_c, 16)
                sp.dma_start(idf[:], ident_d[1]).then_inc(s_c, 16)
                if normed:
                    sp.dma_start(rows[:], rows_d).then_inc(s_c, 16)
                    sp.dma_start(sel[:], sel_d).then_inc(s_c, 16)
                sp.dma_start(x[:, 1].bitcast(F32), state_in[:, :, TILE:2 * TILE]).then_inc(s_x[1], 16)
                sp.dma_start(res[:, 0].bitcast(F32), state_res[:, :, 0:TILE]).then_inc(s_res[0], 16)

                def place(t, u, unit):
                    read, made = BLK * (t - 1) + 2 * unit + 2, 4 * t + 2
                    if not isinstance(t, int):
                        read, made = sp.snap(read), sp.snap(made)
                    need(sp, s_sc, read)
                    sp.wait_ge(s_qkl, made)
                    for hd in range(HA):
                        r = slice(DH * hd, DH * hd + DH)
                        sp.dma_start(kbA[r, unit, :, hd, :].bitcast(F32),
                                     ks[r, u, 0, :, 2 * P * unit:2 * P * unit + 2 * P].bitcast(F32)).then_inc(s_kb[unit], 16)
                    for hd in range(HBN):
                        for k in range(2):
                            r = slice(FB * k + DH * hd, FB * k + DH * hd + DH)
                            sp.dma_start(kbB[r, unit, :, hd, :].bitcast(F32),
                                         ks[r, u, 1, :, 2 * P * unit:2 * P * unit + 2 * P].bitcast(F32)).then_inc(s_kb[unit], 16)

                def body(t, u):
                    last = isinstance(t, int) and t >= NT - 1
                    if not last:
                        place(t + 1, 1 - u, 0)
                        place(t + 1, 1 - u, 1)
                        need(sp, s_pj, t * (4 if normed else 2))
                        sp.dma_start(res[:, 1 - u].bitcast(F32),
                                     state_res[:, :, bass.ds((t + 1) * TILE, TILE)]).then_inc(s_res[1 - u], 16)

                def load_x(t, u):
                    sp.wait_ge(s_v, 2 * (t - 1))
                    sp.dma_start(x[:, u].bitcast(F32), state_in[:, :, bass.ds(t * TILE, TILE)]).then_inc(s_x[u], 16)

                place(0, 0, 0)
                place(0, 0, 1)
                load_x(2, 0)
                body(0, 0)
                with sp.Fori(0, 2) as i:
                    for d in (1, 2):
                        load_x(2 * i + d + 2, d % 2)
                        body(2 * i + d, d % 2)
                load_x(7, 1)
                body(5, 1)
                body(6, 0)

            @block.gpsimd
            def _(pool):
                if normed:
                    nc.gpsimd.memset(half[:], -0.5).then_inc(s_half, 1)
                    pool.wait_ge(s_half, 1)

                def slot(t, u, j):
                    n = BLK * t + j
                    if not (isinstance(t, int) and t >= NT):
                        pool.wait_ge(s_eh, n + 1)
                        need(pool, s_t, n - 1)
                        nc.gpsimd.tensor_tensor(el[:, j % 2], ee[:, j % 2], eh[:, j % 2], ALU.subtract).then_inc(s_el, 1)
                    if normed and not (isinstance(n, int) and not 3 <= n < LASTS + 3):
                        need(pool, s_ve, n - 2)
                        nc.gpsimd.tensor_tensor(rstd[:], ve[:], half[:], ALU.pow).then_inc(s_rt, 1)
                        pool.wait_ge(s_oh, n - 2)
                        pool.dma_start(hidden[bass.ds((n - 3) * P, P), :], out[:, (j - 3) % 2]).then_inc(s_st[(j - 3) % 2], 16)
                    if not normed and j == 3 and not at_start(t):
                        pool.wait_ge(s_oh, 2 * t)
                        pool.wait_ge(s_ol, 2 * t)
                        pool.dma_start(state_out[:, :, bass.ds((t - 1) * TILE, TILE)], out[:, 0].bitcast(F32)).then_inc(s_st[0], 16)

                tiles(pool, lambda t, u: [slot(t, u, j) for j in range(BLK)], NT)
                if normed:
                    pool.wait_ge(s_st[0], 16 * LASTS // 2)
                    pool.wait_ge(s_st[1], 16 * LASTS // 2)
                else:
                    pool.wait_ge(s_st[0], 16 * NT)

            @block.scalar
            def _(act):
                act.wait_ge(s_w, 16)
                for k in range(WCH):
                    nc.scalar.copy(part(wh, k), part(wraw, k)).then_inc(s_wh, 1)
                act.wait_ge(s_c, 80 if normed else 48)
                nc.scalar.copy(idr[:].rearrange("p a b -> p (a b)"), idraw).then_inc(s_id, 1)
                nc.scalar.copy(idh[:], idf[:]).then_inc(s_id, 1)

                def project(t, u, j):
                    act.wait_ge(s_qk, 4 * t + j + 1)
                    b = cols[:, j:j + 1]
                    if j < 2:
                        for unit in range(2):
                            need(act, s_kb[unit], 16 * 16 * (t - 1))
                        nc.scalar.activation(ks[:, u, j, 0], pq[:], ACT.Identity, bias=b).then_inc(s_qkh, 1)
                    else:
                        need(act, s_sc, BLK * (t - 1))
                        dst = q[:, u, 2 * (j - 2)].rearrange("p (s n) -> p s n", n=P)[:, :, 0:TOK]
                        src = pq[:].rearrange("p (s n) -> p s n", n=TOK)
                        nc.scalar.activation(dst, src, ACT.Identity, bias=b).then_inc(s_qkh, 1)

                def values(t, u, v):
                    k = 2 * t + v
                    src = pv[:, 0:2 * D].rearrange("p (b d) -> p b d", b=2)
                    act.wait_ge(s_v, k + 1)
                    need(act, s_vpd, 2 * k)
                    need(act, s_vpa, 2 * k)
                    nc.scalar.copy(vt[:, :, 0], src).then_inc(s_va, 1)
                    act.wait_ge(s_vr, k + 1)
                    nc.scalar.copy(vt[:, :, 1], vr[:, 0]).then_inc(s_vb2, 1)
                    act.wait_ge(s_vr2, k + 1)
                    nc.scalar.copy(vt[:, :, 2], vr[:, 1]).then_inc(s_vc, 1)
                    act.wait_ge(s_vc, k + 1)
                    need(act, s_pv, BLK * (t - 1))
                    for i in range(2):
                        place_v(nc.scalar.copy, u, v, 1, i).then_inc(s_vpa, 1)

                def place_v(copy, u, v, par, i):
                    src = vt[TOK * i:TOK * i + TOK].rearrange("p b t (h c d) -> p (b t) h c d", c=2, d=DH)[:, :, :, par]
                    dst = vb[TOK * par:TOK * par + TOK, u, i, 6 * v:6 * v + 6, :, DH * par:DH * par + DH]
                    return copy(dst, src)

                def slot(t, u, j):
                    n = BLK * t + j
                    if not (isinstance(n, int) and not 3 <= n < LASTS + 3):
                        act.wait_ge(s_ot, n - 2)
                        ou = u if j == 3 else 1 - u
                        at = slice(P * ((j + 1) % 4), P * ((j + 1) % 4) + P)
                        need(act, s_pj, (4 * (t - 1) if normed else 2 * (t - 1)) if not (isinstance(n, int) and n < 8) else 0)
                        nc.scalar.activation(ot[:, ou, 0, at], po[:, 0:P], ACT.Identity, bias=cols[:, 4:5]).then_inc(s_oth, 1)
                        nc.scalar.activation(ot[:, ou, 2, at], po[:, P:2 * P], ACT.Identity, bias=cols[:, 5:6]).then_inc(s_oth, 1)
                    if not (isinstance(t, int) and t >= NT - 1):
                        project(t + 1, 1 - u, j)
                    if not (isinstance(t, int) and t >= NT):
                        act.wait_ge(s_sub, n + 1)
                        need(act, s_el, n - 1)
                        nc.scalar.activation(ee[:, j % 2], es[:], ACT.Exp, scale=DH ** -0.5).then_inc(s_ex, 1)
                        act.wait_ge(s_ex, n + 1)
                        need(act, s_t, n - 1)
                        nc.scalar.copy(eh[:, j % 2], ee[:, j % 2]).then_inc(s_eh, 1)
                    if not (isinstance(t, int) and t >= NT - 1) and j % 2:
                        values(t + 1, 1 - u, j // 2)
                    if not (isinstance(n, int) and not 2 <= n < LASTS + 2):
                        act.wait_ge(s_nm, 2 * (n - 1))
                        nc.scalar.copy(o[:, D:], o[:, FA:D]).then_inc(s_dup, 1)
                    if not (isinstance(n, int) and not 1 <= n < LASTS + 1):
                        act.wait_ge(s_t, n)
                        need(act, s_pv, n - 2)
                        nc.scalar.copy(et[:, (j + 1) % 2, 1], pt[:, 1, 0:SC]).then_inc(s_tl, 1)
                    if not normed and j >= 2 and not at_start(t):
                        k = 2 * (t - 1) + j - 2
                        act.wait_ge(s_pj, k + 1)
                        if j == 2:
                            need(act, s_st[0], 16 * (t - 1))
                        nc.scalar.activation(out[:, 0, 2 * (j - 2)], pp[:], ACT.Identity,
                                             bias=cols[:, 4 + j:5 + j]).then_inc(s_oh, 1)

                for j in range(BLK):
                    project(0, 0, j)
                    if j % 2:
                        values(0, 0, j // 2)
                tiles(act, lambda t, u: [slot(t, u, j) for j in range(BLK)], NT)

            @block.vector
            def _(dve):
                for k in range(WCH):
                    dve.wait_ge(s_wh, k + 1)
                    nc.vector.tensor_tensor(part(wl, k), part(wraw, k), part(wh, k).bitcast(F32), ALU.subtract).then_inc(s_wl, 1)

                def project(t, u, j):
                    dve.wait_ge(s_qkh, 4 * t + j + 1)
                    b = cols[:, j:j + 1]
                    if j < 2:
                        if j == 0:
                            for unit in range(2):
                                need(dve, s_kb[unit], 16 * 16 * (t - 1))
                        nc.vector.scalar_tensor_tensor(out=ks[:, u, j, 1], in0=pq[:], scalar=b,
                                                       in1=ks[:, u, j, 0].bitcast(F32), op0=ALU.add,
                                                       op1=ALU.subtract).then_inc(s_qkl, 1)
                        return
                    r = slice(0, P) if j == 2 else slice(FB, P)
                    view = lambda k: q[r, u, k].rearrange("p (s n) -> p s n", n=P)[:, :, 0:TOK]
                    src = pq[r].rearrange("p (s n) -> p s n", n=TOK)
                    hi, lo = (view(0), view(1)) if j == 2 else (view(2), view(2))
                    need(dve, s_sc, BLK * (t - 1))
                    nc.vector.scalar_tensor_tensor(out=lo, in0=src, scalar=cols[r, j:j + 1], in1=hi.bitcast(F32),
                                                   op0=ALU.add, op1=ALU.subtract).then_inc(s_qkl, 1)

                def values(t, u, v):
                    k = 2 * t + v
                    src = pv[:, 0:2 * D].rearrange("p (b d) -> p b d", b=2)
                    dve.wait_ge(s_va, k + 1)
                    nc.vector.tensor_tensor(vr[:, 0], src, vt[:, :, 0], ALU.subtract).then_inc(s_vr, 1)
                    dve.wait_ge(s_vb2, k + 1)
                    nc.vector.tensor_tensor(vr[:, 1], vr[:, 0], vt[:, :, 1], ALU.subtract).then_inc(s_vr2, 1)

                def place_values(t, u, v):
                    k = 2 * t + v
                    dve.wait_ge(s_vc, k + 1)
                    need(dve, s_pv, BLK * (t - 1))
                    for i in range(2):
                        src = vt[TOK * i:TOK * i + TOK].rearrange("p b t (h c d) -> p (b t) h c d", c=2, d=DH)[:, :, :, 0]
                        dst = vb[0:TOK, u, i, 6 * v:6 * v + 6, :, 0:DH]
                        nc.vector.tensor_copy(dst, src).then_inc(s_vpd, 1)

                def slot(t, u, j):
                    n = BLK * t + j
                    if not (isinstance(t, int) and t >= NT):
                        dve.wait_ge(s_sc, n + 1)
                        s3 = sc[:, 0:SC].rearrange("p (h k) -> p h k", h=NH)
                        need(dve, s_sub, n)
                        nc.vector.tensor_reduce(mx[:], s3, AX.X, ALU.max).then_inc(s_mx, 1)
                    if not (isinstance(n, int) and not 3 <= n < LASTS + 3):
                        dve.wait_ge(s_oth, 2 * (n - 2))
                        ou = u if j == 3 else 1 - u
                        at = slice(P * ((j + 1) % 4), P * ((j + 1) % 4) + P)
                        nc.vector.scalar_tensor_tensor(out=ot[:, ou, 1, at], in0=po[:, 0:P], scalar=cols[:, 4:5],
                                                       in1=ot[:, ou, 0, at].bitcast(F32), op0=ALU.add,
                                                       op1=ALU.subtract).then_inc(s_otl, 1)
                        low = ot[FB:P, ou, 2, at]
                        nc.vector.scalar_tensor_tensor(out=low, in0=po[FB:P, P:2 * P], scalar=cols[FB:P, 5:6],
                                                       in1=low.bitcast(F32), op0=ALU.add,
                                                       op1=ALU.subtract).then_inc(s_otl, 1)
                    if not (isinstance(t, int) and t >= NT):
                        dve.wait_ge(s_mx, n + 1)
                        need(dve, s_ex, n)
                        nc.vector.tensor_tensor(es[:].rearrange("p (h k) -> p h k", h=NH), s3,
                                                mx[:].unsqueeze(2).broadcast_to([P, NH, TOK]), ALU.subtract).then_inc(s_sub, 1)
                    if not (isinstance(t, int) and t >= NT - 1):
                        project(t + 1, 1 - u, j)
                        if j % 2:
                            values(t + 1, 1 - u, j // 2)
                    if not (isinstance(n, int) and not 2 <= n < LASTS + 2):
                        dve.wait_ge(s_pv, n - 1)
                        need(dve, s_ot, n - 2)
                        for i in range(2):
                            r = slice(TOK * i, TOK * i + TOK)
                            pr = po[r, 0:HP * 2 * VW].rearrange("p (h i w) -> p h i w", h=HP, i=2)[:, :, i]
                            nc.vector.reciprocal(rs[r].rearrange("p (h c) -> p h c", c=2), pr[:, :, 2 * DH:]).then_inc(s_rc, 1)
                        for i in range(2):
                            r = slice(TOK * i, TOK * i + TOK)
                            pr = po[r, 0:HP * 2 * VW].rearrange("p (h i w) -> p h i w", h=HP, i=2)[:, :, i]
                            dve.wait_ge(s_rc, 2 * (n - 2) + i + 1)
                            nc.vector.tensor_tensor(o[r, 0:D].rearrange("p (h c d) -> p h c d", h=HP, c=2),
                                                    pr[:, :, 0:2 * DH].rearrange("p h (c d) -> p h c d", c=2),
                                                    rs[r].rearrange("p (h c) -> p h c", c=2).unsqueeze(3).broadcast_to([TOK, HP, 2, DH]),
                                                    ALU.mult).then_inc(s_nm, 1)
                    if not (isinstance(n, int) and not 1 <= n < LASTS + 1):
                        dve.wait_ge(s_t, n)
                        need(dve, s_pv, n - 2)
                        nc.vector.tensor_copy(et[:, (j + 1) % 2, 0], pt[:, 0, 0:SC]).then_inc(s_th, 1)
                    if not (isinstance(t, int) and t >= NT - 1) and j % 2:
                        place_values(t + 1, 1 - u, j // 2)
                    if not normed and j >= 2 and not at_start(t):
                        k = 2 * (t - 1) + j - 2
                        dve.wait_ge(s_oh, k + 1)
                        r, c = (slice(0, P), 1) if j == 2 else (slice(FB, P), 2)
                        nc.vector.scalar_tensor_tensor(out=out[r, 0, c], in0=pp[r], scalar=cols[r, 4 + j:5 + j],
                                                       in1=out[r, 0, 2 * (j - 2)].bitcast(F32), op0=ALU.add,
                                                       op1=ALU.subtract).then_inc(s_ol, 1)
                    if normed and not (isinstance(n, int) and not 3 <= n < LASTS + 3):
                        c = n - 2
                        dve.wait_ge(s_pj, c)
                        nc.vector.tensor_tensor(y[:], pp[:, 0:D], rows[:], ALU.add).then_inc(s_y, 1)
                        dve.wait_ge(s_y, c)
                        nc.vector.bn_stats(st[:], y[:]).then_inc(s_bs, 1)
                        dve.wait_ge(s_bs, c)
                        nc.vector.memset(mark[:], 0.0)
                        nc.vector.bn_aggr(mv[:], st[:]).then_inc(s_ag, 1)
                        dve.wait_ge(s_ag, c)
                        nc.vector.tensor_scalar(ve[:], mv[:, 1:2], EPS, None, ALU.add).then_inc(s_ve, 1)
                        dve.wait_ge(s_rt, c)
                        need(dve, s_mm, c - 2)
                        need(dve, s_st[(j - 3) % 2], 8 * (n - 3 - (j - 3) % 2))
                        nc.vector.tensor_scalar(out[:, (j - 3) % 2], y[:], mv[:, 0:1], rstd[:], ALU.subtract,
                                                ALU.mult).then_inc(s_oh, 1)

                for j in range(BLK):
                    project(0, 0, j)
                    if j % 2:
                        values(0, 0, j // 2)
                        place_values(0, 0, j // 2)
                dve.wait_ge(s_c, 80 if normed else 48)
                tiles(dve, lambda t, u: [slot(t, u, j) for j in range(BLK)], NT)
                if normed:
                    dve.wait_ge(s_mm, LASTS)
                    nc.vector.tensor_copy(means[:, 0:IMGS], pp[:, 2 * P:2 * P + IMGS]).then_inc(s_me, 1)
                    nc.vector.tensor_copy(means[0:FB, IMGS:2 * IMGS], pp[0:FB, 3 * P:3 * P + IMGS]).then_inc(s_me, 1)

            @block.tensor
            def _(pe):

                def project(t, u, j):
                    xs = (x[:, u, 0], x[:, u, 1], x[:, u, 2])
                    if j == 0:
                        need(pe, s_x[u], 8 * (t - u) + 16)
                    need(pe, s_qkl, 4 * t + j)
                    product_fm(nc, pq[:], WK, slice(P * j, P * j + P), xs).then_inc(s_qk, 1)
                    if j % 2:
                        v = j // 2
                        need(pe, s_vr, 2 * t + v)
                        for b in range(2):
                            at = slice(P * (2 * v + b), P * (2 * v + b) + P)
                            last = product_tm(nc, pv[:, D * b:D * b + D], tuple(k[:, at] for k in xs), WV, slice(0, D))
                        last.then_inc(s_v, 1)

                def scores(t, u, j):
                    n = BLK * t + j
                    unit, g = j // 2, j % 2
                    pe.wait_ge(s_kb[unit], 16 * 16 * (t + 1))
                    pe.wait_ge(s_qkl, 4 * t + 4)
                    need(pe, s_sub, n)
                    for a in range(2):
                        kb = (kbA, kbB)[a]
                        o_ = sc[:, 0:HA * TOK] if a == 0 else sc[:, HA * TOK:SC]
                        for i in range(2):
                            at = slice(P * g + TOK * i, P * g + TOK * i + TOK)
                            kh, kl = kb[:, unit, 0, :, at], kb[:, unit, 1, :, at]
                            own = slice(P * (2 * j + i) - TOK * i, P * (2 * j + i) - TOK * i + P)
                            if a == 0:
                                qh, ql = q[:, u, 0, own], q[:, u, 1, own]
                                nc.tensor.matmul(o_, qh, kh, start=i == 0, stop=False)
                                nc.tensor.matmul(o_, qh, kl, start=False, stop=False)
                                last = nc.tensor.matmul(o_, ql, kh, start=False, stop=i == 1)
                            else:
                                qb = q[:, u, 2, own]
                                nc.tensor.matmul(o_, qb, kh, start=i == 0, stop=False)
                                last = nc.tensor.matmul(o_, qb, kl, start=False, stop=i == 1)
                    last.then_inc(s_sc, 1)

                def slot(t, u, j):
                    n = BLK * t + j
                    if not (isinstance(t, int) and t >= NT):
                        scores(t, u, j)
                    if not (isinstance(n, int) and not 3 <= n < LASTS + 3):
                        pe.wait_ge(s_nm, 2 * (n - 2))
                        pe.wait_ge(s_dup, n - 2)
                        for k in range(2):
                            last = nc.tensor.transpose(po[:, P * k:P * k + P], o[:, P * k:P * k + P], idf[:])
                        last.then_inc(s_ot, 1)
                    if not (isinstance(t, int) and t >= NT - 1):
                        project(t + 1, 1 - u, j)
                    if not (isinstance(n, int) and not 2 <= n < LASTS + 2):
                        jj, uu = (j - 2) % 4, u if j >= 2 else 1 - u
                        pe.wait_ge(s_th, n - 1)
                        pe.wait_ge(s_tl, n - 1)
                        need(pe, s_otl, 2 * (n - 2))
                        if jj == 0 or jj == 2:
                            tt = (t if j >= 2 else t - 1)
                            pe.wait_ge(s_vpa, 4 * tt + 2 * (jj // 2) + 2)
                            pe.wait_ge(s_vpd, 4 * tt + 2 * (jj // 2) + 2)
                        for hp in range(HP):
                            o_ = po[:, 2 * VW * hp:2 * VW * hp + 2 * VW].rearrange("p (i w) -> p i w", i=2)
                            terms = [(0, 0), (0, 1), (0, 2), (1, 0), (1, 1)]
                            for k, (e, v) in enumerate(terms):
                                last = nc.tensor.matmul(o_, et[:, j % 2, e, P * hp:P * hp + P], vb[:, uu, :, 3 * jj + v, hp],
                                                        start=k == 0, stop=k == len(terms) - 1)
                        last.then_inc(s_pv, 1)
                    if not (isinstance(n, int) and not 1 <= n < LASTS + 1):
                        pe.wait_ge(s_el, n)
                        need(pe, s_th, n - 1)
                        need(pe, s_tl, n - 1)
                        for e, src in ((0, eh), (1, el)):
                            for hp in range(HP):
                                last = nc.tensor.transpose(pt[:, e, P * hp:P * hp + P], src[:, (j + 1) % 2, P * hp:P * hp + P], idh[:])
                        last.then_inc(s_t, 1)
                    if not normed and j >= 2 and not at_start(t):
                        a, uu = j - 2, 1 - u
                        pe.wait_ge(s_otl, 2 * BLK * t)
                        need(pe, s_ol, 2 * (t - 1) + a)
                        if a == 0:
                            need(pe, s_res[uu], 8 * (t - 1 - uu) + 16)
                        product_fm(nc, pp[:], WO, slice(P * a, P * a + P), (ot[:, uu, 0], ot[:, uu, 1], ot[:, uu, 2]), last=False)
                        if a == 0:
                            nc.tensor.matmul(pp[:], idr[:, 0], res[:, uu, 0], start=False, stop=False)
                            nc.tensor.matmul(pp[:], idr[:, 0], res[:, uu, 1], start=False, stop=True).then_inc(s_pj, 1)
                        else:
                            nc.tensor.matmul(pp[:], idr[:, 1], res[:, uu, 2], start=False, stop=True).then_inc(s_pj, 1)
                            
                    if normed:
                        if not (isinstance(n, int) and not 4 <= n < LASTS + 4):
                            pe.wait_ge(s_oh, n - 3)
                            src = out[:, (j - 4) % 2]
                            c = 2 * (n - 4)
                            nc.tensor.matmul(pp[:, bass.ds(2 * P + c, 2)], src[:, 0:P], sel[:], start=True, stop=True)
                            nc.tensor.matmul(pp[0:FB, bass.ds(3 * P + c, 2)], src[:, P:D], sel[:], start=True,
                                             stop=True).then_inc(s_mm, 1)
                        if not (isinstance(n, int) and not 3 <= n < LASTS + 3):
                            uu, at = (u if j == 3 else 1 - u), slice(P * ((j + 1) % 4), P * ((j + 1) % 4) + P)
                            pe.wait_ge(s_otl, 2 * (n - 2))
                            need(pe, s_y, n - 3)
                            if j == 3:
                                need(pe, s_res[uu], 8 * (t - uu) + 16)
                            product_tm(nc, pp[:, 0:D], tuple(ot[:, uu, k, at] for k in range(3)), WO, slice(0, D), last=False)
                            nc.tensor.matmul(pp[:, 0:D], res[:, uu, 0, at], idr[:, 0], start=False, stop=False)
                            nc.tensor.matmul(pp[:, 0:D], res[:, uu, 1, at], idr[:, 0], start=False, stop=False)
                            nc.tensor.matmul(pp[:, 0:D], res[:, uu, 2, at], idr[:, 1], start=False, stop=True).then_inc(s_pj, 1)

                for j in range(BLK):
                    pe.wait_ge(s_wl, (1, 3, 3, 3)[j])
                    project(0, 0, j)
                pe.wait_ge(s_wl, WCH)
                pe.wait_ge(s_id, 2)
                tiles(pe, lambda t, u: [slot(t, u, j) for j in range(BLK)], NT)




def route_stage(nc, means, wg_d, consts_d, hidden, lists, weights):
    with ExitStack() as ctx:
        m = Memory(nc, ctx, "ro")
        wg = m.sb("wg", [P, 2, NE], F32)
        C = m.sb("consts", [P, 3 * P + SLOTS], F32)
        ones = m.sb("ones", [TOK, P], F32)
        zero = m.sb("zero", [TOK, D], F32)
        s1 = m.sb("s1", [TOK, 32], F32)
        e3 = m.sb("e3", [TOK, 8, NE], F32)
        cnt = m.sb("cnt", [P, 4, NE], F32)
        gt = m.sb("gt", [P, NE, 8], F32)
        pm = m.sb("pm", [TOK, 2, SLOTS], F32)
        row = m.sb("row", [1, 4, SLOTS], F32)
        ps = m.ps("ps", [P, TILE])
        pr = m.ps("pr", [P, TILE])
        s_ld, s_d, s_p, s_e, s_z = m.sem("loaded"), m.sem("dve_step"), m.sem("product"), m.sem("exp"), m.sem("zeros_stored")
        before, image = C[0:IMGS, 0:IMGS], C[0:IMGS, IMGS:IMGS + 1]
        thresholds = C[:, P:P + 8]
        slots = C[:, 3 * P:3 * P + SLOTS]
        prob, onehot = e3[:, 2], e3[:, 5]
        with nc.Block() as block:

            @block.sync
            def _(sp):
                sp.dma_start(wg[:], wg_d).then_inc(s_ld, 16)
                sp.dma_start(C[:], consts_d).then_inc(s_ld, 16)
                sp.wait_ge(s_d, 2)
                sp.dma_start(hidden[IMGS * TOK:], zero[:]).then_inc(s_z, 16)
                sp.wait_ge(s_z, 16)

            @block.scalar
            def _(act):
                act.wait_ge(s_d, 4)
                nc.scalar.activation(e3[:, 1], e3[:, 0], ACT.Exp).then_inc(s_e, 1)

            @block.vector
            def _(dve):
                steps = [0]

                def step(ins):
                    ins.then_inc(s_d, 1)
                    steps[0] += 1
                    dve.wait_ge(s_d, steps[0])

                v = nc.vector
                step(v.memset(ones[:], 1.0))
                step(v.memset(zero[:], 0.0))
                dve.wait_ge(s_ld, 32)
                dve.wait_ge(s_p, 1)
                step(v.tensor_reduce(s1[:, 0:1], ps[0:IMGS, 0:NE], AX.X, ALU.max))
                step(v.tensor_scalar(e3[:, 0], ps[0:IMGS, 0:NE], s1[:, 0:1], None, ALU.subtract))
                dve.wait_ge(s_e, 1)
                step(v.tensor_reduce(s1[:, 1:2], e3[:, 1], AX.X, ALU.add))
                step(v.reciprocal(s1[:, 2:3], s1[:, 1:2]))
                step(v.tensor_scalar(prob, e3[:, 1], s1[:, 2:3], None, ALU.mult))
                step(v.tensor_reduce(s1[:, 3:4], prob, AX.X, ALU.max))
                step(v.tensor_scalar(e3[:, 3], prob, s1[:, 3:4], None, ALU.is_equal))
                step(v.tensor_scalar(e3[:, 4], e3[:, 3], -1.0, 1.0, ALU.mult, ALU.add))
                step(v.tensor_copy(onehot[:, 0:1], e3[:, 3, 0:1]))
                step(v.tensor_tensor(onehot[:, 1:2], e3[:, 3, 1:2], e3[:, 4, 0:1], ALU.mult))
                step(v.tensor_tensor(s1[:, 4:5], e3[:, 4, 0:1], e3[:, 4, 1:2], ALU.mult))
                step(v.tensor_tensor(onehot[:, 2:3], e3[:, 3, 2:3], s1[:, 4:5], ALU.mult))
                dve.wait_ge(s_p, 2)
                step(v.tensor_copy(cnt[:, 0], ps[:, P:P + NE]))
                step(v.tensor_tensor(gt[:], cnt[:, 0].unsqueeze(2).broadcast_to([P, NE, 8]),
                                     thresholds.unsqueeze(1).broadcast_to([P, NE, 8]), ALU.is_gt))
                step(v.tensor_reduce(cnt[:, 1], gt[:], AX.X, ALU.add))
                step(v.memset(cnt[:, 2], 0.0))
                step(v.tensor_copy(cnt[:, 2, 1:2], cnt[:, 1, 0:1]))
                step(v.tensor_tensor(cnt[:, 2, 2:3], cnt[:, 1, 0:1], cnt[:, 1, 1:2], ALU.add))
                step(v.scalar_tensor_tensor(out=e3[:, 6], in0=cnt[0:IMGS, 2], scalar=float(GRP), in1=ps[0:IMGS, 2 * P:2 * P + NE],
                                            op0=ALU.mult, op1=ALU.add))
                step(v.tensor_tensor(e3[:, 7], e3[:, 6], onehot, ALU.mult))
                step(v.tensor_reduce(s1[:, 5:6], e3[:, 7], AX.X, ALU.add))
                step(v.tensor_scalar(pm[:, 0], slots[0:IMGS], s1[:, 5:6], None, ALU.is_equal))
                step(v.tensor_scalar(pm[:, 1], pm[:, 0], s1[:, 3:4], None, ALU.mult))
                dve.wait_ge(s_p, 3)
                step(v.tensor_scalar(row[:, 0], pr[0:1, P:P + SLOTS], -1.0, 1.0, ALU.mult, ALU.add))
                step(v.scalar_tensor_tensor(out=row[:, 1], in0=row[:, 0], scalar=float(IMGS), in1=pr[0:1, 0:SLOTS],
                                            op0=ALU.mult, op1=ALU.add))
                step(v.tensor_tensor(row[:, 2], row[:, 0], slots[0:1], ALU.mult))
                step(v.tensor_tensor(row[:, 3], row[:, 1], row[:, 2], ALU.add))
                step(v.tensor_scalar(lists[:, 0:SLOTS], row[:, 1], float(TOK), None, ALU.mult))
                step(v.tensor_scalar(lists[:, SLOTS:2 * SLOTS], row[:, 3], float(TOK), None, ALU.mult))
                step(v.tensor_scalar(row[:, 0, 0:NB], slots[0:1, 0:NB], cnt[0:1, 2, 1:2], None, ALU.is_ge))
                step(v.scalar_tensor_tensor(out=lists[:, 2 * SLOTS:], in0=slots[0:1, 0:NB], scalar=cnt[0:1, 2, 2:3],
                                            in1=row[:, 0, 0:NB], op0=ALU.is_ge, op1=ALU.add))
                for i in range(2):
                    r = slice(TOK * i, TOK * i + TOK)
                    step(v.tensor_copy(weights[r], pr[r, 2 * P:2 * P + SLOTS].rearrange("p (k c) -> p k c", c=2)[:, :, i]))

            @block.tensor
            def _(pe):
                pe.wait_ge(s_ld, 32)
                nc.tensor.matmul(ps[0:IMGS, 0:NE], means[:, 0:IMGS], wg[:, 0], start=True, stop=False)
                nc.tensor.matmul(ps[0:IMGS, 0:NE], means[0:FB, IMGS:2 * IMGS], wg[0:FB, 1], start=False, stop=True).then_inc(s_p, 1)
                pe.wait_ge(s_d, 14)
                nc.tensor.matmul(ps[:, P:P + NE], ones[:], onehot, start=True, stop=True)
                nc.tensor.matmul(ps[0:IMGS, 2 * P:2 * P + NE], before, onehot, start=True, stop=True).then_inc(s_p, 1)
                pe.wait_ge(s_d, 25)
                nc.tensor.matmul(pr[0:1, 0:SLOTS], image, pm[:, 0], start=True, stop=True)
                nc.tensor.matmul(pr[0:1, P:P + SLOTS], ones[:, 0:1], pm[:, 0], start=True, stop=True)
                nc.tensor.matmul(pr[:, 2 * P:2 * P + SLOTS], ones[:], pm[:, 1], start=True, stop=True).then_inc(s_p, 1)


def moe_stage(nc, stored, hidden, lists, weights, first, second, ident_d, out_d):
    UN = 4
    HB, AB, RING = 3, 3, 2 * NC
    with ExitStack() as ctx:
        m = Memory(nc, ctx, "mo")
        xt = m.sb("xt", [P, UN, BLK, 2 * P], F32)
        xs = m.sb("xs", [P, 2, 3, TILE], F32R)
        w1 = m.sb("w1", [P, 2, W1C], F32R)
        w2 = m.sb("w2", [P, 2, W2C], F32R)
        idf = m.sb("idf", [P, P], F32)
        g = m.sb("g", [P, 4, TILE], F32)
        gh = m.sb("gh", [P, RING, TILE], F32R)
        gl = m.sb("gl", [P, RING, TILE], F32R)
        wc = m.sb("wc", [P, BLK], F32)
        ya = m.sb("ya", [P, D], F32)
        yb = m.sb("yb", [P, BLK, D], F32)
        st = m.sb("st", [P, 6], F32)
        mv = m.sb("mv", [P, BLK, 2], F32)
        ve = m.sb("ve", [P, BLK], F32)
        half = m.sb("half", [P, BLK], F32)
        mark = m.sb("mark", [P, 1], F32)
        rstd = m.sb("rstd", [P, BLK], F32)
        out = m.sb("out", [P, 2, BLK, D], F32)
        hid = [m.ps(f"hid{i}", [P, TILE]) for i in range(HB)]
        acc = [m.ps(f"acc{i}", [P, TILE]) for i in range(2)]
        tr = m.ps("tr", [P, 2, TILE])
        s_id, s_half = m.sem("ident"), m.sem("half")
        s_x = m.sems("x_loaded", UN)
        s_w1, s_w2 = m.sems("w1_loaded", 2), m.sems("w2_loaded", 2)
        s_dup, s_tr, s_xh, s_xl = m.sem("x_dup"), m.sem("transposed"), m.sem("x_hi"), m.sem("x_lo")
        s_hid, s_g, s_gh, s_gl, s_acc = (m.sem(n) for n in ("hidden", "gelu", "gelu_hi", "gelu_lo", "summed"))
        s_wc, s_ya, s_yb, s_bs, s_ag, s_ve, s_rt, s_o = (m.sem(n) for n in
            ("weight", "biased", "added", "stats", "aggr", "var_eps", "rstd", "out_ready"))
        s_st = stored

        def blocks(eng, body):
            body(0, 0)
            with eng.Fori(0, (NB - 2) // UN) as i:
                for d in range(UN):
                    body(UN * i + 1 + d, (1 + d) % UN)
            for b in range(UN * ((NB - 2) // UN) + 1, NB + 1):
                body(b, b % UN)

        def final(b):
            return isinstance(b, int) and b >= NB - 1

        def ended(b):
            return isinstance(b, int) and b == NB

        def started(b):
            return not (isinstance(b, int) and b == 0)

        W1 = lambda u: (w1[:, u, 0:FF], w1[:, u, 2 * FF:3 * FF], w1[:, u, FF:2 * FF], w1[:, u, 3 * FF:4 * FF])
        with nc.Block() as block:

            @block.sync
            def _(sp):
                sp.dma_start(idf[:], ident_d).then_inc(s_id, 16)

                def entry(eng, at, most):
                    return eng.value_load(lists[0:1, bass.ds(at, 1)], min_val=0, max_val=most)

                def load(b, r):
                    u = r % 2
                    for s in range(GRP):
                        rows = entry(sp, GRP * b + s, IMGS * TOK)
                        if s == 0:
                            need(sp, s_o, BLK * (b - 2) if not isinstance(b, int) or b > 3 else 0)
                        sp.dma_start(xt[TOK * (s % 2):TOK * (s % 2) + TOK, r, s // 2, 0:D],
                                     hidden[bass.ds(rows, TOK), :]).then_inc(s_x[r], 16)
                    e = entry(sp, 2 * SLOTS + b, NE - 1)
                    need(sp, s_g, NC * (b - 1))
                    sp.dma_start(w1[:, u].bitcast(F32), first[:, bass.ds(e * W1C, W1C)]).then_inc(s_w1[u], 16)

                def load2(b, r):
                    u = r % 2
                    e = entry(sp, 2 * SLOTS + b, NE - 1)
                    need(sp, s_ya, BLK * (b - 1))
                    sp.dma_start(w2[:, u].bitcast(F32), second[:, bass.ds(e * W2C, W2C)]).then_inc(s_w2[u], 16)

                def body(b, r):
                    if not final(b):
                        load(b + 1, (r + 1) % UN)
                    if not ended(b):
                        load2(b, r)

                load(0, 0)
                blocks(sp, body)

            @block.gpsimd
            def _(pool):
                nc.gpsimd.memset(half[:], -0.5).then_inc(s_half, 1)
                pool.wait_ge(s_half, 1)

                def body(b, r):
                    if not started(b):
                        return
                    p, u = b - 1, (r - 1) % 2
                    pool.wait_ge(s_ve, p + 1)
                    nc.gpsimd.tensor_tensor(rstd[:], ve[:], half[:], ALU.pow).then_inc(s_rt, 1)
                    for j in range(BLK):
                        for i in range(2):
                            rows = pool.value_load(lists[0:1, bass.ds(SLOTS + GRP * p + 2 * j + i, 1)], min_val=0,
                                                   max_val=(IMGS + SLOTS - 1) * TOK)
                            if i == 0:
                                pool.wait_ge(s_o, BLK * p + j + 1 + BLK)
                            pool.dma_start(out_d[bass.ds(rows, TOK), :], out[TOK * i:TOK * i + TOK, u, j]).then_inc(s_st[u], 16)

                blocks(pool, body)
                for s in s_st:
                    pool.wait_ge(s, 16 * GRP * NB // 2)

            @block.scalar
            def _(act):
                def ready(b, r):
                    u = r % 2
                    need(act, s_x[r], 16 * GRP // UN * (b - r) + 16 * GRP)
                    need(act, s_tr, 2 * (b - 2))
                    nc.scalar.copy(xt[:, r, :, D:], xt[:, r, :, FA:D]).then_inc(s_dup, 1)
                    act.wait_ge(s_tr, 2 * b + 2)
                    need(act, s_hid, NC * (b - 1))
                    nc.scalar.copy(xs[:, u, 0], tr[:, 0]).then_inc(s_xh, 1)
                    nc.scalar.copy(xs[:, u, 2], tr[:, 1]).then_inc(s_xh, 1)

                def body(b, r):
                    u = r % 2
                    if ended(b):
                        return
                    need(act, s_w1[u], 8 * (b - u) + 16)
                    for f in range(NC):
                        n = NC * u + f
                        k = NC * b + f
                        act.wait_ge(s_hid, k + 1)
                        need(act, s_gl, k - 3)
                        nc.scalar.activation(g[:, n % 4], hid[n % HB][:], ACT.Gelu,
                                             bias=w1[:, u, 4 * FF + f:4 * FF + f + 1].bitcast(F32)).then_inc(s_g, 1)
                    if not final(b):
                        ready(b + 1, (r + 1) % UN)

                ready(0, 0)
                blocks(act, body)

            @block.vector
            def _(dve):
                def ready(b, r):
                    u = r % 2
                    dve.wait_ge(s_xh, 2 * b + 1)
                    nc.vector.tensor_tensor(xs[:, u, 1], tr[:, 0], xs[:, u, 0].bitcast(F32), ALU.subtract).then_inc(s_xl, 1)
                    dve.wait_ge(s_xh, 2 * b + 2)
                    low = xs[FB:P, u, 2]
                    nc.vector.tensor_tensor(low, tr[FB:P, 1], low.bitcast(F32), ALU.subtract).then_inc(s_xl, 1)

                def finish(b, r):
                    u = r % 2
                    nc.vector.tensor_copy(wc[:], weights[:, bass.ds(BLK * b, BLK)]).then_inc(s_wc, 1)
                    dve.wait_ge(s_wc, b + 1)
                    for j in range(BLK):
                        k = BLK * b + j
                        c = k + 1
                        dve.wait_ge(s_acc, c)
                        nc.vector.tensor_tensor(ya[:], acc[j % 2][:, 0:D], w2[:, u, 2 * NC * D:].bitcast(F32), ALU.add).then_inc(s_ya, 1)
                        dve.wait_ge(s_ya, c)
                        nc.vector.scalar_tensor_tensor(out=yb[:, j], in0=ya[:], scalar=wc[:, j:j + 1], in1=xt[:, r, j, 0:D],
                                                       op0=ALU.mult, op1=ALU.add).then_inc(s_yb, 1)
                        dve.wait_ge(s_yb, c)
                        nc.vector.bn_stats(st[:], yb[:, j]).then_inc(s_bs, 1)
                        dve.wait_ge(s_bs, c)
                        nc.vector.memset(mark[:], 0.0)
                        nc.vector.bn_aggr(mv[:, j], st[:]).then_inc(s_ag, 1)
                    dve.wait_ge(s_ag, BLK * b + BLK)
                    nc.vector.tensor_scalar(ve[:], mv[:, :, 1], EPS, None, ALU.add).then_inc(s_ve, 1)
                    dve.wait_ge(s_rt, b + 1)
                    need(dve, s_st[u], 8 * GRP * (b - u))
                    for j in range(BLK):
                        nc.vector.tensor_scalar(out[:, u, j], yb[:, j], mv[:, j, 0:1], rstd[:, j:j + 1], ALU.subtract,
                                                ALU.mult).then_inc(s_o, 1)

                def body(b, r):
                    u = r % 2
                    if not ended(b):
                        for f in range(NC):
                            n = NC * u + f
                            k = NC * b + f
                            dve.wait_ge(s_g, k + 1)
                            if f == 0:
                                need(dve, s_acc, BLK * (b - 1))
                            nc.vector.tensor_copy(gh[:, n], g[:, n % 4]).then_inc(s_gh, 1)
                            dve.wait_ge(s_gh, k + 1)
                            nc.vector.tensor_tensor(gl[:, n], g[:, n % 4], gh[:, n].bitcast(F32), ALU.subtract).then_inc(s_gl, 1)
                    if not final(b):
                        ready(b + 1, (r + 1) % UN)
                    if started(b):
                        finish(b - 1, (r - 1) % UN)

                nc.vector.memset(mark[:], 0.0).then_inc(s_o, BLK)
                ready(0, 0)
                blocks(dve, body)

            @block.tensor
            def _(pe):
                pe.wait_ge(s_id, 16)

                def transpose(b, r):
                    pe.wait_ge(s_dup, b + 1)
                    need(pe, s_xl, 2 * b)
                    for k in range(2):
                        for j in range(BLK):
                            last = nc.tensor.transpose(tr[:, k, P * j:P * j + P], xt[:, r, j, P * k:P * k + P], idf[:])
                        last.then_inc(s_tr, 1)

                def second_product(b, r):
                    u = r % 2
                    need(pe, s_w2[u], 8 * (b - u) + 16)
                    pe.wait_ge(s_gl, NC * b + NC)
                    for j in range(BLK):
                        need(pe, s_ya, BLK * b + max(j - 1, 0))
                        o = acc[j % 2][:, 0:D]
                        at = slice(P * j, P * j + P)
                        for f in range(NC):
                            n = NC * u + f
                            h, l = gh[:, n, at], gl[:, n, at]
                            a, c = w2[:, u, D * f:D * f + D], w2[:, u, D * (NC + f):D * (NC + f) + D]
                            nc.tensor.matmul(o, h, a, start=f == 0, stop=False)
                            nc.tensor.matmul(o, h, c, start=False, stop=False)
                            last = nc.tensor.matmul(o, l, a, start=False, stop=f == NC - 1)
                        last.then_inc(s_acc, 1)

                def body(b, r):
                    u = r % 2
                    if not ended(b):
                        need(pe, s_w1[u], 8 * (b - u) + 16)
                        pe.wait_ge(s_xl, 2 * b + 2)
                        for f in range(NC):
                            n = NC * u + f
                            need(pe, s_g, NC * b + f + 1 - HB)
                            product_fm(nc, hid[n % HB][:], W1(u), slice(P * f, P * f + P),
                                       (xs[:, u, 0], xs[:, u, 1], xs[:, u, 2])).then_inc(s_hid, 1)
                    if not final(b):
                        transpose(b + 1, (r + 1) % UN)
                    if started(b):
                        second_product(b - 1, (r - 1) % UN)

                transpose(0, 0)
                blocks(pe, body)


def positions():
    pos = np.arange(TOK, dtype=np.float32)[:, None]
    i = np.arange(D // 2, dtype=np.float32)[None, :]
    ang = (pos / np.power(np.float32(10000.0), np.float32(2.0) * i / np.float32(D))).astype(np.float32)
    pe = np.zeros((TOK, D), np.float32)
    pe[:, 0::2] = np.sin(ang)
    pe[:, 1::2] = np.cos(ang)
    return pe


def stacked(w):
    return np.stack([w[:FA], np.concatenate([w[FA:], w[FA:]])], 1)


def doubled(w):
    return np.concatenate([w, w[..., FA:]], -1)


def lay_out(**a):
    a = {k: np.asarray(v) for k, v in a.items()}
    out = {}
    x = a["x"].reshape(IMGS, 3, 8, 16, 8, 16).transpose(1, 3, 5, 0, 2, 4).reshape(PC, P, NT, TILE)
    out["patches"] = x.transpose(2, 1, 0, 3)
    out["w_patch"] = a["L0_tok_patch_w"].reshape(D, PC, P).transpose(2, 1, 0).reshape(P, PC * D)
    pe = np.concatenate([positions()] * 2)
    row = lambda v: np.broadcast_to(v, (P, D))
    out["rows"] = np.stack([row(a["L0_tok_patch_b"]), row(a["L0_tok_ln_g"]), pe, row(a["L0_tok_ln_b"])], 1)
    eye = np.eye(P, dtype=np.float32)
    out["ident"] = np.concatenate([eye, np.tile(np.eye(FB, dtype=np.float32), (2, 2))], 1)
    w1 = stacked(a["L0_tok_ff1_w"]).reshape(P, 2, NC, P).transpose(0, 2, 1, 3).reshape(P, NC, 2 * P)
    w2 = doubled(a["L0_tok_ff2_w"]).reshape(NC, P, 2 * P).transpose(1, 0, 2)
    out["w_ff"] = np.concatenate([w1, w2], 2).reshape(P, W_FF)
    fm = lambda b: doubled(b).reshape(2, P).T
    out["b_ff"] = np.concatenate([a["L0_tok_ff1_b"].reshape(NC, P).T, fm(a["L0_tok_ff2_b"])], 1)
    def att(wq, bq, wp, bp, normed):
        wq = stacked(np.concatenate([doubled(wq[:, D:2 * D]), doubled(wq[:, 0:D]), wq[:, 2 * D:]], 1))
        wp = stacked(wp if normed else doubled(wp))
        bs = [fm(bq[D:2 * D]), fm(bq[0:D]), fm(bq[2 * D:]), fm(bp)]
        return np.concatenate([wq, wp], 2).reshape(P, -1), np.concatenate(bs, 1)

    out["w_att1"], out["c_att1"] = att(*(a[f"L0_tok_{k}"] for k in ("qkv_w", "qkv_b", "proj_w", "proj_b")), False)
    out["w_att2"], out["c_att2"] = att(*(a[f"L0_attn_{k}"] for k in ("w_qkv", "b_qkv", "w_proj", "b_proj")), True)
    out["b_out2"] = row(a["L0_attn_b_proj"])
    tm = np.zeros((P, 2, D), np.float32)
    tm[:, 0, 0:P] = eye
    tm[:, 1, P:] = np.tile(np.eye(FB, dtype=np.float32), (2, 1))
    out["ident_tm"] = tm.reshape(P, 2 * D)
    sel = np.zeros((P, 2), np.float32)
    sel[:TOK, 0] = sel[TOK:, 1] = 1.0 / TOK
    out["sel"] = sel
    out["wg"] = stacked(a["L0_ffn_Wg"].T)
    c = np.zeros((P, 3 * P + SLOTS), np.float32)
    c[:IMGS, :IMGS] = np.triu(np.ones((IMGS, IMGS)), 1)
    c[:IMGS, IMGS] = np.arange(IMGS)
    c[:, P:P + 8] = GRP * np.arange(8)
    c[:, 3 * P:] = np.arange(SLOTS)
    out["route_consts"] = c
    w1 = np.stack([stacked(w).reshape(P, 2 * FF) for w in a["L0_ffn_W1"]])
    w2 = a["L0_ffn_W2"].reshape(NE, NC, P, D).transpose(0, 2, 1, 3).reshape(NE, P, NC * D)
    out["w_exp"] = np.concatenate([w1, w2], 2).transpose(1, 0, 2).reshape(P, NE * W_MOE)
    out["b1_exp"] = a["L0_ffn_b1"].reshape(NE, NC, P).transpose(0, 2, 1)
    out["b2_exp"] = np.broadcast_to(a["L0_ffn_b2"][:, None], (NE, P, D))
    return {k: np.ascontiguousarray(v) for k, v in out.items()}


def build(nc, arrays, debug=False, upto=9):
    ins = {k: nc.dram_tensor(k, v.shape, mybir.dt.from_np(v.dtype), kind="ExternalInput").ap() for k, v in arrays.items()}
    kind = "ExternalOutput" if debug else "Internal"
    T = IMGS * TOK
    x0, y, x2, x3 = (nc.dram_tensor(n, (P, 3, T), F32, kind=kind).ap() for n in ("x0", "y", "x2", "x3"))
    h = nc.dram_tensor("h", (T + TOK, D), F32, kind=kind).ap()
    idf = ins["ident"][:, 0:P]
    first = nc.dram_tensor("expert_first", (P, NE * W1C), F32, kind="Internal").ap()
    second = nc.dram_tensor("expert_second", (P, NE * W2C), F32, kind="Internal").ap()
    out = nc.dram_tensor("out", ((IMGS + SLOTS) * TOK, D), F32, kind="ExternalOutput").ap()
    stored = [[nc.alloc_semaphore(f"stored{k}{i}") for i in range(2)] for k in range(6)]
    with (
        nc.sbuf_tensor("means", [P, 2 * IMGS], F32) as means,
        nc.sbuf_tensor("lists", [1, 2 * SLOTS + NB], I32) as lists,
        nc.sbuf_tensor("weights", [P, SLOTS // 2], F32) as weights,
    ):
        patch_stage(nc, stored[0], ins["patches"], ins["w_patch"], ins["rows"], idf, x0)
        with (
            nc.sbuf_tensor("q", [P, 2, 3, GRP * P], F32R) as q,
            nc.sbuf_tensor("kbA", [P, 2, 2, HA, 2 * P], F32R) as kbA,
            nc.sbuf_tensor("kbB", [P, 2, 2, HBN, 2 * P], F32R) as kbB,
            nc.sbuf_tensor("vb", [P, 2, 2, BLK * 3, HP, VW], BF16) as vb,
        ):
            operands = (q, kbA, kbB, vb)
            ff_stage(nc, stored[1], "ff1", x0, y, ins["w_ff"], ins["b_ff"], ins["ident"], False, operands=operands)
            att_stage(nc, stored[2], "at1", y, x0, ins["w_att1"], ins["c_att1"], (ins["ident"], idf), state_out=x2,
                      operands=operands)
            ff_stage(nc, stored[3], "ff2", x2, x3, ins["w_ff"], ins["b_ff"], ins["ident"], True,
                     experts=(ins["w_exp"], ins["b1_exp"], ins["b2_exp"], first, second))
            att_stage(nc, stored[4], "at2", x3, x3, ins["w_att2"], ins["c_att2"], (ins["ident_tm"], idf),
                      rows_d=ins["b_out2"], sel_d=ins["sel"], hidden=h, means=means, operands=operands)
        route_stage(nc, means, ins["wg"], ins["route_consts"], h, lists, weights)
        moe_stage(nc, stored[5], h, lists, weights, first, second, idf, out)
    return ["x0", "y", "x2", "x3", "h", "out"] if debug else ["out"]


def kernel(**inputs):
    from concourse import bacc
    from concourse.bass_utils import run_bass_kernel_spmd

    arrays = lay_out(**inputs)
    nc = bacc.Bacc("TRN2", target_bir_lowering=False, num_devices=1)
    build(nc, arrays)
    got = run_bass_kernel_spmd(nc, [arrays], core_ids=[0]).results[0]["out"]
    return got[:IMGS * TOK].reshape(IMGS, TOK, D)
```

```python
from contextlib import ExitStack

import numpy as np

import concourse.bass as bass
from concourse import mybir

F32 = mybir.dt.float32
F32R = mybir.dt.float32r
BF16 = mybir.dt.bfloat16
F16 = mybir.dt.float16
I32 = mybir.dt.int32
ACT = mybir.ActivationFunctionType
ALU = mybir.AluOpType
AX = mybir.AxisListType

P = 128
IMGS, TOK = 64, 64
D, FF, NH, DH = 192, 768, 12, 16
FA, FB = 128, 64
TILE = 512
NT = IMGS * TOK // TILE
BLK = TILE // P
NC = FF // P
PC = 3 * 16 * 16 // P
EPS = 1e-5
NE = 3
GRP = TILE // TOK
NB = IMGS // GRP + NE - 1
SLOTS = NB * GRP
W_FF = NC * 4 * P
W_MOE = 2 * FF + NC * D
W1C = 2 * (2 * FF) + NC
W2C = 2 * NC * D + D
SC = NH * TOK
HP = NH // 2
HA = FA // DH
HBN = NH - HA
VW = 2 * DH + 2


def need(eng, sem, value):
    if isinstance(value, int) and value <= 0:
        return
    eng.wait_ge(sem, value)


def tiles(eng, body, last, peeled=1):
    for t in range(peeled):
        body(t, t % 2)
    pairs = (NT - 1 - peeled) // 2
    with eng.Fori(0, pairs) as i:
        body(2 * i + peeled, peeled % 2)
        body(2 * i + peeled + 1, (peeled + 1) % 2)
    for t in range(peeled + 2 * pairs, last + 1):
        body(t, t % 2)


def product_fm(nc, out, w, cols, x, last=True):
    wah, wal, wbh, wbl = w
    xah, xal, xb = x
    nc.tensor.matmul(out, wah[:, cols], xah, start=True, stop=False)
    nc.tensor.matmul(out, wah[:, cols], xal, start=False, stop=False)
    nc.tensor.matmul(out, wal[:, cols], xah, start=False, stop=False)
    nc.tensor.matmul(out, wbh[:, cols], xb, start=False, stop=False)
    return nc.tensor.matmul(out, wbl[:, cols], xb, start=False, stop=last)


def product_tm(nc, out, x, w, cols, last=True):
    wah, wal, wbh, wbl = w
    xah, xal, xb = x
    nc.tensor.matmul(out, xah, wah[:, cols], start=True, stop=False)
    nc.tensor.matmul(out, xah, wal[:, cols], start=False, stop=False)
    nc.tensor.matmul(out, xal, wah[:, cols], start=False, stop=False)
    nc.tensor.matmul(out, xb, wbh[:, cols], start=False, stop=False)
    return nc.tensor.matmul(out, xb, wbl[:, cols], start=False, stop=last)


class Memory:
    def __init__(self, nc, ctx, stage):
        self.nc, self.ctx, self.stage = nc, ctx, stage
        self.semaphores = []
        ctx.callback(self.clear)

    def clear(self):
        self.nc.all_engine_barrier()
        self.nc.clear_and_free_semaphores(self.semaphores)
        self.nc.all_engine_barrier()

    def sb(self, name, shape, dt):
        return self.ctx.enter_context(self.nc.sbuf_tensor(f"{self.stage}_{name}", shape, dt))

    def ps(self, name, shape, dt=F32):
        return self.ctx.enter_context(self.nc.psum_tensor(f"{self.stage}_{name}", shape, dt))

    def sem(self, name):
        self.semaphores.append(self.nc.alloc_semaphore(f"{self.stage}_{name}"))
        return self.semaphores[-1]

    def sems(self, name, n):
        return [self.sem(f"{name}{i}") for i in range(n)]


def patch_stage(nc, stored, patches, w_patch, rows, ident_d, state_out):
    OWN = 4
    with ExitStack() as ctx:
        m = Memory(nc, ctx, "pe")
        raw = m.sb("raw", [P, 2, PC, TILE], F32)
        xh = m.sb("xh", [P, 2, PC, TILE], F32R)
        xl = m.sb("xl", [P, 2, PC, TILE], F32R)
        wraw = m.sb("wraw", [P, PC * D], F32)
        wh = m.sb("wh", [P, PC * D], F32R)
        wl = m.sb("wl", [P, PC * D], F32R)
        cst = m.sb("cst", [P, 3, D], F32)
        lnb = m.sb("lnb", [P, D], F32)
        ident = m.sb("ident", [P, P], F32)
        half = m.sb("half", [P, BLK], F32)
        y = m.sb("y", [P, BLK, D], F32)
        st = m.sb("st", [P, BLK, 6], F32)
        mv = m.sb("mv", [P, BLK, 2], F32)
        ve = m.sb("ve", [P, BLK], F32)
        mark = m.sb("mark", [P, 1], F32)
        rstd = m.sb("rstd", [P, BLK], F32)
        z = m.sb("z", [P, BLK, D], F32)
        x0 = m.sb("x0", [P, BLK, 2 * P], F32)
        out = m.sb("out", [P, 2, 3, TILE], F32R)
        emb = [m.ps(f"emb{i}", [P, BLK, 2 * P]) for i in range(2)]
        tr = m.ps("tr", [P, 2, TILE])
        s_w, s_const = m.sem("w_loaded"), m.sem("const_loaded")
        s_wh, s_wl, s_pos, s_half = m.sem("w_hi"), m.sem("w_lo"), m.sem("pos_ready"), m.sem("half_ready")
        s_ld = m.sems("patches_loaded", 2)
        s_lo_pool = m.sem("patch_lo_pool")
        s_hi, s_lo, s_emb, s_y = m.sem("patch_hi"), m.sem("patch_lo"), m.sem("embedded"), m.sem("emb_read")
        s_st, s_ag, s_ve, s_rs, s_z, s_x0, s_dup = (m.sem(n) for n in
            ("stats", "aggr", "var_eps", "rstd", "centered", "x0_ready", "x0_dup"))
        s_tr, s_oh, s_ol = m.sem("transposed"), m.sem("out_hi"), m.sem("out_lo")
        s_st_out = stored
        with nc.Block() as block:

            @block.sync
            def _(sp):
                sp.dma_start(raw[:, 0], patches[0]).then_inc(s_ld[0], 16)
                sp.dma_start(wraw[:], w_patch).then_inc(s_w, 16)
                sp.dma_start(cst[:], rows[:, 0:3]).then_inc(s_const, 16)
                sp.dma_start(lnb[:], rows[:, 3]).then_inc(s_const, 16)
                sp.dma_start(ident[:], ident_d).then_inc(s_const, 16)

                def load(t, u):
                    split, split_pool = OWN // 2 * (t - 1), (PC - OWN) // 2 * (t - 1)
                    if not isinstance(t, int):
                        split, split_pool = sp.snap(split), sp.snap(split_pool)
                    need(sp, s_lo, split)
                    need(sp, s_lo_pool, split_pool)
                    src = patches[t] if isinstance(t, int) else patches[bass.ds(t, 1)].squeeze(0)
                    sp.dma_start(raw[:, u], src).then_inc(s_ld[u], 16)

                sp.dma_start(raw[:, 1], patches[1]).then_inc(s_ld[1], 16)
                with sp.Fori(0, 3) as i:
                    load(2 * i + 2, 0)
                    load(2 * i + 3, 1)

            @block.gpsimd
            def _(pool):
                nc.gpsimd.memset(half[:], -0.5).then_inc(s_half, 1)
                pool.wait_ge(s_half, 1)

                def split(t, u):
                    need(pool, s_emb, BLK * (t - 1))
                    for k, c in enumerate(range(OWN, PC, 2)):
                        pool.wait_ge(s_hi, PC // 2 * t + c // 2 + 1)
                        nc.gpsimd.tensor_tensor(xl[:, u, c:c + 2], raw[:, u, c:c + 2], xh[:, u, c:c + 2].bitcast(F32),
                                                ALU.subtract).then_inc(s_lo_pool, 1)

                def factor(t):
                    pool.wait_ge(s_ve, t + 1)
                    need(pool, s_x0, BLK * t)
                    nc.gpsimd.tensor_tensor(rstd[:], ve[:], half[:], ALU.pow).then_inc(s_rs, 1)

                def store(t, u):
                    pool.wait_ge(s_oh, 2 * t + 2)
                    pool.wait_ge(s_ol, 2 * t + 2)
                    dst = state_out[:, :, bass.ds(t * TILE, TILE)]
                    pool.dma_start(dst, out[:, u].bitcast(F32)).then_inc(s_st_out[u], 16)

                def body(t, u):
                    if not (isinstance(t, int) and t >= NT - 1):
                        split(t + 1, 1 - u)
                    if not (isinstance(t, int) and t == NT):
                        factor(t)
                    if not (isinstance(t, int) and t == 0):
                        store(t - 1, 1 - u)

                split(0, 0)
                tiles(pool, body, NT)
                for s in s_st_out:
                    pool.wait_ge(s, 16 * NT // 2)

            @block.scalar
            def _(act):
                def split(t, u):
                    need(act, s_ld[u], 16 * ((t - u) // 2 + 1) if isinstance(t, int) else (t - u) * 8 + 16)
                    need(act, s_emb, BLK * (t - 1))
                    for c in range(0, PC, 2):
                        nc.scalar.copy(xh[:, u, c:c + 2], raw[:, u, c:c + 2]).then_inc(s_hi, 1)

                def duplicate(t):
                    act.wait_ge(s_x0, BLK * t + BLK)
                    need(act, s_tr, 2 * t)
                    nc.scalar.copy(x0[:, :, P + FB:], x0[:, :, P:P + FB]).then_inc(s_dup, 1)

                def finish(t, u):
                    act.wait_ge(s_tr, 2 * t + 2)
                    need(act, s_st_out[u], 8 * (t - u))
                    nc.scalar.copy(out[:, u, 0], tr[:, 0]).then_inc(s_oh, 1)
                    nc.scalar.copy(out[:, u, 2], tr[:, 1]).then_inc(s_oh, 1)

                def body(t, u):
                    if not (isinstance(t, int) and t >= NT - 1):
                        split(t + 1, 1 - u)
                    if not (isinstance(t, int) and t < 2):
                        finish(t - 2, u)
                    if not (isinstance(t, int) and not 1 <= t <= NT):
                        duplicate(t - 1)

                split(0, 0)
                act.wait_ge(s_w, 16)
                nc.scalar.copy(wh[:], wraw[:]).then_inc(s_wh, 1)
                tiles(act, body, NT + 1, 2)

            @block.vector
            def _(dve):
                def split(t, u):
                    need(dve, s_emb, BLK * (t - 1))
                    for k, c in enumerate(range(0, OWN, 2)):
                        dve.wait_ge(s_hi, 3 * t + k + 1)
                        nc.vector.tensor_tensor(xl[:, u, c:c + 2], raw[:, u, c:c + 2],
                                                xh[:, u, c:c + 2].bitcast(F32), ALU.subtract).then_inc(s_lo, 1)

                def normalize(t, u):
                    dve.wait_ge(s_emb, BLK * t + BLK)
                    nc.vector.tensor_tensor(y[:], emb[u][:, :, 0:D],
                                            cst[:, 0].unsqueeze(1).broadcast_to([P, BLK, D]), ALU.add).then_inc(s_y, 1)
                    dve.wait_ge(s_y, t + 1)
                    for b in range(BLK):
                        nc.vector.bn_stats(st[:, b], y[:, b]).then_inc(s_st, 1)
                    dve.wait_ge(s_st, BLK * t + BLK)
                    nc.vector.memset(mark[:], 0.0)
                    for b in range(BLK):
                        nc.vector.bn_aggr(mv[:, b], st[:, b]).then_inc(s_ag, 1)
                    dve.wait_ge(s_ag, BLK * t + BLK)
                    need(dve, s_rs, t)
                    nc.vector.tensor_scalar(ve[:], mv[:, :, 1], EPS, None, ALU.add).then_inc(s_ve, 1)
                    for b in range(BLK):
                        nc.vector.scalar_tensor_tensor(out=z[:, b], in0=y[:, b], scalar=mv[:, b, 0:1], in1=cst[:, 1],
                                                       op0=ALU.subtract, op1=ALU.mult).then_inc(s_z, 1)
                    dve.wait_ge(s_rs, t + 1)
                    need(dve, s_tr, 2 * t)
                    for b in range(BLK):
                        dve.wait_ge(s_z, BLK * t + b + 1)
                        nc.vector.scalar_tensor_tensor(out=x0[:, b, 0:D], in0=z[:, b], scalar=rstd[:, b:b + 1],
                                                       in1=cst[:, 2], op0=ALU.mult, op1=ALU.add).then_inc(s_x0, 1)

                def finish(t, u):
                    dve.wait_ge(s_oh, 2 * t + 1)
                    nc.vector.tensor_tensor(out[:, u, 1], tr[:, 0], out[:, u, 0].bitcast(F32),
                                            ALU.subtract).then_inc(s_ol, 1)
                    dve.wait_ge(s_oh, 2 * t + 2)
                    low = out[FB:P, u, 2]
                    nc.vector.tensor_tensor(low, tr[FB:P, 1], low.bitcast(F32), ALU.subtract).then_inc(s_ol, 1)

                def body(t, u):
                    if not (isinstance(t, int) and t >= NT - 1):
                        split(t + 1, 1 - u)
                    if not (isinstance(t, int) and t == NT):
                        normalize(t, u)
                    if not (isinstance(t, int) and t == 0):
                        finish(t - 1, 1 - u)

                split(0, 0)
                dve.wait_ge(s_wh, 1)
                nc.vector.tensor_tensor(wl[:], wraw[:], wh[:].bitcast(F32), ALU.subtract).then_inc(s_wl, 1)
                dve.wait_ge(s_const, 48)
                nc.vector.tensor_tensor(cst[:, 2], cst[:, 2], lnb[:], ALU.add).then_inc(s_pos, 1)
                dve.wait_ge(s_pos, 1)
                tiles(dve, body, NT)

            @block.tensor
            def _(pe):
                pe.wait_ge(s_wl, 1)
                pe.wait_ge(s_const, 48)

                def embed(t, u):
                    need(pe, s_y, t - 1)
                    for b in range(BLK):
                        o = emb[u][:, b, 0:D]
                        for c in range(PC):
                            if b == 0 and c % 2 == 0 and c < OWN:
                                pe.wait_ge(s_lo, OWN // 2 * t + c // 2 + 1)
                            if b == 0 and c % 2 == 0 and c >= OWN:
                                pe.wait_ge(s_lo_pool, (PC - OWN) // 2 * t + (c - OWN) // 2 + 1)
                            h, l = xh[:, u, c, P * b:P * b + P], xl[:, u, c, P * b:P * b + P]
                            w0, w1 = wh[:, D * c:D * c + D], wl[:, D * c:D * c + D]
                            nc.tensor.matmul(o, h, w0, start=c == 0, stop=False)
                            nc.tensor.matmul(o, h, w1, start=False, stop=False)
                            last = nc.tensor.matmul(o, l, w0, start=False, stop=c == PC - 1)
                        last.then_inc(s_emb, 1)

                def transpose(t, u):
                    pe.wait_ge(s_dup, t + 1)
                    need(pe, s_oh, 2 * t)
                    need(pe, s_ol, 2 * t)
                    for k in range(2):
                        for b in range(BLK):
                            last = nc.tensor.transpose(tr[:, k, P * b:P * b + P], x0[:, b, P * k:P * k + P], ident[:])
                        last.then_inc(s_tr, 1)

                def body(t, u):
                    if not (isinstance(t, int) and t == NT - 1):
                        embed(t + 1, 1 - u)
                    transpose(t, u)

                embed(0, 0)
                tiles(pe, body, NT - 1)


def ff_stage(nc, stored, name, state_in, state_out, w_ff, b_ff, ident_d, residual, operands=None, experts=None):
    LAG, HB = 3, 4
    RING = 6
    with ExitStack() as ctx:
        m = Memory(nc, ctx, name)
        x = m.sb("x", [P, 2, 3, TILE], F32R)
        wraw = m.sb("wraw", [P, W_FF], F32)
        wh = m.sb("wh", [P, W_FF], F32R)
        wl = m.sb("wl", [P, W_FF], F32R)
        bias = m.sb("bias", [P, NC + 2], F32)
        idraw = m.sb("idraw", [P, 2 * P], F32)
        ident = m.sb("ident", [P, 2, P], F32R)
        g = m.sb("g", [P, HB, TILE], F32)
        gh = m.sb("gh", [P, RING, TILE], F32R)
        gl = m.sb("gl", [P, RING, TILE], F32R)
        out = m.sb("out", [P, 2, 3, TILE], F32R)
        hid = [m.ps(f"hid{i}", [P, TILE]) for i in range(HB)]
        acc = [[m.ps(f"acc{u}{k}", [P, TILE]) for k in range(2)] for u in range(2)]
        s_w = m.sems("w_loaded", NC)
        s_wh, s_wl, s_idl, s_id, s_bias = (m.sem(n) for n in ("w_hi", "w_lo", "ident_loaded", "ident_ready", "bias_loaded"))
        s_ld = m.sems("x_loaded", 2)
        s_hid, s_g, s_gh, s_gl, s_ff2 = (m.sem(n) for n in ("hidden", "gelu", "gelu_hi", "gelu_lo", "second_used"))
        s_oh, s_ol = m.sem("out_hi"), m.sem("out_lo")
        s_st = stored
        if operands:
            q, kbA, kbB, vb = operands
            s_zero = m.sem("zeroed")
        if experts:
            w_exp, b1, b2, blob1, blob2 = experts
            eraw = m.sb("eraw", [P, 2 * FF], F32)
            eh = m.sb("eh", [P, 2 * FF], F32R)
            el = m.sb("el", [P, 2 * FF], F32R)
            s_er, s_eh, s_el, s_es, s_eb = (m.sem(n) for n in
                ("expert_loaded", "expert_hi", "expert_lo", "expert_stored", "expert_biases"))
        CH = W_FF // NC

        def chunk(w, f):
            return w[:, CH * f:CH * f + CH]

        def w1(f):
            a, b = slice(CH * f, CH * f + P), slice(CH * f + P, CH * f + 2 * P)
            return wh[:, a], wl[:, a], wh[:, b], wl[:, b]

        def w2(w, f, k):
            at = CH * f + 2 * P + P * k
            return w[:, at:at + P]

        def piece(t, u):
            return (2 * FF, (t - 1) * (W_MOE // 2), (t - 1) * (W1C // 2)) if u else (
                NC * D, (t - 2) * (W_MOE // 2) + 2 * FF, (t - 2) * (W2C // 2))

        def with_piece(t):
            return experts and not (isinstance(t, int) and not 1 <= t <= 2 * NE)

        with nc.Block() as block:

            @block.sync
            def _(sp):
                sp.dma_start(chunk(wraw, 0), chunk(w_ff, 0)).then_inc(s_w[0], 16)
                sp.dma_start(x[:, 0].bitcast(F32), state_in[:, :, 0:TILE]).then_inc(s_ld[0], 16)
                sp.dma_start(bias[:], b_ff).then_inc(s_bias, 16)
                for f in range(1, NC):
                    sp.dma_start(chunk(wraw, f), chunk(w_ff, f)).then_inc(s_w[f], 16)
                sp.dma_start(idraw[:], ident_d).then_inc(s_idl, 16)
                sp.dma_start(x[:, 1].bitcast(F32), state_in[:, :, TILE:2 * TILE]).then_inc(s_ld[1], 16)
                if experts:
                    for e in range(NE):
                        sp.dma_start(blob1[:, W1C * e + 4 * FF:W1C * e + W1C], b1[e]).then_inc(s_eb, 16)
                        sp.dma_start(blob2[:, W2C * e + 2 * NC * D:W2C * e + W2C], b2[e]).then_inc(s_eb, 16)

                def load(t, u):
                    sp.wait_ge(s_ff2, NC * (t - 1))
                    sp.dma_start(x[:, u].bitcast(F32), state_in[:, :, bass.ds(t * TILE, TILE)]).then_inc(s_ld[u], 16)

                def load_piece(t, u):
                    n, at, to = piece(t, u)
                    sp.wait_ge(s_el, t)
                    sp.dma_start(eraw[:, 0:n], w_exp[:, bass.ds(at, n)]).then_inc(s_er, 16)

                def store_piece(t, u):
                    n, at, to = piece(t, u)
                    blob = blob1 if u else blob2
                    sp.wait_ge(s_eh, t)
                    sp.dma_start(blob[:, bass.ds(to, n)], eh[:, 0:n].bitcast(F32)).then_inc(s_es, 16)
                    sp.wait_ge(s_el, t + 1)
                    sp.dma_start(blob[:, bass.ds(to + n, n)], el[:, 0:n].bitcast(F32)).then_inc(s_es, 16)

                with sp.Fori(0, 3) as i:
                    if experts:
                        load_piece(2 * i + 1, 1)
                    load(2 * i + 2, 0)
                    if experts:
                        store_piece(2 * i + 1, 1)
                        load_piece(2 * i + 2, 0)
                    load(2 * i + 3, 1)
                    if experts:
                        store_piece(2 * i + 2, 0)
                if experts:
                    sp.wait_ge(s_es, 16 * 2 * 2 * NE)
                    sp.wait_ge(s_eb, 16 * 2 * NE)

            @block.gpsimd
            def _(pool):
                if operands:
                    nc.gpsimd.memset(q[:].rearrange("p a b c -> p (a b c)").bitcast(F32), 0.0)
                    nc.gpsimd.memset(kbA[:].rearrange("p a b c d -> p (a b c d)").bitcast(F32), 0.0)
                    nc.gpsimd.memset(kbB[:].rearrange("p a b c d -> p (a b c d)").bitcast(F32), 0.0)
                    nc.gpsimd.memset(vb[:].rearrange("p a b c d e -> p (a b c d e)").bitcast(F32), 0.0).then_inc(s_zero, 1)
                    pool.wait_ge(s_zero, 1)
                    for par in range(2):
                        ones = vb[TOK * par:TOK * par + TOK].rearrange("p a i k h w -> p (a i) k h w")
                        nc.gpsimd.memset(ones[:, :, 0::3, :, 2 * DH + par:2 * DH + par + 1], 1.0).then_inc(s_zero, 1)
                if experts:
                    nc.gpsimd.memset(el[0:1, 0:1].bitcast(F32), 0.0).then_inc(s_el, 1)
                    pool.wait_ge(s_el, 1)

                def store(t, u):
                    if with_piece(t):
                        n = piece(t, u)[0]
                        pool.wait_ge(s_eh, t)
                        need(pool, s_es, 32 * (t - 1))
                        nc.gpsimd.tensor_tensor(el[:, 0:n], eraw[:, 0:n], eh[:, 0:n].bitcast(F32), ALU.subtract).then_inc(s_el, 1)
                    pool.wait_ge(s_oh, 2 * t + 2)
                    pool.wait_ge(s_ol, 2 * t + 2)
                    pool.dma_start(state_out[:, :, bass.ds(t * TILE, TILE)], out[:, u].bitcast(F32)).then_inc(s_st[u], 16)

                tiles(pool, store, NT - 1)
                for s in s_st:
                    pool.wait_ge(s, 16 * NT // 2)

            @block.scalar
            def _(act):
                for f in range(NC):
                    act.wait_ge(s_w[f], 16)
                    nc.scalar.copy(chunk(wh, f), chunk(wraw, f)).then_inc(s_wh, 1)
                act.wait_ge(s_bias, 16)

                def finish(t, u):
                    act.wait_ge(s_ff2, NC * t + NC)
                    need(act, s_st[u], 8 * (t - u))
                    nc.scalar.activation(out[:, u, 0], acc[u][0][:], ACT.Identity, bias=bias[:, NC:NC + 1]).then_inc(s_oh, 1)
                    nc.scalar.activation(out[:, u, 2], acc[u][1][:], ACT.Identity, bias=bias[:, NC + 1:]).then_inc(s_oh, 1)

                def body(t, u):
                    if isinstance(t, int) and t == NT:
                        return finish(t - 1, 1 - u)
                    for f in range(NC):
                        n = (NC * u + f)
                        act.wait_ge(s_hid, NC * t + f + 1)
                        need(act, s_gl, NC * t + f + 1 - HB)
                        nc.scalar.activation(g[:, n % HB], hid[n % HB][:], ACT.Gelu_apprx_tanh,
                                             bias=bias[:, f:f + 1]).then_inc(s_g, 1)
                        if f == LAG + 1 and not (isinstance(t, int) and t == 0):
                            finish(t - 1, 1 - u)
                        if f == NC - 1 and with_piece(t):
                            n = piece(t, u)[0]
                            act.wait_ge(s_er, 16 * t)
                            need(act, s_es, 32 * (t - 1))
                            nc.scalar.copy(eh[:, 0:n], eraw[:, 0:n]).then_inc(s_eh, 1)

                tiles(act, body, NT)

            @block.vector
            def _(dve):
                for f in range(NC):
                    dve.wait_ge(s_wh, f + 1)
                    nc.vector.tensor_tensor(chunk(wl, f), chunk(wraw, f), chunk(wh, f).bitcast(F32), ALU.subtract).then_inc(s_wl, 1)
                dve.wait_ge(s_idl, 16)
                dve.wait_ge(s_bias, 16)
                nc.vector.tensor_copy(ident[:].rearrange("p k c -> p (k c)"), idraw[:]).then_inc(s_id, 1)

                def finish(t, u):
                    dve.wait_ge(s_oh, 2 * t + 1)
                    nc.vector.scalar_tensor_tensor(out=out[:, u, 1], in0=acc[u][0][:], scalar=bias[:, NC:NC + 1],
                                                   in1=out[:, u, 0].bitcast(F32), op0=ALU.add,
                                                   op1=ALU.subtract).then_inc(s_ol, 1)
                    dve.wait_ge(s_oh, 2 * t + 2)
                    low = out[FB:P, u, 2]
                    nc.vector.scalar_tensor_tensor(out=low, in0=acc[u][1][FB:P], scalar=bias[FB:P, NC + 1:],
                                                   in1=low.bitcast(F32), op0=ALU.add, op1=ALU.subtract).then_inc(s_ol, 1)

                def body(t, u):
                    if isinstance(t, int) and t == NT:
                        return finish(t - 1, 1 - u)
                    for f in range(NC):
                        n = (NC * u + f)
                        dve.wait_ge(s_g, NC * t + f + 1)
                        need(dve, s_ff2, NC * t + f + 1 - RING)
                        nc.vector.tensor_copy(gh[:, n % RING], g[:, n % HB]).then_inc(s_gh, 1)
                        dve.wait_ge(s_gh, NC * t + f + 1)
                        nc.vector.tensor_tensor(gl[:, n % RING], g[:, n % HB], gh[:, n % RING].bitcast(F32),
                                                ALU.subtract).then_inc(s_gl, 1)
                        if f == LAG + 1 and not (isinstance(t, int) and t == 0):
                            finish(t - 1, 1 - u)

                tiles(dve, body, NT)

            @block.tensor
            def _(pe):
                def second(t, u, f):
                    n = NC * u + f
                    pe.wait_ge(s_gl, NC * t + f + 1)
                    if f == 0:
                        need(pe, s_ol, 2 * (t - 1))
                        need(pe, s_oh, 2 * (t - 1))
                    h, l = gh[:, n % RING], gl[:, n % RING]
                    if f == NC - 1 and isinstance(t, int) and t == 0:
                        pe.wait_ge(s_id, 1)
                    if f == NC - 1 and residual:
                        nc.tensor.matmul(acc[u][0][:], ident[:, 0], x[:, u, 0], start=False, stop=False)
                        nc.tensor.matmul(acc[u][0][:], ident[:, 0], x[:, u, 1], start=False, stop=False)
                        nc.tensor.matmul(acc[u][1][:], ident[:, 1], x[:, u, 2], start=False, stop=False)
                    for k in range(2):
                        o = acc[u][k][:]
                        end = f == NC - 1
                        nc.tensor.matmul(o, w2(wh, f, k), h, start=f == 0, stop=False)
                        nc.tensor.matmul(o, w2(wl, f, k), h, start=False, stop=False)
                        last = nc.tensor.matmul(o, w2(wh, f, k), l, start=False, stop=end)
                    last.then_inc(s_ff2, 1)

                def body(t, u):
                    if isinstance(t, int) and t == NT:
                        for f in range(LAG):
                            second(t - 1, 1 - u, f + NC - LAG)
                        return
                    need(pe, s_ld[u], (t - u) * 8 + 16)
                    for f in range(NC):
                        n = NC * u + f
                        need(pe, s_g, NC * t + f + 1 - HB)
                        if isinstance(t, int) and t == 0:
                            pe.wait_ge(s_wl, f + 1)
                        product_fm(nc, hid[n % HB][:], w1(f), slice(0, P),
                                   (x[:, u, 0], x[:, u, 1], x[:, u, 2])).then_inc(s_hid, 1)
                        if f >= LAG:
                            second(t, u, f - LAG)
                        elif not (isinstance(t, int) and t == 0):
                            second(t - 1, 1 - u, f + NC - LAG)

                tiles(pe, body, NT)


def att_stage(nc, stored, s_kp, name, state_in, state_res, w_att, cols_d, ident_d, state_out=None, rows_d=None, sel_d=None,
              hidden=None, means=None, operands=None, preload=()):
    normed = state_out is None
    WP = D if normed else 2 * P
    WQ = 4 * P + D
    LASTS = NT * BLK
    with ExitStack() as ctx:
        m = Memory(nc, ctx, name)
        x = m.sb("x", [P, 2, 3, TILE], F32R)
        res = m.sb("res", [P, 2, 3, TILE], F32R)
        wh = m.sb("wh", [P, 2, WQ + WP], F32R)
        wl = m.sb("wl", [P, 2, WQ + WP], F32R)
        cols = m.sb("cols", [P, 8], F32)
        idf = m.sb("idf", [P, P], F32)
        idh = m.sb("idh", [P, P], F16)
        idr = m.sb("idr", [P, 2, D if normed else P], F32R)
        q, kbA, kbB, vb = operands
        ks = m.sb("ks", [P, 2, 2, 2, TILE], F32R)
        vt = m.sb("vt", [P, 2, 3, D], BF16)
        vr = m.sb("vr", [P, 2, 2, D], F32)
        mx = m.sb("mx", [P, NH], F32)
        es = m.sb("es", [P, SC], F32)
        ee = m.sb("ee", [P, 2, SC], F32)
        eh = m.sb("eh", [P, 2, SC], F16)
        el = m.sb("el", [P, 2, SC], F16)
        et = m.sb("et", [P, 2, 2, SC], F16)
        rs = m.sb("rs", [P, NH], F32)
        o = m.sb("o", [P, 2 * P], F32)
        ot = m.sb("ot", [P, 2, 3, TILE], F32R)
        sc = m.ps("sc", [P, 1024])
        pt = m.ps("pt", [P, 2, 1024], F16)
        pq = m.ps("pq", [P, TILE])
        pv = m.ps("pv", [P, TILE])
        po = m.ps("po", [P, TILE])
        pp = m.ps("pp", [P, TILE])
        s_wl, s_wh, s_c0, s_c, s_id = (m.sem(n) for n in ("w_lo", "w_hi", "biases_loaded", "consts_loaded", "ident"))
        s_w = m.sems("w_loaded", 4)
        s_x, s_res = m.sems("x_loaded", 2), m.sems("res_loaded", 2)
        s_kb, s_pre = m.sems("k_placed", 2), m.sem("preloaded")
        s_qk, s_qkh, s_qkl = m.sem("qk"), m.sem("qk_hi"), m.sem("qk_lo")
        s_v, s_va, s_vr, s_vb2, s_vr2, s_vc, s_vpd, s_vpa = (m.sem(n) for n in
            ("v", "v_first", "v_rest", "v_second", "v_rest2", "v_third", "v_placed_dve", "v_placed_act"))
        s_sc, s_mx, s_sub, s_ex, s_eh, s_el = (m.sem(n) for n in ("scores", "max", "sub", "exp", "e_hi", "e_lo"))
        s_t, s_th, s_tl, s_pv, s_rc, s_nm, s_dup = (m.sem(n) for n in
            ("e_transposed", "et_hi", "et_lo", "pv", "recip", "normed", "o_dup"))
        s_ot, s_oth, s_otl, s_pj = m.sem("o_transposed"), m.sem("ot_hi"), m.sem("ot_lo"), m.sem("projected")
        s_oh, s_ol = m.sem("out_hi"), m.sem("out_lo")
        s_st = stored
        if normed:
            rows = m.sb("rows", [P, D], F32)
            sel = m.sb("sel", [P, 2], F32)
            y = m.sb("y", [P, D], F32)
            st = m.sb("st", [P, 6], F32)
            mv = m.sb("mv", [P, 2], F32)
            ve = m.sb("ve", [P, 1], F32)
            mark = m.sb("mark", [P, 1], F32)
            half = m.sb("half", [P, 1], F32)
            rstd = m.sb("rstd", [P, 1], F32)
            out = m.sb("out", [P, 2, D], F32)
            s_y, s_bs, s_ag, s_ve, s_rt, s_mm, s_half = (m.sem(n) for n in
                ("y", "stats", "aggr", "var_eps", "rstd", "mean", "half"))
            s_me = m.sem("means_out")
        else:
            out = m.sb("out", [P, 1, 3, TILE], F32R)

        def weights(at):
            return wh[:, 0, at:], wl[:, 0, at:], wh[:, 1, at:], wl[:, 1, at:]

        WK, WV, WO = weights(0), weights(4 * P), weights(WQ)
        cuts = (0, 2 * P, 4 * P, WQ, WQ + WP)
        WCH = len(cuts) - 1

        def part(w, k):
            return w[:, :, cuts[k]:cuts[k + 1]]

        wraw = m.sb("wraw", [P, 2, WQ + WP], F32)
        idraw = m.sb("idraw", [P, 2 * (D if normed else P)], F32)[:]

        def at_start(t):
            return isinstance(t, int) and t == 0

        def projected(t, j):
            return po if isinstance(t, int) and t == 0 and j % 2 else pq

        def placed(unit, count):
            return 16 * 16 * count - (16 * HBN if unit == 0 else 0)

        def value_of(t, u, j):
            if j == 0 and not (isinstance(t, int) and not 1 <= t < NT):
                return t, u, 1
            if j == 2 and not (isinstance(t, int) and t >= NT - 1):
                return t + 1, 1 - u, 0
            return None

        def out_of(t, j):
            if normed or j not in (0, 3):
                return None
            if isinstance(t, int) and not (1 <= t <= NT if j == 3 else 2 <= t <= NT + 1):
                return None
            return 2 * (t - 1) if j == 3 else 2 * (t - 2) + 1

        def place_values(eng, copy, t, u, v, par, sem):
            eng.wait_ge(s_vc, 2 * t + v + 1)
            need(eng, s_pv, BLK * (t - 1))
            for i in range(2):
                src = vt[TOK * i:TOK * i + TOK].rearrange("p b t (h c d) -> p (b t) h c d", c=2, d=DH)[:, :, :, par]
                dst = vb[TOK * par:TOK * par + TOK, u, i, 6 * v:6 * v + 6, :, DH * par:DH * par + DH]
                copy(dst, src).then_inc(sem, 1)

        def place_b(eng, u, unit, sem, halves=(0, 1)):
            for hd in range(HBN):
                for k in halves:
                    r = slice(FB * k + DH * hd, FB * k + DH * hd + DH)
                    eng.dma_start(kbB[r, unit, :, hd, :].bitcast(F32),
                                  ks[r, u, 1, :, 2 * P * unit:2 * P * unit + 2 * P].bitcast(F32)).then_inc(sem, 16)

        with nc.Block() as block:

            @block.sync
            def _(sp):
                w_d = w_att.rearrange("p (a b) -> p a b", a=2)
                sp.dma_start(part(wraw, 0), part(w_d, 0)).then_inc(s_w[0], 16)
                sp.dma_start(x[:, 0].bitcast(F32), state_in[:, :, 0:TILE]).then_inc(s_x[0], 16)
                sp.dma_start(cols[:], cols_d).then_inc(s_c0, 16)
                for k in range(1, WCH):
                    sp.dma_start(part(wraw, k), part(w_d, k)).then_inc(s_w[k], 16)
                sp.dma_start(idraw, ident_d[0]).then_inc(s_c, 16)
                sp.dma_start(idf[:], ident_d[1]).then_inc(s_c, 16)
                if normed:
                    sp.dma_start(rows[:], rows_d).then_inc(s_c, 16)
                    sp.dma_start(sel[:], sel_d).then_inc(s_c, 16)
                sp.dma_start(x[:, 1].bitcast(F32), state_in[:, :, TILE:2 * TILE]).then_inc(s_x[1], 16)
                for to, src in preload:
                    sp.dma_start(to[:], src).then_inc(s_pre, 16)
                sp.dma_start(res[:, 0].bitcast(F32), state_res[:, :, 0:TILE]).then_inc(s_res[0], 16)

                def place(t, u, unit):
                    read, made = BLK * (t - 1) + 2 * unit + 2, 4 * t + 2
                    first = isinstance(t, int) and t == 0
                    if not isinstance(t, int):
                        read, made = sp.snap(read), sp.snap(made)
                    need(sp, s_sc, read)
                    sp.wait_ge(s_qkl, 1 if first else made)
                    for hd in range(HA):
                        r = slice(DH * hd, DH * hd + DH)
                        sp.dma_start(kbA[r, unit, :, hd, :].bitcast(F32),
                                     ks[r, u, 0, :, 2 * P * unit:2 * P * unit + 2 * P].bitcast(F32)).then_inc(s_kb[unit], 16)
                    if first:
                        sp.wait_ge(s_qkl, made)
                    place_b(sp, u, unit, s_kb[unit], (0,) if first and unit == 0 else (0, 1))

                def body(t, u):
                    last = isinstance(t, int) and t >= NT - 1
                    if not last:
                        place(t + 1, 1 - u, 0)
                        place(t + 1, 1 - u, 1)
                        need(sp, s_pj, t * (4 if normed else 2))
                        sp.dma_start(res[:, 1 - u].bitcast(F32),
                                     state_res[:, :, bass.ds((t + 1) * TILE, TILE)]).then_inc(s_res[1 - u], 16)

                def load_x(t, u):
                    sp.wait_ge(s_v, 2 * (t - 1))
                    sp.dma_start(x[:, u].bitcast(F32), state_in[:, :, bass.ds(t * TILE, TILE)]).then_inc(s_x[u], 16)

                place(0, 0, 0)
                place(0, 0, 1)
                load_x(2, 0)
                body(0, 0)
                with sp.Fori(0, 2) as i:
                    for d in (1, 2):
                        load_x(2 * i + d + 2, d % 2)
                        body(2 * i + d, d % 2)
                load_x(7, 1)
                body(5, 1)
                body(6, 0)
                if preload:
                    sp.wait_ge(s_pre, 16 * len(preload))

            @block.gpsimd
            def _(pool):
                pool.wait_ge(s_qkl, 2)
                place_b(pool, 0, 0, s_kp, (1,))
                if normed:
                    nc.gpsimd.memset(half[:], -0.5).then_inc(s_half, 1)
                    pool.wait_ge(s_half, 1)

                def slot(t, u, j):
                    n = BLK * t + j
                    with_norm = normed and not (isinstance(n, int) and not 4 <= n < LASTS + 4)
                    if with_norm:
                        pool.wait_ge(s_ve, n - 3)
                        nc.gpsimd.tensor_tensor(rstd[:], ve[:], half[:], ALU.pow).then_inc(s_rt, 1)
                    if not (isinstance(t, int) and t >= NT):
                        pool.wait_ge(s_eh, n + 1)
                        need(pool, s_t, n - 1)
                        nc.gpsimd.tensor_tensor(el[:, j % 2], ee[:, j % 2], eh[:, j % 2], ALU.subtract).then_inc(s_el, 1)
                    if with_norm:
                        pool.wait_ge(s_oh, n - 3)
                        pool.dma_start(hidden[bass.ds((n - 4) * P, P), :], out[:, j % 2]).then_inc(s_st[j % 2], 16)
                    if j == 0 and out_of(t, j) is not None:
                        pool.wait_ge(s_oh, 2 * (t - 1))
                        pool.wait_ge(s_ol, 2 * (t - 1))
                        pool.dma_start(state_out[:, :, bass.ds((t - 2) * TILE, TILE)], out[:, 0].bitcast(F32)).then_inc(s_st[0], 16)

                tiles(pool, lambda t, u: [slot(t, u, j) for j in range(BLK)], NT, 2)
                if not normed:
                    slot(NT + 1, (NT + 1) % 2, 0)
                if normed:
                    pool.wait_ge(s_st[0], 16 * LASTS // 2)
                    pool.wait_ge(s_st[1], 16 * LASTS // 2)
                else:
                    pool.wait_ge(s_st[0], 16 * NT)

            @block.scalar
            def _(act):
                for k in range(WCH):
                    act.wait_ge(s_w[k], 16)
                    nc.scalar.copy(part(wh, k), part(wraw, k)).then_inc(s_wh, 1)
                act.wait_ge(s_c0, 16)

                def project(t, u, j):
                    act.wait_ge(s_qk, 4 * t + j + 1)
                    b = cols[:, j:j + 1]
                    if j < 2:
                        for unit in range(2):
                            need(act, s_kb[unit], placed(unit, t - 1))
                        nc.scalar.activation(ks[:, u, j, 0], projected(t, j)[:], ACT.Identity, bias=b).then_inc(s_qkh, 1)
                    else:
                        need(act, s_sc, BLK * (t - 1))
                        dst = q[:, u, 2 * (j - 2)].rearrange("p (s n) -> p s n", n=P)[:, :, 0:TOK]
                        src = projected(t, j)[:].rearrange("p (s n) -> p s n", n=TOK)
                        nc.scalar.activation(dst, src, ACT.Identity, bias=b).then_inc(s_qkh, 1)

                def value_first(t, u, v):
                    k = 2 * t + v
                    src = pv[:, 0:2 * D].rearrange("p (b d) -> p b d", b=2)
                    act.wait_ge(s_v, k + 1)
                    need(act, s_vpd, 2 * k)
                    need(act, s_vpa, 2 * k)
                    nc.scalar.copy(vt[:, :, 0], src).then_inc(s_va, 1)

                def value_second(t, u, v):
                    act.wait_ge(s_vr, 2 * t + v + 1)
                    nc.scalar.copy(vt[:, :, 1], vr[:, 0]).then_inc(s_vb2, 1)

                def value_third(t, u, v):
                    act.wait_ge(s_vr2, 2 * t + v + 1)
                    nc.scalar.copy(vt[:, :, 2], vr[:, 1]).then_inc(s_vc, 1)

                def slot(t, u, j):
                    n = BLK * t + j
                    made = out_of(t, j)
                    if made is not None:
                        act.wait_ge(s_pj, made + 1)
                        if j == 3:
                            need(act, s_st[0], 16 * (t - 1))
                        a = 0 if j == 3 else 1
                        nc.scalar.activation(out[:, 0, 2 * a], pp[:], ACT.Identity, bias=cols[:, 6 + a:7 + a]).then_inc(s_oh, 1)
                    if not (isinstance(n, int) and not 3 <= n < LASTS + 3):
                        act.wait_ge(s_ot, n - 2)
                        ou = u if j == 3 else 1 - u
                        at = slice(P * ((j + 1) % 4), P * ((j + 1) % 4) + P)
                        need(act, s_pj, (4 * (t - 1) if normed else 2 * (t - 1)) if not (isinstance(n, int) and n < 8) else 0)
                        nc.scalar.activation(ot[:, ou, 0, at], po[:, 0:P], ACT.Identity, bias=cols[:, 4:5]).then_inc(s_oth, 1)
                        nc.scalar.activation(ot[:, ou, 2, at], po[:, P:2 * P], ACT.Identity, bias=cols[:, 5:6]).then_inc(s_oth, 1)
                    if not (isinstance(t, int) and t >= NT - 1):
                        project(t + 1, 1 - u, j)
                    of = value_of(t, u, j)
                    if of:
                        value_second(*of)
                    if not (isinstance(t, int) and t >= NT):
                        act.wait_ge(s_sub, n + 1)
                        need(act, s_el, n - 1)
                        nc.scalar.activation(ee[:, j % 2], es[:], ACT.Exp, scale=DH ** -0.5).then_inc(s_ex, 1)
                        act.wait_ge(s_ex, n + 1)
                        need(act, s_t, n - 1)
                        nc.scalar.copy(eh[:, j % 2], ee[:, j % 2]).then_inc(s_eh, 1)
                    if not (isinstance(n, int) and not 1 <= n < LASTS + 1):
                        act.wait_ge(s_t, n)
                        need(act, s_pv, n - 2)
                        nc.scalar.copy(et[:, (j + 1) % 2, 1], pt[:, 1, 0:SC]).then_inc(s_tl, 1)
                    if not (isinstance(n, int) and not 2 <= n < LASTS + 2):
                        act.wait_ge(s_nm, 2 * (n - 1))
                        nc.scalar.copy(o[:, D:], o[:, FA:D]).then_inc(s_dup, 1)
                    if of:
                        value_third(*of)
                    if not (isinstance(t, int) and t >= NT - 1) and j % 2:
                        value_first(t + 1, 1 - u, j // 2)

                for j in range(BLK):
                    project(0, 0, j)
                act.wait_ge(s_c, 64 if normed else 32)
                nc.scalar.copy(idr[:].rearrange("p a b -> p (a b)"), idraw).then_inc(s_id, 1)
                nc.scalar.copy(idh[:], idf[:]).then_inc(s_id, 1)
                for v in range(2):
                    value_first(0, 0, v)
                    value_second(0, 0, v)
                    value_third(0, 0, v)
                    place_values(act, nc.scalar.copy, 0, 0, v, 1, s_vpa)
                tiles(act, lambda t, u: [slot(t, u, j) for j in range(BLK)], NT, 2)
                if not normed:
                    slot(NT + 1, (NT + 1) % 2, 0)

            @block.vector
            def _(dve):
                for k in range(WCH):
                    dve.wait_ge(s_wh, k + 1)
                    nc.vector.tensor_tensor(part(wl, k), part(wraw, k), part(wh, k).bitcast(F32), ALU.subtract).then_inc(s_wl, 1)

                def project(t, u, j):
                    dve.wait_ge(s_qkh, 4 * t + j + 1)
                    b = cols[:, j:j + 1]
                    if j < 2:
                        if j == 0:
                            for unit in range(2):
                                need(dve, s_kb[unit], placed(unit, t - 1))
                        nc.vector.scalar_tensor_tensor(out=ks[:, u, j, 1], in0=projected(t, j)[:], scalar=b,
                                                       in1=ks[:, u, j, 0].bitcast(F32), op0=ALU.add,
                                                       op1=ALU.subtract).then_inc(s_qkl, 1)
                        return
                    r = slice(0, P) if j == 2 else slice(FB, P)
                    view = lambda k: q[r, u, k].rearrange("p (s n) -> p s n", n=P)[:, :, 0:TOK]
                    src = projected(t, j)[r].rearrange("p (s n) -> p s n", n=TOK)
                    hi, lo = (view(0), view(1)) if j == 2 else (view(2), view(2))
                    need(dve, s_sc, BLK * (t - 1))
                    nc.vector.scalar_tensor_tensor(out=lo, in0=src, scalar=cols[r, j:j + 1], in1=hi.bitcast(F32),
                                                   op0=ALU.add, op1=ALU.subtract).then_inc(s_qkl, 1)

                def rest(t, u, v):
                    k = 2 * t + v
                    src = pv[:, 0:2 * D].rearrange("p (b d) -> p b d", b=2)
                    dve.wait_ge(s_va, k + 1)
                    nc.vector.tensor_tensor(vr[:, 0], src, vt[:, :, 0], ALU.subtract).then_inc(s_vr, 1)

                def second_rest(t, u, v):
                    dve.wait_ge(s_vb2, 2 * t + v + 1)
                    nc.vector.tensor_tensor(vr[:, 1], vr[:, 0], vt[:, :, 1], ALU.subtract).then_inc(s_vr2, 1)

                def slot(t, u, j):
                    n = BLK * t + j
                    with_norm = normed and not (isinstance(n, int) and not 4 <= n < LASTS + 4)
                    c = n - 3
                    if with_norm:
                        need(dve, s_oh, c - 1)
                        dve.wait_ge(s_pj, c)
                        nc.vector.tensor_tensor(y[:], pp[:, 0:D], rows[:], ALU.add).then_inc(s_y, 1)
                        dve.wait_ge(s_y, c)
                        nc.vector.bn_stats(st[:], y[:]).then_inc(s_bs, 1)
                        dve.wait_ge(s_bs, c)
                        nc.vector.memset(mark[:], 0.0)
                        nc.vector.bn_aggr(mv[:], st[:]).then_inc(s_ag, 1)
                        dve.wait_ge(s_ag, c)
                        nc.vector.tensor_scalar(ve[:], mv[:, 1:2], EPS, None, ALU.add).then_inc(s_ve, 1)
                    made = out_of(t, j)
                    if made is not None:
                        a = 0 if j == 3 else 1
                        dve.wait_ge(s_oh, made + 1)
                        r, c = (slice(FB, P), 2) if a else (slice(0, P), 1)
                        nc.vector.scalar_tensor_tensor(out=out[r, 0, c], in0=pp[r], scalar=cols[r, 6 + a:7 + a],
                                                       in1=out[r, 0, 2 * a].bitcast(F32), op0=ALU.add,
                                                       op1=ALU.subtract).then_inc(s_ol, 1)
                    if not (isinstance(t, int) and t >= NT):
                        dve.wait_ge(s_sc, n + 1)
                        s3 = sc[:, 0:SC].rearrange("p (h k) -> p h k", h=NH)
                        need(dve, s_sub, n)
                        nc.vector.tensor_reduce(mx[:], s3, AX.X, ALU.max).then_inc(s_mx, 1)
                    if not (isinstance(n, int) and not 3 <= n < LASTS + 3):
                        dve.wait_ge(s_oth, 2 * (n - 2))
                        ou = u if j == 3 else 1 - u
                        at = slice(P * ((j + 1) % 4), P * ((j + 1) % 4) + P)
                        nc.vector.scalar_tensor_tensor(out=ot[:, ou, 1, at], in0=po[:, 0:P], scalar=cols[:, 4:5],
                                                       in1=ot[:, ou, 0, at].bitcast(F32), op0=ALU.add,
                                                       op1=ALU.subtract).then_inc(s_otl, 1)
                        low = ot[FB:P, ou, 2, at]
                        nc.vector.scalar_tensor_tensor(out=low, in0=po[FB:P, P:2 * P], scalar=cols[FB:P, 5:6],
                                                       in1=low.bitcast(F32), op0=ALU.add,
                                                       op1=ALU.subtract).then_inc(s_otl, 1)
                    of = value_of(t, u, j)
                    if of:
                        rest(*of)
                    if not (isinstance(t, int) and t >= NT):
                        dve.wait_ge(s_mx, n + 1)
                        need(dve, s_ex, n)
                        nc.vector.tensor_tensor(es[:].rearrange("p (h k) -> p h k", h=NH), s3,
                                                mx[:].unsqueeze(2).broadcast_to([P, NH, TOK]), ALU.subtract).then_inc(s_sub, 1)
                    if with_norm:
                        dve.wait_ge(s_rt, c)
                        need(dve, s_mm, c - 1)
                        need(dve, s_st[j % 2], 8 * (n - 4 - j % 2))
                        nc.vector.tensor_scalar(out[:, j % 2], y[:], mv[:, 0:1], rstd[:], ALU.subtract,
                                                ALU.mult).then_inc(s_oh, 1)
                    if not (isinstance(n, int) and not 1 <= n < LASTS + 1):
                        dve.wait_ge(s_t, n)
                        need(dve, s_pv, n - 2)
                        nc.vector.tensor_copy(et[:, (j + 1) % 2, 0], pt[:, 0, 0:SC]).then_inc(s_th, 1)
                    if not (isinstance(t, int) and t >= NT - 1):
                        project(t + 1, 1 - u, j)
                    if of:
                        second_rest(*of)
                    if not (isinstance(n, int) and not 2 <= n < LASTS + 2):
                        dve.wait_ge(s_pv, n - 1)
                        need(dve, s_ot, n - 2)
                        for i in range(2):
                            r = slice(TOK * i, TOK * i + TOK)
                            pr = po[r, 0:HP * 2 * VW].rearrange("p (h i w) -> p h i w", h=HP, i=2)[:, :, i]
                            nc.vector.reciprocal(rs[r].rearrange("p (h c) -> p h c", c=2), pr[:, :, 2 * DH:]).then_inc(s_rc, 1)
                        for i in range(2):
                            r = slice(TOK * i, TOK * i + TOK)
                            pr = po[r, 0:HP * 2 * VW].rearrange("p (h i w) -> p h i w", h=HP, i=2)[:, :, i]
                            dve.wait_ge(s_rc, 2 * (n - 2) + i + 1)
                            nc.vector.tensor_tensor(o[r, 0:D].rearrange("p (h c d) -> p h c d", h=HP, c=2),
                                                    pr[:, :, 0:2 * DH].rearrange("p h (c d) -> p h c d", c=2),
                                                    rs[r].rearrange("p (h c) -> p h c", c=2).unsqueeze(3).broadcast_to([TOK, HP, 2, DH]),
                                                    ALU.mult).then_inc(s_nm, 1)
                    if of:
                        place_values(dve, nc.vector.tensor_copy, *of, 0, s_vpd)
                        place_values(dve, nc.vector.tensor_copy, *of, 1, s_vpa)
                dve.wait_ge(s_c0, 16)
                for j in range(BLK):
                    project(0, 0, j)
                for v in range(2):
                    rest(0, 0, v)
                    second_rest(0, 0, v)
                    place_values(dve, nc.vector.tensor_copy, 0, 0, v, 0, s_vpd)
                dve.wait_ge(s_c, 64 if normed else 32)
                tiles(dve, lambda t, u: [slot(t, u, j) for j in range(BLK)], NT, 2)
                if not normed:
                    slot(NT + 1, (NT + 1) % 2, 0)
                if normed:
                    dve.wait_ge(s_mm, LASTS)
                    nc.vector.tensor_copy(means[:, 0:IMGS], sc[:, SC:SC + IMGS]).then_inc(s_me, 1)
                    nc.vector.tensor_copy(means[0:FB, IMGS:2 * IMGS], sc[0:FB, SC + IMGS:SC + 2 * IMGS]).then_inc(s_me, 1)

            @block.tensor
            def _(pe):

                def project(t, u, j):
                    xs = (x[:, u, 0], x[:, u, 1], x[:, u, 2])
                    if j == 0:
                        need(pe, s_x[u], 8 * (t - u) + 16)
                    first = isinstance(t, int) and t == 0
                    if first:
                        need(pe, s_qkl, j - 1)
                    else:
                        need(pe, s_qkl, 4 * t + j)
                    product_fm(nc, projected(t, j)[:], WK, slice(P * j, P * j + P), xs).then_inc(s_qk, 1)
                    if j % 2 and not first:
                        values(t, u, j // 2)

                def values(t, u, v):
                    xs = (x[:, u, 0], x[:, u, 1], x[:, u, 2])
                    need(pe, s_vr, 2 * t + v)
                    for b in range(2):
                        at = slice(P * (2 * v + b), P * (2 * v + b) + P)
                        last = product_tm(nc, pv[:, D * b:D * b + D], tuple(k[:, at] for k in xs), WV, slice(0, D))
                    last.then_inc(s_v, 1)

                def scores(t, u, j):
                    n = BLK * t + j
                    unit, g = j // 2, j % 2
                    if isinstance(t, int) and t == 0 and j == 0:
                        pe.wait_ge(s_kp, 16 * HBN)
                    pe.wait_ge(s_kb[unit], placed(unit, t + 1))
                    pe.wait_ge(s_qkl, 4 * t + 4)
                    need(pe, s_sub, n)
                    for a in range(2):
                        kb = (kbA, kbB)[a]
                        o_ = sc[:, 0:HA * TOK] if a == 0 else sc[:, HA * TOK:SC]
                        for i in range(2):
                            at = slice(P * g + TOK * i, P * g + TOK * i + TOK)
                            kh, kl = kb[:, unit, 0, :, at], kb[:, unit, 1, :, at]
                            own = slice(P * (2 * j + i) - TOK * i, P * (2 * j + i) - TOK * i + P)
                            if a == 0:
                                qh, ql = q[:, u, 0, own], q[:, u, 1, own]
                                nc.tensor.matmul(o_, qh, kh, start=i == 0, stop=False)
                                nc.tensor.matmul(o_, qh, kl, start=False, stop=False)
                                last = nc.tensor.matmul(o_, ql, kh, start=False, stop=i == 1)
                            else:
                                qb = q[:, u, 2, own]
                                nc.tensor.matmul(o_, qb, kh, start=i == 0, stop=False)
                                last = nc.tensor.matmul(o_, qb, kl, start=False, stop=i == 1)
                    last.then_inc(s_sc, 1)

                def image_means(n, j):
                    need(pe, s_sub, n if not (isinstance(n, int) and n > LASTS) else LASTS)
                    pe.wait_ge(s_oh, n - 4)
                    src = out[:, (j - 1) % 2]
                    c = SC + 2 * (n - 5)
                    nc.tensor.matmul(sc[:, bass.ds(c, 2)], src[:, 0:P], sel[:], start=True, stop=True)
                    nc.tensor.matmul(sc[0:FB, bass.ds(c + IMGS, 2)], src[:, P:D], sel[:], start=True,
                                     stop=True).then_inc(s_mm, 1)

                def slot(t, u, j):
                    n = BLK * t + j
                    if normed and not (isinstance(n, int) and n < 5):
                        image_means(n, j)
                    if not (isinstance(t, int) and t >= NT):
                        scores(t, u, j)
                    if not (isinstance(n, int) and not 3 <= n < LASTS + 3):
                        pe.wait_ge(s_nm, 2 * (n - 2))
                        pe.wait_ge(s_dup, n - 2)
                        for k in range(2):
                            last = nc.tensor.transpose(po[:, P * k:P * k + P], o[:, P * k:P * k + P], idf[:])
                        last.then_inc(s_ot, 1)
                    if not (isinstance(t, int) and t >= NT - 1):
                        project(t + 1, 1 - u, j)
                    if not (isinstance(n, int) and not 1 <= n < LASTS + 1):
                        pe.wait_ge(s_el, n)
                        need(pe, s_th, n - 1)
                        need(pe, s_tl, n - 1)
                        for e, src in ((0, eh), (1, el)):
                            for hp in range(HP):
                                last = nc.tensor.transpose(pt[:, e, P * hp:P * hp + P], src[:, (j + 1) % 2, P * hp:P * hp + P], idh[:])
                        last.then_inc(s_t, 1)
                    if not (isinstance(n, int) and not 2 <= n < LASTS + 2):
                        jj, uu = (j - 2) % 4, u if j >= 2 else 1 - u
                        pe.wait_ge(s_th, n - 1)
                        pe.wait_ge(s_tl, n - 1)
                        need(pe, s_otl, 2 * (n - 2))
                        if jj == 0 or jj == 2:
                            tt = (t if j >= 2 else t - 1)
                            pe.wait_ge(s_vpa, 4 * tt + 2 * (jj // 2) + 2)
                            pe.wait_ge(s_vpd, 4 * tt + 2 * (jj // 2) + 2)
                        for hp in range(HP):
                            o_ = po[:, 2 * VW * hp:2 * VW * hp + 2 * VW].rearrange("p (i w) -> p i w", i=2)
                            terms = [(0, 0), (0, 1), (0, 2), (1, 0), (1, 1)]
                            for k, (e, v) in enumerate(terms):
                                last = nc.tensor.matmul(o_, et[:, j % 2, e, P * hp:P * hp + P], vb[:, uu, :, 3 * jj + v, hp],
                                                        start=k == 0, stop=k == len(terms) - 1)
                        last.then_inc(s_pv, 1)
                    if not normed and j >= 2 and not at_start(t):
                        a, uu = j - 2, 1 - u
                        pe.wait_ge(s_otl, 2 * BLK * t)
                        need(pe, s_ol, 2 * (t - 1) + a)
                        if a == 0:
                            need(pe, s_res[uu], 8 * (t - 1 - uu) + 16)
                        product_fm(nc, pp[:], WO, slice(P * a, P * a + P), (ot[:, uu, 0], ot[:, uu, 1], ot[:, uu, 2]), last=False)
                        if a == 0:
                            nc.tensor.matmul(pp[:], idr[:, 0], res[:, uu, 0], start=False, stop=False)
                            nc.tensor.matmul(pp[:], idr[:, 0], res[:, uu, 1], start=False, stop=True).then_inc(s_pj, 1)
                        else:
                            nc.tensor.matmul(pp[:], idr[:, 1], res[:, uu, 2], start=False, stop=True).then_inc(s_pj, 1)
                            
                    if normed:
                        if not (isinstance(n, int) and not 3 <= n < LASTS + 3):
                            uu, at = (u if j == 3 else 1 - u), slice(P * ((j + 1) % 4), P * ((j + 1) % 4) + P)
                            pe.wait_ge(s_otl, 2 * (n - 2))
                            need(pe, s_y, n - 3)
                            if j == 3:
                                need(pe, s_res[uu], 8 * (t - uu) + 16)
                            product_tm(nc, pp[:, 0:D], tuple(ot[:, uu, k, at] for k in range(3)), WO, slice(0, D), last=False)
                            nc.tensor.matmul(pp[:, 0:D], res[:, uu, 0, at], idr[:, 0], start=False, stop=False)
                            nc.tensor.matmul(pp[:, 0:D], res[:, uu, 1, at], idr[:, 0], start=False, stop=False)
                            nc.tensor.matmul(pp[:, 0:D], res[:, uu, 2, at], idr[:, 1], start=False, stop=True).then_inc(s_pj, 1)

                for j in range(BLK):
                    pe.wait_ge(s_wl, 1 + j // 2)
                    project(0, 0, j)
                pe.wait_ge(s_wl, WCH)
                for v in range(2):
                    values(0, 0, v)
                pe.wait_ge(s_id, 2)
                tiles(pe, lambda t, u: [slot(t, u, j) for j in range(BLK)], NT, 2)
                if normed:
                    image_means(LASTS + 4, 0)




def route_stage(nc, means, wg, C, hidden, lists, weights):
    with ExitStack() as ctx:
        m = Memory(nc, ctx, "ro")
        ones = m.sb("ones", [TOK, P], F32)
        zero = m.sb("zero", [TOK, D], F32)
        s1 = m.sb("s1", [TOK, 32], F32)
        e3 = m.sb("e3", [TOK, 8, NE], F32)
        cnt = m.sb("cnt", [P, 4, NE], F32)
        gt = m.sb("gt", [P, NE, 8], F32)
        pm = m.sb("pm", [TOK, 2, SLOTS], F32)
        row = m.sb("row", [1, 4, SLOTS], F32)
        ps = m.ps("ps", [P, TILE])
        pr = m.ps("pr", [P, TILE])
        s_d, s_p, s_e, s_z = m.sem("dve_step"), m.sem("product"), m.sem("exp"), m.sem("zeros_stored")
        before, image = C[0:IMGS, 0:IMGS], C[0:IMGS, IMGS:IMGS + 1]
        thresholds = C[:, P:P + 8]
        slots = C[:, 3 * P:3 * P + SLOTS]
        prob, onehot = e3[:, 2], e3[:, 5]
        with nc.Block() as block:

            @block.sync
            def _(sp):
                sp.wait_ge(s_d, 2)
                sp.dma_start(hidden[IMGS * TOK:], zero[:]).then_inc(s_z, 16)
                sp.wait_ge(s_z, 16)

            @block.scalar
            def _(act):
                act.wait_ge(s_d, 4)
                nc.scalar.activation(e3[:, 1], e3[:, 0], ACT.Exp).then_inc(s_e, 1)

            @block.vector
            def _(dve):
                steps = [0]

                def step(ins):
                    ins.then_inc(s_d, 1)
                    steps[0] += 1
                    dve.wait_ge(s_d, steps[0])

                v = nc.vector
                step(v.memset(ones[:], 1.0))
                step(v.memset(zero[:], 0.0))
                dve.wait_ge(s_p, 1)
                step(v.tensor_reduce(s1[:, 0:1], ps[0:IMGS, 0:NE], AX.X, ALU.max))
                step(v.tensor_scalar(e3[:, 0], ps[0:IMGS, 0:NE], s1[:, 0:1], None, ALU.subtract))
                dve.wait_ge(s_e, 1)
                step(v.tensor_reduce(s1[:, 1:2], e3[:, 1], AX.X, ALU.add))
                step(v.reciprocal(s1[:, 2:3], s1[:, 1:2]))
                step(v.tensor_scalar(prob, e3[:, 1], s1[:, 2:3], None, ALU.mult))
                step(v.tensor_reduce(s1[:, 3:4], prob, AX.X, ALU.max))
                step(v.tensor_scalar(e3[:, 3], prob, s1[:, 3:4], None, ALU.is_equal))
                step(v.tensor_scalar(e3[:, 4], e3[:, 3], -1.0, 1.0, ALU.mult, ALU.add))
                step(v.tensor_copy(onehot[:, 0:1], e3[:, 3, 0:1]))
                step(v.tensor_tensor(onehot[:, 1:2], e3[:, 3, 1:2], e3[:, 4, 0:1], ALU.mult))
                step(v.tensor_tensor(s1[:, 4:5], e3[:, 4, 0:1], e3[:, 4, 1:2], ALU.mult))
                step(v.tensor_tensor(onehot[:, 2:3], e3[:, 3, 2:3], s1[:, 4:5], ALU.mult))
                dve.wait_ge(s_p, 2)
                step(v.tensor_copy(cnt[:, 0], ps[:, P:P + NE]))
                step(v.tensor_tensor(gt[:], cnt[:, 0].unsqueeze(2).broadcast_to([P, NE, 8]),
                                     thresholds.unsqueeze(1).broadcast_to([P, NE, 8]), ALU.is_gt))
                step(v.tensor_reduce(cnt[:, 1], gt[:], AX.X, ALU.add))
                step(v.memset(cnt[:, 2], 0.0))
                step(v.tensor_copy(cnt[:, 2, 1:2], cnt[:, 1, 0:1]))
                step(v.tensor_tensor(cnt[:, 2, 2:3], cnt[:, 1, 0:1], cnt[:, 1, 1:2], ALU.add))
                step(v.scalar_tensor_tensor(out=e3[:, 6], in0=cnt[0:IMGS, 2], scalar=float(GRP), in1=ps[0:IMGS, 2 * P:2 * P + NE],
                                            op0=ALU.mult, op1=ALU.add))
                step(v.tensor_tensor(e3[:, 7], e3[:, 6], onehot, ALU.mult))
                step(v.tensor_reduce(s1[:, 5:6], e3[:, 7], AX.X, ALU.add))
                step(v.tensor_scalar(pm[:, 0], slots[0:IMGS], s1[:, 5:6], None, ALU.is_equal))
                step(v.tensor_scalar(pm[:, 1], pm[:, 0], s1[:, 3:4], None, ALU.mult))
                dve.wait_ge(s_p, 3)
                step(v.tensor_scalar(row[:, 0], pr[0:1, P:P + SLOTS], -1.0, 1.0, ALU.mult, ALU.add))
                step(v.scalar_tensor_tensor(out=row[:, 1], in0=row[:, 0], scalar=float(IMGS), in1=pr[0:1, 0:SLOTS],
                                            op0=ALU.mult, op1=ALU.add))
                step(v.tensor_tensor(row[:, 2], row[:, 0], slots[0:1], ALU.mult))
                step(v.tensor_tensor(row[:, 3], row[:, 1], row[:, 2], ALU.add))
                step(v.tensor_scalar(lists[:, 0:SLOTS], row[:, 1], float(TOK), None, ALU.mult))
                step(v.tensor_scalar(lists[:, SLOTS:2 * SLOTS], row[:, 3], float(TOK), None, ALU.mult))
                step(v.tensor_scalar(row[:, 0, 0:NB], slots[0:1, 0:NB], cnt[0:1, 2, 1:2], None, ALU.is_ge))
                step(v.scalar_tensor_tensor(out=lists[:, 2 * SLOTS:], in0=slots[0:1, 0:NB], scalar=cnt[0:1, 2, 2:3],
                                            in1=row[:, 0, 0:NB], op0=ALU.is_ge, op1=ALU.add))
                for i in range(2):
                    r = slice(TOK * i, TOK * i + TOK)
                    step(v.tensor_copy(weights[r], pr[r, 2 * P:2 * P + SLOTS].rearrange("p (k c) -> p k c", c=2)[:, :, i]))

            @block.tensor
            def _(pe):
                nc.tensor.matmul(ps[0:IMGS, 0:NE], means[:, 0:IMGS], wg[:, 0], start=True, stop=False)
                nc.tensor.matmul(ps[0:IMGS, 0:NE], means[0:FB, IMGS:2 * IMGS], wg[0:FB, 1], start=False, stop=True).then_inc(s_p, 1)
                pe.wait_ge(s_d, 14)
                nc.tensor.matmul(ps[:, P:P + NE], ones[:], onehot, start=True, stop=True)
                nc.tensor.matmul(ps[0:IMGS, 2 * P:2 * P + NE], before, onehot, start=True, stop=True).then_inc(s_p, 1)
                pe.wait_ge(s_d, 25)
                nc.tensor.matmul(pr[0:1, 0:SLOTS], image, pm[:, 0], start=True, stop=True)
                nc.tensor.matmul(pr[0:1, P:P + SLOTS], ones[:, 0:1], pm[:, 0], start=True, stop=True)
                nc.tensor.matmul(pr[:, 2 * P:2 * P + SLOTS], ones[:], pm[:, 1], start=True, stop=True).then_inc(s_p, 1)


def moe_stage(nc, stored, hidden, lists, weights, first, second, ident_d, out_d):
    UN = 4
    HB, AB, RING = 3, 3, 2 * NC
    with ExitStack() as ctx:
        m = Memory(nc, ctx, "mo")
        xt = m.sb("xt", [P, UN, BLK, 2 * P], F32)
        xs = m.sb("xs", [P, 2, 3, TILE], F32R)
        w1 = m.sb("w1", [P, 2, W1C], F32R)
        w2 = m.sb("w2", [P, 2, W2C], F32R)
        idf = m.sb("idf", [P, P], F32)
        g = m.sb("g", [P, 4, TILE], F32)
        gh = m.sb("gh", [P, RING, TILE], F32R)
        gl = m.sb("gl", [P, RING, TILE], F32R)
        wc = m.sb("wc", [P, BLK], F32)
        ya = m.sb("ya", [P, D], F32)
        yb = m.sb("yb", [P, BLK, D], F32)
        st = m.sb("st", [P, 6], F32)
        mv = m.sb("mv", [P, BLK, 2], F32)
        ve = m.sb("ve", [P, BLK], F32)
        half = m.sb("half", [P, BLK], F32)
        mark = m.sb("mark", [P, 1], F32)
        rstd = m.sb("rstd", [P, BLK], F32)
        out = m.sb("out", [P, 2, BLK, D], F32)
        hid = [m.ps(f"hid{i}", [P, TILE]) for i in range(HB)]
        acc = [m.ps(f"acc{i}", [P, TILE]) for i in range(2)]
        tr = m.ps("tr", [P, 2, TILE])
        s_id, s_half, s_end = m.sem("ident"), m.sem("half"), m.sem("last_rows_stored")
        s_x = m.sems("x_loaded", UN)
        s_w1, s_w2 = m.sems("w1_loaded", 2), m.sems("w2_loaded", 2)
        s_dup, s_tr, s_xh, s_xl = m.sem("x_dup"), m.sem("transposed"), m.sem("x_hi"), m.sem("x_lo")
        s_hid, s_g, s_gh, s_gl, s_acc = (m.sem(n) for n in ("hidden", "gelu", "gelu_hi", "gelu_lo", "summed"))
        s_wc, s_ya, s_yb, s_bs, s_ag, s_ve, s_rt, s_o = (m.sem(n) for n in
            ("weight", "biased", "added", "stats", "aggr", "var_eps", "rstd", "out_ready"))
        s_st = stored

        def blocks(eng, body):
            body(0, 0)
            with eng.Fori(0, (NB - 2) // UN) as i:
                for d in range(UN):
                    body(UN * i + 1 + d, (1 + d) % UN)
            for b in range(UN * ((NB - 2) // UN) + 1, NB + 1):
                body(b, b % UN)

        def final(b):
            return isinstance(b, int) and b >= NB - 1

        def ended(b):
            return isinstance(b, int) and b == NB

        def started(b):
            return not (isinstance(b, int) and b == 0)

        def entry(eng, at, most):
            return eng.value_load(lists[0:1, bass.ds(at, 1)], min_val=0, max_val=most)

        def load_image(eng, b, r, s):
            rows = entry(eng, GRP * b + s, IMGS * TOK)
            if s == 0:
                need(eng, s_o, BLK * (b - 2) if not isinstance(b, int) or b > 3 else 0)
            eng.dma_start(xt[TOK * (s % 2):TOK * (s % 2) + TOK, r, s // 2, 0:D],
                          hidden[bass.ds(rows, TOK), :]).then_inc(s_x[r], 16)

        def store_image(eng, p, u, j, i, sem):
            rows = entry(eng, SLOTS + GRP * p + 2 * j + i, (IMGS + SLOTS - 1) * TOK)
            eng.wait_ge(s_o, BLK * p + j + 1 + BLK)
            eng.dma_start(out_d[bass.ds(rows, TOK), :], out[TOK * i:TOK * i + TOK, u, j]).then_inc(sem, 16)

        W1 = lambda u: (w1[:, u, 0:FF], w1[:, u, 2 * FF:3 * FF], w1[:, u, FF:2 * FF], w1[:, u, 3 * FF:4 * FF])
        with nc.Block() as block:

            @block.sync
            def _(sp):
                sp.dma_start(idf[:], ident_d).then_inc(s_id, 16)

                def load(b, r):
                    for s in range(GRP):
                        load_image(sp, b, r, s)
                    load1(b, r)

                def load1(b, r):
                    u = r % 2
                    e = entry(sp, 2 * SLOTS + b, NE - 1)
                    need(sp, s_g, NC * (b - 1))
                    sp.dma_start(w1[:, u].bitcast(F32), first[:, bass.ds(e * W1C, W1C)]).then_inc(s_w1[u], 16)

                def load2(b, r):
                    u = r % 2
                    e = entry(sp, 2 * SLOTS + b, NE - 1)
                    need(sp, s_ya, BLK * (b - 1))
                    sp.dma_start(w2[:, u].bitcast(F32), second[:, bass.ds(e * W2C, W2C)]).then_inc(s_w2[u], 16)

                def body(b, r):
                    if not final(b):
                        load(b + 1, (r + 1) % UN)
                    if not ended(b):
                        load2(b, r)

                load1(0, 0)
                for s in range(GRP // 2):
                    load_image(sp, 0, 0, s)
                blocks(sp, body)
                for j in range(BLK):
                    store_image(sp, NB - 1, (NB - 1) % 2, j, 1, s_end)
                sp.wait_ge(s_end, 16 * BLK)

            @block.gpsimd
            def _(pool):
                nc.gpsimd.memset(half[:], -0.5).then_inc(s_half, 1)
                pool.wait_ge(s_half, 1)

                def body(b, r):
                    if not started(b):
                        return
                    p, u = b - 1, (r - 1) % 2
                    pool.wait_ge(s_ve, p + 1)
                    nc.gpsimd.tensor_tensor(rstd[:], ve[:], half[:], ALU.pow).then_inc(s_rt, 1)
                    for j in range(BLK):
                        for i in range(1 if ended(b) else 2):
                            store_image(pool, p, u, j, i, s_st[u])

                blocks(pool, body)
                for u in range(2):
                    pool.wait_ge(s_st[u], 16 * (GRP * NB // 2 - (BLK if u == (NB - 1) % 2 else 0)))

            @block.scalar
            def _(act):
                def duplicate(b, r):
                    need(act, s_x[r], 16 * GRP // UN * (b - r) + 16 * GRP)
                    need(act, s_tr, 2 * (b - 2))
                    nc.scalar.copy(xt[:, r, :, D:], xt[:, r, :, FA:D]).then_inc(s_dup, 1)

                def ready(b, r):
                    u = r % 2
                    act.wait_ge(s_tr, 2 * b + 2)
                    need(act, s_hid, NC * (b - 1))
                    nc.scalar.copy(xs[:, u, 0], tr[:, 0]).then_inc(s_xh, 1)
                    nc.scalar.copy(xs[:, u, 2], tr[:, 1]).then_inc(s_xh, 1)

                def body(b, r):
                    u = r % 2
                    if ended(b):
                        return
                    need(act, s_w1[u], 8 * (b - u) + 16)
                    for f in range(NC):
                        n = NC * u + f
                        k = NC * b + f
                        act.wait_ge(s_hid, k + 1)
                        need(act, s_gl, k - 3)
                        nc.scalar.activation(g[:, n % 4], hid[n % HB][:], ACT.Gelu,
                                             bias=w1[:, u, 4 * FF + f:4 * FF + f + 1].bitcast(F32)).then_inc(s_g, 1)
                        act.wait_ge(s_g, k + 1)
                        if f == 0:
                            need(act, s_acc, BLK * (b - 1))
                        nc.scalar.copy(gh[:, n], g[:, n % 4]).then_inc(s_gh, 1)
                        if f == NC // 2 and not final(b):
                            duplicate(b + 1, (r + 1) % UN)
                    if not final(b):
                        ready(b + 1, (r + 1) % UN)

                for s in range(GRP // 2, GRP):
                    load_image(act, 0, 0, s)
                duplicate(0, 0)
                ready(0, 0)
                blocks(act, body)

            @block.vector
            def _(dve):
                def ready(b, r):
                    u = r % 2
                    dve.wait_ge(s_xh, 2 * b + 1)
                    nc.vector.tensor_tensor(xs[:, u, 1], tr[:, 0], xs[:, u, 0].bitcast(F32), ALU.subtract).then_inc(s_xl, 1)
                    dve.wait_ge(s_xh, 2 * b + 2)
                    low = xs[FB:P, u, 2]
                    nc.vector.tensor_tensor(low, tr[FB:P, 1], low.bitcast(F32), ALU.subtract).then_inc(s_xl, 1)

                def finish(b, r):
                    u = r % 2
                    nc.vector.tensor_copy(wc[:], weights[:, bass.ds(BLK * b, BLK)]).then_inc(s_wc, 1)
                    dve.wait_ge(s_wc, b + 1)
                    for j in range(BLK):
                        k = BLK * b + j
                        c = k + 1
                        dve.wait_ge(s_acc, c)
                        nc.vector.tensor_tensor(ya[:], acc[j % 2][:, 0:D], w2[:, u, 2 * NC * D:].bitcast(F32), ALU.add).then_inc(s_ya, 1)
                        dve.wait_ge(s_ya, c)
                        nc.vector.scalar_tensor_tensor(out=yb[:, j], in0=ya[:], scalar=wc[:, j:j + 1], in1=xt[:, r, j, 0:D],
                                                       op0=ALU.mult, op1=ALU.add).then_inc(s_yb, 1)
                        dve.wait_ge(s_yb, c)
                        nc.vector.bn_stats(st[:], yb[:, j]).then_inc(s_bs, 1)
                        dve.wait_ge(s_bs, c)
                        nc.vector.memset(mark[:], 0.0)
                        nc.vector.bn_aggr(mv[:, j], st[:]).then_inc(s_ag, 1)
                    dve.wait_ge(s_ag, BLK * b + BLK)
                    nc.vector.tensor_scalar(ve[:], mv[:, :, 1], EPS, None, ALU.add).then_inc(s_ve, 1)
                    dve.wait_ge(s_rt, b + 1)
                    need(dve, s_st[u], 8 * GRP * (b - u))
                    for j in range(BLK):
                        nc.vector.tensor_scalar(out[:, u, j], yb[:, j], mv[:, j, 0:1], rstd[:, j:j + 1], ALU.subtract,
                                                ALU.mult).then_inc(s_o, 1)

                def body(b, r):
                    u = r % 2
                    if not ended(b):
                        for f in range(NC):
                            n = NC * u + f
                            k = NC * b + f
                            if f == 0:
                                need(dve, s_acc, BLK * (b - 1))
                            dve.wait_ge(s_gh, k + 1)
                            nc.vector.tensor_tensor(gl[:, n], g[:, n % 4], gh[:, n].bitcast(F32), ALU.subtract).then_inc(s_gl, 1)
                    if not final(b):
                        ready(b + 1, (r + 1) % UN)
                    if started(b):
                        finish(b - 1, (r - 1) % UN)

                nc.vector.memset(mark[:], 0.0).then_inc(s_o, BLK)
                ready(0, 0)
                blocks(dve, body)

            @block.tensor
            def _(pe):
                pe.wait_ge(s_id, 16)

                def transpose(b, r):
                    pe.wait_ge(s_dup, b + 1)
                    need(pe, s_xl, 2 * b)
                    for k in range(2):
                        for j in range(BLK):
                            last = nc.tensor.transpose(tr[:, k, P * j:P * j + P], xt[:, r, j, P * k:P * k + P], idf[:])
                        last.then_inc(s_tr, 1)

                def second_product(b, r):
                    u = r % 2
                    need(pe, s_w2[u], 8 * (b - u) + 16)
                    pe.wait_ge(s_gl, NC * b + NC)
                    for j in range(BLK):
                        need(pe, s_ya, BLK * b + max(j - 1, 0))
                        o = acc[j % 2][:, 0:D]
                        at = slice(P * j, P * j + P)
                        for f in range(NC):
                            n = NC * u + f
                            h, l = gh[:, n, at], gl[:, n, at]
                            a, c = w2[:, u, D * f:D * f + D], w2[:, u, D * (NC + f):D * (NC + f) + D]
                            nc.tensor.matmul(o, h, a, start=f == 0, stop=False)
                            nc.tensor.matmul(o, h, c, start=False, stop=False)
                            last = nc.tensor.matmul(o, l, a, start=False, stop=f == NC - 1)
                        last.then_inc(s_acc, 1)

                def body(b, r):
                    u = r % 2
                    if not ended(b):
                        need(pe, s_w1[u], 8 * (b - u) + 16)
                        pe.wait_ge(s_xl, 2 * b + 2)
                        for f in range(NC):
                            n = NC * u + f
                            need(pe, s_g, NC * b + f + 1 - HB)
                            product_fm(nc, hid[n % HB][:], W1(u), slice(P * f, P * f + P),
                                       (xs[:, u, 0], xs[:, u, 1], xs[:, u, 2])).then_inc(s_hid, 1)
                    if not final(b):
                        transpose(b + 1, (r + 1) % UN)
                    if started(b):
                        second_product(b - 1, (r - 1) % UN)

                transpose(0, 0)
                blocks(pe, body)


def positions():
    pos = np.arange(TOK, dtype=np.float32)[:, None]
    i = np.arange(D // 2, dtype=np.float32)[None, :]
    ang = (pos / np.power(np.float32(10000.0), np.float32(2.0) * i / np.float32(D))).astype(np.float32)
    pe = np.zeros((TOK, D), np.float32)
    pe[:, 0::2] = np.sin(ang)
    pe[:, 1::2] = np.cos(ang)
    return pe


def stacked(w):
    return np.stack([w[:FA], np.concatenate([w[FA:], w[FA:]])], 1)


def doubled(w):
    return np.concatenate([w, w[..., FA:]], -1)


def lay_out(**a):
    a = {k: np.asarray(v) for k, v in a.items()}
    out = {}
    x = a["x"].reshape(IMGS, 3, 8, 16, 8, 16).transpose(1, 3, 5, 0, 2, 4).reshape(PC, P, NT, TILE)
    out["patches"] = x.transpose(2, 1, 0, 3)
    out["w_patch"] = a["L0_tok_patch_w"].reshape(D, PC, P).transpose(2, 1, 0).reshape(P, PC * D)
    pe = np.concatenate([positions()] * 2)
    row = lambda v: np.broadcast_to(v, (P, D))
    out["rows"] = np.stack([row(a["L0_tok_patch_b"]), row(a["L0_tok_ln_g"]), pe, row(a["L0_tok_ln_b"])], 1)
    eye = np.eye(P, dtype=np.float32)
    out["ident"] = np.concatenate([eye, np.tile(np.eye(FB, dtype=np.float32), (2, 2))], 1)
    w1 = stacked(a["L0_tok_ff1_w"]).reshape(P, 2, NC, P).transpose(0, 2, 1, 3).reshape(P, NC, 2 * P)
    w2 = doubled(a["L0_tok_ff2_w"]).reshape(NC, P, 2 * P).transpose(1, 0, 2)
    out["w_ff"] = np.concatenate([w1, w2], 2).reshape(P, W_FF)
    fm = lambda b: doubled(b).reshape(2, P).T
    out["b_ff"] = np.concatenate([a["L0_tok_ff1_b"].reshape(NC, P).T, fm(a["L0_tok_ff2_b"])], 1)
    def att(wq, bq, wp, bp, normed):
        wq = stacked(np.concatenate([doubled(wq[:, D:2 * D]), doubled(wq[:, 0:D]), wq[:, 2 * D:]], 1))
        wp = stacked(wp if normed else doubled(wp))
        bs = [fm(bq[D:2 * D]), fm(bq[0:D]), fm(bq[2 * D:]), fm(bp)]
        return np.concatenate([wq, wp], 2).reshape(P, -1), np.concatenate(bs, 1)

    out["w_att1"], out["c_att1"] = att(*(a[f"L0_tok_{k}"] for k in ("qkv_w", "qkv_b", "proj_w", "proj_b")), False)
    out["w_att2"], out["c_att2"] = att(*(a[f"L0_attn_{k}"] for k in ("w_qkv", "b_qkv", "w_proj", "b_proj")), True)
    out["b_out2"] = row(a["L0_attn_b_proj"])
    tm = np.zeros((P, 2, D), np.float32)
    tm[:, 0, 0:P] = eye
    tm[:, 1, P:] = np.tile(np.eye(FB, dtype=np.float32), (2, 1))
    out["ident_tm"] = tm.reshape(P, 2 * D)
    sel = np.zeros((P, 2), np.float32)
    sel[:TOK, 0] = sel[TOK:, 1] = 1.0 / TOK
    out["sel"] = sel
    out["wg"] = stacked(a["L0_ffn_Wg"].T)
    c = np.zeros((P, 3 * P + SLOTS), np.float32)
    c[:IMGS, :IMGS] = np.triu(np.ones((IMGS, IMGS)), 1)
    c[:IMGS, IMGS] = np.arange(IMGS)
    c[:, P:P + 8] = GRP * np.arange(8)
    c[:, 3 * P:] = np.arange(SLOTS)
    out["route_consts"] = c
    w1 = np.stack([stacked(w).reshape(P, 2 * FF) for w in a["L0_ffn_W1"]])
    w2 = a["L0_ffn_W2"].reshape(NE, NC, P, D).transpose(0, 2, 1, 3).reshape(NE, P, NC * D)
    out["w_exp"] = np.concatenate([w1, w2], 2).transpose(1, 0, 2).reshape(P, NE * W_MOE)
    out["b1_exp"] = a["L0_ffn_b1"].reshape(NE, NC, P).transpose(0, 2, 1)
    out["b2_exp"] = np.broadcast_to(a["L0_ffn_b2"][:, None], (NE, P, D))
    return {k: np.ascontiguousarray(v) for k, v in out.items()}


def build(nc, arrays, debug=False):
    ins = {k: nc.dram_tensor(k, v.shape, mybir.dt.from_np(v.dtype), kind="ExternalInput").ap() for k, v in arrays.items()}
    kind = "ExternalOutput" if debug else "Internal"
    T = IMGS * TOK
    x0, y, x2, x3 = (nc.dram_tensor(n, (P, 3, T), F32, kind=kind).ap() for n in ("x0", "y", "x2", "x3"))
    h = nc.dram_tensor("h", (T + TOK, D), F32, kind=kind).ap()
    idf = ins["ident"][:, 0:P]
    first = nc.dram_tensor("expert_first", (P, NE * W1C), F32, kind="Internal").ap()
    second = nc.dram_tensor("expert_second", (P, NE * W2C), F32, kind="Internal").ap()
    out = nc.dram_tensor("out", ((IMGS + SLOTS) * TOK, D), F32, kind="ExternalOutput").ap()
    stored = [[nc.alloc_semaphore(f"stored{k}{i}") for i in range(2)] for k in range(6)]
    placed = [nc.alloc_semaphore(f"placed{k}") for k in range(2)]
    with (
        nc.sbuf_tensor("means", [P, 2 * IMGS], F32) as means,
        nc.sbuf_tensor("lists", [1, 2 * SLOTS + NB], I32) as lists,
        nc.sbuf_tensor("weights", [P, SLOTS // 2], F32) as weights,
        nc.sbuf_tensor("gate", [P, 2, NE], F32) as wg,
        nc.sbuf_tensor("routing", [P, 3 * P + SLOTS], F32) as consts,
    ):
        patch_stage(nc, stored[0], ins["patches"], ins["w_patch"], ins["rows"], idf, x0)
        with (
            nc.sbuf_tensor("q", [P, 2, 3, GRP * P], F32R) as q,
            nc.sbuf_tensor("kbA", [P, 2, 2, HA, 2 * P], F32R) as kbA,
            nc.sbuf_tensor("kbB", [P, 2, 2, HBN, 2 * P], F32R) as kbB,
            nc.sbuf_tensor("vb", [P, 2, 2, BLK * 3, HP, VW], BF16) as vb,
        ):
            operands = (q, kbA, kbB, vb)
            ff_stage(nc, stored[1], "ff1", x0, y, ins["w_ff"], ins["b_ff"], ins["ident"], False, operands=operands)
            att_stage(nc, stored[2], placed[0], "at1", y, x0, ins["w_att1"], ins["c_att1"], (ins["ident"], idf), state_out=x2,
                      operands=operands)
            ff_stage(nc, stored[3], "ff2", x2, x3, ins["w_ff"], ins["b_ff"], ins["ident"], True,
                     experts=(ins["w_exp"], ins["b1_exp"], ins["b2_exp"], first, second))
            att_stage(nc, stored[4], placed[1], "at2", x3, x3, ins["w_att2"], ins["c_att2"], (ins["ident_tm"], idf),
                      rows_d=ins["b_out2"], sel_d=ins["sel"], hidden=h, means=means, operands=operands,
                      preload=((wg, ins["wg"]), (consts, ins["route_consts"])))
        route_stage(nc, means, wg, consts, h, lists, weights)
        moe_stage(nc, stored[5], h, lists, weights, first, second, idf, out)
    return ["x0", "y", "x2", "x3", "h", "out"] if debug else ["out"]


def kernel(**inputs):
    from concourse import bacc
    from concourse.bass_utils import run_bass_kernel_spmd

    arrays = lay_out(**inputs)
    nc = bacc.Bacc("TRN2", target_bir_lowering=False, num_devices=1)
    build(nc, arrays)
    got = run_bass_kernel_spmd(nc, [arrays], core_ids=[0]).results[0]["out"]
    return got[:IMGS * TOK].reshape(IMGS, TOK, D)
```
